# Optimizing a Trainium2 kernel written in Bass

```python
import numpy as np
import jax
import jax.numpy as jnp

def _softmax(x, axis=-1):
    return jax.nn.softmax(x, axis=axis)

def _gelu(x):
    return jax.nn.gelu(x, approximate=True)

def _silu(x):
    return jax.nn.silu(x)

def _sigmoid(x):
    return jax.nn.sigmoid(x)

def _layernorm(x, axis=-1, eps=1e-05):
    m = jnp.mean(x, axis=axis, keepdims=True)
    v = jnp.var(x, axis=axis, keepdims=True)
    return (x - m) / jnp.sqrt(v + eps)

def _scatter_add(tgt, idx, src, axis=0):
    return tgt.at[idx].add(src)

def _segment_sum(src, seg, n):
    return jax.ops.segment_sum(src, seg, n)
kernel_name = 'mk_macaron_d1_jaxref_r4_dad05e'

def setup_inputs(seed: int=0):
    np.random.seed(seed)
    _w = jnp.asarray

    def _L0_attn_setup():
        import jax, jax.numpy as jnp
        import numpy as np
        DIM = 512
        HEADS = 16
        HEAD_DIM = DIM // HEADS
        CHUNK = 128
        B, N = (4, 512)

        def _rmsnorm(x, w, eps):
            return x * jax.lax.rsqrt(jnp.mean(x * x, axis=-1, keepdims=True) + eps) * w

        def _weight_quant(w):
            scale = 1.0 / jnp.clip(jnp.mean(jnp.abs(w)), 1e-05, None)
            q = jnp.clip(jnp.round(w * scale), -1.0, 1.0) / scale
            return w + jax.lax.stop_gradient(q - w)

        def _forward(x, qkv_w, qkv_norm_w, proj_w, proj_norm_w, norm_w, s):
            Bb, Nn, C = x.shape
            H, D, T = (HEADS, HEAD_DIM, CHUNK)
            nc = Nn // T
            eps = jnp.finfo(x.dtype).eps
            scale = D ** (-0.5)
            h = _rmsnorm(x, qkv_norm_w, eps)
            qkv = h @ _weight_quant(qkv_w).T
            qkv = qkv.reshape(Bb, Nn, 3, H, D)
            q, k, v = (qkv[:, :, 0], qkv[:, :, 1], qkv[:, :, 2])

            def chunks(t):
                return t.reshape(Bb, nc, T, H, D).transpose(1, 0, 3, 2, 4)
            qc, kc, vc = (chunks(q), chunks(k), chunks(v))
            tt = jnp.arange(T, dtype=x.dtype)
            lam_t = jnp.exp(-s[:, None] * tt)
            lam_rev = jnp.exp(-s[:, None] * (T - tt))
            diff = tt[:, None] - tt[None, :]
            mask = jnp.where(diff >= 0, jnp.exp(-s[:, None, None] * diff), 0.0)
            lam_T = jnp.exp(-s * T)[:, None, None]

            def step(S, qkv_c):
                qi, ki, vi = qkv_c
                scores = jnp.einsum('bhtd,bhsd,hts->bhts', qi, ki, mask)
                intra = jnp.einsum('bhts,bhsd->bhtd', scores, vi)
                cross = jnp.einsum('bhtd,ht,bhde->bhte', qi, lam_t, S)
                o = scale * (intra + cross)
                kv = jnp.einsum('bhtd,ht,bhte->bhde', ki, lam_rev, vi)
                return (lam_T * S + kv, o)
            S0 = jnp.zeros((Bb, H, D, D), x.dtype)
            _, outs = jax.lax.scan(step, S0, (qc, kc, vc))
            out = outs.transpose(1, 0, 3, 2, 4).reshape(Bb, Nn, C)
            out = _rmsnorm(out, norm_w, 1e-06)
            out = _rmsnorm(out, proj_norm_w, eps) @ _weight_quant(proj_w).T
            return out
        key = jax.random.key(seed)
        ks = jax.random.split(key, 3)
        x = jax.random.normal(ks[0], (B, N, DIM), jnp.float32)
        bound = float(1.0 / np.sqrt(DIM))
        qkv_w = jax.random.uniform(ks[1], (3 * DIM, DIM), jnp.float32, -bound, bound)
        proj_w = jax.random.uniform(ks[2], (DIM, DIM), jnp.float32, -bound, bound)
        return {'x': x, 'qkv_w': qkv_w, 'qkv_norm_w': jnp.ones((DIM,), jnp.float32), 'proj_w': proj_w, 'proj_norm_w': jnp.ones((DIM,), jnp.float32), 'norm_w': jnp.ones((DIM,), jnp.float32), 's': jnp.full((HEADS,), 0.02, jnp.float32)}
    _L0_attn_in = _L0_attn_setup()

    def _L0_ffn_setup():
        import jax, jax.numpy as jnp
        import numpy as np
        B, S, D, H = (4, 512, 512, 2048)

        def fwht(x):
            orig_shape = x.shape
            n = orig_shape[-1]
            x = x.reshape(-1, n)
            h = 1
            while h < n:
                xb = x.reshape(-1, n // (2 * h), 2, h)
                a = xb[:, :, 0, :]
                b = xb[:, :, 1, :]
                x = jnp.stack([a + b, a - b], axis=2).reshape(-1, n)
                h *= 2
            scale = jnp.asarray(1.0 / np.sqrt(n), dtype=x.dtype)
            return (x * scale).reshape(orig_shape)
        key = jax.random.key(seed)
        kx, k1, k2, k3 = jax.random.split(key, 4)
        x = jax.random.normal(kx, (B, S, D), dtype=jnp.float32)
        W1 = jax.random.normal(k1, (H, D), dtype=jnp.float32) * (1.0 / np.sqrt(D))
        W2 = jax.random.normal(k2, (D, H), dtype=jnp.float32) * (1.0 / np.sqrt(H))
        W3 = jax.random.normal(k3, (H, D), dtype=jnp.float32) * (1.0 / np.sqrt(D))
        return {'x': x, 'W1': W1, 'W2': W2, 'W3': W3}
    _L0_ffn_in = _L0_ffn_setup()
    _d = {'L0_attn_x': _L0_attn_in['x'], 'L0_attn_qkv_w': _L0_attn_in['qkv_w'], 'L0_attn_qkv_norm_w': _L0_attn_in['qkv_norm_w'], 'L0_attn_proj_w': _L0_attn_in['proj_w'], 'L0_attn_proj_norm_w': _L0_attn_in['proj_norm_w'], 'L0_attn_norm_w': _L0_attn_in['norm_w'], 'L0_attn_s': _L0_attn_in['s'], 'L0_ffn_W1': _L0_ffn_in['W1'], 'L0_ffn_W2': _L0_ffn_in['W2'], 'L0_ffn_W3': _L0_ffn_in['W3']}
    _x0 = _d['L0_attn_x']
    _d['L0_attn_x'] = jax.random.normal(jax.random.fold_in(jax.random.key(seed), 1), (8, 512, 512), dtype=_x0.dtype)
    del _x0
    return _d

def reference(L0_attn_x, L0_attn_qkv_w, L0_attn_qkv_norm_w, L0_attn_proj_w, L0_attn_proj_norm_w, L0_attn_norm_w, L0_attn_s, L0_ffn_W1, L0_ffn_W2, L0_ffn_W3):

    def _L0_attn_ref(x, qkv_w, qkv_norm_w, proj_w, proj_norm_w, norm_w, s):
        import jax, jax.numpy as jnp
        import numpy as np
        DIM = 512
        HEADS = 16
        HEAD_DIM = DIM // HEADS
        CHUNK = 128
        B, N = (4, 512)

        def _rmsnorm(x, w, eps):
            return x * jax.lax.rsqrt(jnp.mean(x * x, axis=-1, keepdims=True) + eps) * w

        def _weight_quant(w):
            scale = 1.0 / jnp.clip(jnp.mean(jnp.abs(w)), 1e-05, None)
            q = jnp.clip(jnp.round(w * scale), -1.0, 1.0) / scale
            return w + jax.lax.stop_gradient(q - w)

        def _forward(x, qkv_w, qkv_norm_w, proj_w, proj_norm_w, norm_w, s):
            Bb, Nn, C = x.shape
            H, D, T = (HEADS, HEAD_DIM, CHUNK)
            nc = Nn // T
            eps = jnp.finfo(x.dtype).eps
            scale = D ** (-0.5)
            h = _rmsnorm(x, qkv_norm_w, eps)
            qkv = h @ _weight_quant(qkv_w).T
            qkv = qkv.reshape(Bb, Nn, 3, H, D)
            q, k, v = (qkv[:, :, 0], qkv[:, :, 1], qkv[:, :, 2])

            def chunks(t):
                return t.reshape(Bb, nc, T, H, D).transpose(1, 0, 3, 2, 4)
            qc, kc, vc = (chunks(q), chunks(k), chunks(v))
            tt = jnp.arange(T, dtype=x.dtype)
            lam_t = jnp.exp(-s[:, None] * tt)
            lam_rev = jnp.exp(-s[:, None] * (T - tt))
            diff = tt[:, None] - tt[None, :]
            mask = jnp.where(diff >= 0, jnp.exp(-s[:, None, None] * diff), 0.0)
            lam_T = jnp.exp(-s * T)[:, None, None]

            def step(S, qkv_c):
                qi, ki, vi = qkv_c
                scores = jnp.einsum('bhtd,bhsd,hts->bhts', qi, ki, mask)
                intra = jnp.einsum('bhts,bhsd->bhtd', scores, vi)
                cross = jnp.einsum('bhtd,ht,bhde->bhte', qi, lam_t, S)
                o = scale * (intra + cross)
                kv = jnp.einsum('bhtd,ht,bhte->bhde', ki, lam_rev, vi)
                return (lam_T * S + kv, o)
            S0 = jnp.zeros((Bb, H, D, D), x.dtype)
            _, outs = jax.lax.scan(step, S0, (qc, kc, vc))
            out = outs.transpose(1, 0, 3, 2, 4).reshape(Bb, Nn, C)
            out = _rmsnorm(out, norm_w, 1e-06)
            out = _rmsnorm(out, proj_norm_w, eps) @ _weight_quant(proj_w).T
            return out
        return _forward(x, qkv_w, qkv_norm_w, proj_w, proj_norm_w, norm_w, s)

    def _L0_ffn_ref(x, W1, W2, W3):
        import jax, jax.numpy as jnp
        import numpy as np
        B, S, D, H = (4, 512, 512, 2048)

        def fwht(x):
            orig_shape = x.shape
            n = orig_shape[-1]
            x = x.reshape(-1, n)
            h = 1
            while h < n:
                xb = x.reshape(-1, n // (2 * h), 2, h)
                a = xb[:, :, 0, :]
                b = xb[:, :, 1, :]
                x = jnp.stack([a + b, a - b], axis=2).reshape(-1, n)
                h *= 2
            scale = jnp.asarray(1.0 / np.sqrt(n), dtype=x.dtype)
            return (x * scale).reshape(orig_shape)
        up_gate = jnp.einsum('bsd,hd->bsh', x, W1)
        up_lin = jnp.einsum('bsd,hd->bsh', x, W3)
        hidden = jax.nn.silu(up_gate) * up_lin
        hidden = fwht(hidden)
        out = jnp.einsum('bsh,dh->bsd', hidden, W2)
        return out
    x = L0_attn_x
    x = x + 0.5 * _L0_ffn_ref(_layernorm(x, axis=-1), L0_ffn_W1, L0_ffn_W2, L0_ffn_W3)
    x = x + _L0_attn_ref(_layernorm(x, axis=-1), L0_attn_qkv_w, L0_attn_qkv_norm_w, L0_attn_proj_w, L0_attn_proj_norm_w, L0_attn_norm_w, L0_attn_s)
    x = x + 0.5 * _L0_ffn_ref(_layernorm(x, axis=-1), L0_ffn_W1, L0_ffn_W2, L0_ffn_W3)
    return x

_drawn_inputs = setup_inputs


def setup_inputs(seed=0):
    import zlib

    import numpy as np

    out = dict(_drawn_inputs(seed))
    spreads = {'L0_attn_qkv_norm_w': (1.0, 0.2),
     'L0_attn_proj_norm_w': (1.0, 0.2),
     'L0_attn_norm_w': (1.0, 0.2),
     'L0_attn_s': (0.019999999552965164, 0.2)}
    factors = {}
    for name, (base, spread) in spreads.items():
        noise = np.random.default_rng([zlib.crc32(name.encode()), seed]).standard_normal(out[name].shape)
        drawn = base * np.exp(spread * noise) if base else spread * noise
        out[name] = jnp.asarray(drawn.astype(out[name].dtype))
    for name, factor in factors.items():
        out[name] = (out[name] * factor).astype(out[name].dtype)
    return out
```

```python
from contextlib import ExitStack

import numpy as np

import concourse.bass as bass
from concourse import mybir

ALU = mybir.AluOpType
ACT = mybir.ActivationFunctionType
AX = mybir.AxisListType
F32 = mybir.dt.float32
F16 = mybir.dt.float16
I32 = mybir.dt.int32

P = 128
EXPONENT = 0x7F800000
LN_EPS = 1e-5
RMS_EPS = float(np.finfo(np.float32).eps)
OUT_NORM_EPS = 1e-6
TINY = 1e-30
X_SCALE = 2.0 ** 11
W_SCALE = 2.0 ** 15


def macaron_kernel(nc, x, qkv_w, qkv_norm_w, proj_w, proj_norm_w, norm_w, s, w1, w2, w3, out):
    B, T, D = x.shape
    H = w1.shape[0]
    HEADS = s.shape[0]
    HD = D // HEADS
    TT = T // P
    KT = D // P
    HT = H // P
    HG = P // HD
    GROUPS = HEADS // HG
    QKV_T = 3 * D // P
    PROJ_T = D // P
    QK_SCALE = float(HD) ** -0.5
    WAVES = HT // 2
    BUTTERFLIES = HT.bit_length() - 1
    assert (D, T, HG, QKV_T + PROJ_T, HT) == (512, 512, 4, 16, 16)

    HID_SCALE = W_SCALE / D

    ctx = ExitStack()
    with ctx:
        def sb(name, shape, dt=F32):
            return ctx.enter_context(nc.sbuf_tensor(name, shape, dt))

        def sem(name):
            return ctx.enter_context(nc.semaphore(name))

        w1t = sb("w1t", [P, 2, KT, H], F16)
        w3t = sb("w3t", [P, 2, KT, H], F16)
        w2t = sb("w2t", [P, 2, HT, D], F16)
        wqkv = sb("wqkv", [P, KT, 3 * D], F16)
        wproj = sb("wproj", [P, KT, D], F16)
        mask = sb("mask", [P, HEADS, P])
        xin = sb("xin", [P, TT, D])
        xt = sb("xt", [P, 2, KT, T], F16)
        cent = sb("cent", [P, 2, D])
        hl = cent[:].bitcast(F16).rearrange("p b (a d) -> p b a d", a=2)
        qT = sb("qT", [P, T])
        junk = qT
        sizes = dict(x1=TT * D, hid=2 * D, gate=D, hfull=D, x2=TT * D, yt=KT * T, qblk=TT * HG * P, qdec=T, kT=T,
                     vnat=T, kdec=(TT - 1) * P, sc=2 * HG * P, state=(TT - 1) * P)
        work = sb("work", [P, sum(sizes.values())])
        at, start = {}, 0
        for name, n in sizes.items():
            at[name] = work[:, start:start + n]
            start += n
        x1 = at["x1"].rearrange("p (t d) -> p t d", t=TT)
        x2 = at["x2"].rearrange("p (t d) -> p t d", t=TT)
        yt = at["yt"].bitcast(F16).rearrange("p (a k t) -> p a k t", a=2, k=KT)
        hid = at["hid"].bitcast(F16).rearrange("p (b a t) -> p b a t", b=2, a=2)
        gate, hfull, qdec, kT = at["gate"], at["hfull"], at["qdec"], at["kT"]
        qblk = at["qblk"].rearrange("p (c h t) -> p c h t", c=TT, h=HG)
        vnat = at["vnat"].rearrange("p (c e) -> p c e", c=TT)
        kdec = at["kdec"].rearrange("p (c e) -> p c e", c=TT - 1)
        sc = at["sc"].rearrange("p (b h t) -> p b h t", b=2, h=HG)
        vT = at["sc"][:, 0:T]
        state = at["state"].rearrange("p (c e) -> p c e", c=TT - 1)
        first = sizes["x1"] + sizes["hid"] + sizes["gate"] + sizes["hfull"]
        stage = work[:, 0:first].rearrange("p (b q d) -> p b q d", b=2, q=4)
        w2n = work[:, first:first + TT * H].rearrange("p (t h) -> p t h", t=KT)
        wst = work[:, first:first + 16 * D].rearrange("p (r d) -> p r d", r=16)
        w2c = work[:, first + KT * H:first + KT * H + 2 * D].rearrange("p (b d) -> p b d", b=2)
        w2p = xt[:].rearrange("p a k t -> p (a k t)").bitcast(F32)
        ident = sb("ident", [P, P])
        ident16 = sb("ident16", [P, P], F16)
        hadamard = sb("hadamard", [P, P])
        lam_t = sb("lam_t", [P, GROUPS, P])
        lam_rev = sb("lam_rev", [P, HEADS])
        lam_T = sb("lam_T", [P, GROUPS])
        diag = sb("diag", [P, P])
        qnw_row = sb("qnw_row", [P, D])
        nw_row = sb("nw_row", [P, D])
        pw_row = sb("pw_row", [P, D])
        s_row = sb("s_row", [P, HEADS])
        s_col = sb("s_col", [P, GROUPS])
        ones = hadamard
        rows = sb("rows", [P, 2, WAVES, 4])
        row_ss = sb("row_ss", [P, WAVES, 4])
        row_sc = sb("row_sc", [P, WAVES, 4])
        g_scale = sb("g_scale", [P, HT])
        l_scale = sb("l_scale", [P, HT])
        f2 = sb("f2", [P, HT])
        ss2 = sb("ss2", [P, KT, 4])
        tops = sb("tops", [P, 2])
        top_all = sb("top_all", [P, 2])
        half = sb("half", [P, 4])
        asum = sb("asum", [P, 16])
        tiny = sb("tiny", [P, 16])
        ffn_unscale = sb("ffn_unscale", [P, 1])
        q_scale = sb("q_scale", [P, 1])
        kv_scale = sb("kv_scale", [P, 1])
        proj_scale = sb("proj_scale", [P, 1])
        stat = sb("stat", [P, 2 * TT, 6])
        mean = sb("mean", [P, TT])
        ms = sb("ms", [P, 3, 2 * TT])
        veps = sb("veps", [P, TT])
        rstd = sb("rstd", [P, TT])

        def bank(name):
            return ctx.enter_context(nc.psum_tensor(name, [P, 512], F32))

        g_bank, l_bank = bank("g_bank"), bank("l_bank")
        d_bank = [bank(f"d_bank{t}") for t in range(TT)]
        a_bank = [bank("a_bank0"), bank("a_bank1")]
        a_bank16 = [b[:].bitcast(F16).rearrange("p (a k t) -> p a k t", a=2, k=KT) for b in a_bank]

        x_loaded, y_stored = sem("x_loaded"), sem("y_stored")
        g_ready, l_ready, d_ready = sem("g_ready"), sem("l_ready"), sem("d_ready")
        d_step = sem("d_step")
        gate_ready, hfull_ready = sem("gate_ready"), sem("hfull_ready")
        hi_ready, lo_ready = sem("hi_ready"), sem("lo_ready")
        res_done = sem("res_done")
        a_ready = [sem("a_ready0"), sem("a_ready1")]
        a_free = [sem("a_free0"), sem("a_free1")]
        ln_stats, ln_small, ln_veps, ln_rstd = sem("ln_stats"), sem("ln_small"), sem("ln_veps"), sem("ln_rstd")
        ln_cent, ln_norm = sem("ln_cent"), sem("ln_norm")
        q_spread, q_dec = sem("q_spread"), sem("q_dec")
        o_stats, o_scaled, o_small = sem("o_stats"), sem("o_scaled"), sem("o_small")
        state_part, state_done = sem("state_part"), sem("state_done")
        rows_loaded = sem("rows_loaded")
        w_loaded = [sem("w_loaded0"), sem("w_loaded1")]
        w2_loaded = [sem(f"w2_loaded{t}") for t in range(KT)]
        wst_loaded = [sem(f"wst_loaded{q}") for q in range(4)]
        pool_const, dve_const, act_const = sem("pool_const"), sem("dve_const"), sem("act_const")
        pool_chain, dve_chain = sem("pool_chain"), sem("dve_chain")
        w_ss, w_pow, w_sc, w_hi, w_lo = sem("w_ss"), sem("w_pow"), sem("w_sc"), sem("w_hi"), sem("w_lo")
        w_copied = sem("w_copied")
        w2_ss, w2_but, w2_tops, w2_all, w2_pow, w2_f = (sem("w2_ss"), sem("w2_but"), sem("w2_tops"), sem("w2_all"),
                                                        sem("w2_pow"), sem("w2_f"))
        w2_tr, w2_c, w2_had, w2_hi, w2_lo = sem("w2_tr"), sem("w2_c"), sem("w2_had"), sem("w2_hi"), sem("w2_lo")
        q_ones, q_sum, q_tot, q_scales, q_tern, qblk_zero = (sem("q_ones"), sem("q_sum"), sem("q_tot"),
                                                             sem("q_scales"), sem("q_tern"), sem("q_zero"))

        def feed_forward(which, slots):
            steps = []
            for j in range(HT):
                steps += [("gate", j)] + slots.get(3 * j, []) + [("lin", j)] + slots.get(3 * j + 1, [])
                if j:
                    steps += [("down", j - 1)]
                steps += slots.get(3 * j + 2, [])
            return steps + [("down", HT - 1)] + slots.get(3 * HT, []) + [("resid", (which, t)) for t in range(TT)]

        def norm_steps(which):
            pre = [("stat", which), ("prep", (which, 0)), ("prep", (which, 1))]
            tr0 = [("turn", (which, 0)), ("prep", (which, 2)), ("turn", (which, 1)), ("prep", (which, 3))]
            tr1 = [("turn", (which, 2)), ("turn", (which, 3))]
            return pre, tr0, tr1

        def add(slots, at, steps):
            slots.setdefault(at, []).extend(steps)

        def attention_slots(at):
            slots = {}
            pre, tr0, tr1 = norm_steps("qkv")
            add(slots, at, tr0)
            add(slots, at + 1, tr1)
            at += 2
            for g in range(GROUPS):
                add(slots, at, [("q", g)])
                add(slots, at + 1, [("v", g), ("k", g)])
                add(slots, at + 2, [("vturn", g), ("kturn", g)])
                add(slots, at + 3, [("score", (g, 0)), ("kv", g)])
                for c in range(1, TT):
                    add(slots, at + 3 + c, [("score", (g, c)), ("pv", (g, c - 1))])
                at += 3 + TT
                add(slots, at, [("pv", (g, TT - 1))])
            pre, tr0, tr1 = norm_steps("o")
            add(slots, at + 1, [("ostat", 0), ("ostat", 1)])
            add(slots, at + 4, [("ostat", 2), ("ostat", 3)])
            add(slots, at + 6, pre)
            add(slots, at + 8, tr0)
            add(slots, at + 9, tr1)
            add(slots, at + 10, [("proj", 0), ("proj", 1)])
            add(slots, at + 11, [("proj", 2), ("proj", 3)])
            pre, tr0, tr1 = norm_steps("ffn2")
            add(slots, at + 12, pre[:1])
            add(slots, at + 13, pre[1:])
            add(slots, at + 15, tr0)
            add(slots, at + 16, tr1)
            assert at + 16 <= 3 * HT
            return slots

        def second_slots():
            slots = {}
            pre, tr0, tr1 = norm_steps("ffn1")
            add(slots, 10, pre)
            add(slots, 14, tr0)
            add(slots, 15, tr1)
            add(slots, 40, norm_steps("qkv")[0])
            return slots

        def last_attention_slots():
            slots = attention_slots(2)
            return {**slots, 0: norm_steps("qkv")[0]}

        quant_slots = {1: [("qsum", 0)], 2: [("qsum", 1)], 3: [("qsum", 2)], 4: [("qsum", 3)], 5: [("qtot", 0)]}
        quant_slots.update({8 + 4 * r: [("qturn", r)] for r in range(8)})
        quant_slots[40] = [("qzero", 0)]
        FIRST = feed_forward("ffn1", quant_slots)
        WITH_ATTENTION = feed_forward("ffn1", attention_slots(0))
        SECOND = feed_forward("ffn2", second_slots())
        SECOND_WITH_ATTENTION = feed_forward("ffn2", last_attention_slots())
        LAST = feed_forward("ffn2", {})
        NORM = sum(norm_steps("ffn1"), [])
        TWO_NORMS = NORM + norm_steps("qkv")[0]

        def bank_use(step, arg):
            if step == "turn":
                return arg[1] % 2, 2
            if step == "proj":
                return arg % 2, 1
            if step == "qturn":
                return arg % 2, 1
            if step == "qtot":
                return 0, 1
            if step == "pv":
                return (1, 1) if arg[1] == 0 else None
            return {"q": (0, 1), "v": (0, 1), "vturn": (0, 1), "score": (0, 1),
                    "k": (1, 1), "kturn": (1, 1), "kv": (1, 1)}.get(step)

        def count_uses(steps):
            fills, copies, uses, before = [0, 0], [0, 0], {}, {}
            for step, arg in steps:
                before[step, arg] = tuple(copies)
                use = bank_use(step, arg)
                if use:
                    uses[step, arg] = (use[0], fills[use[0]])
                    fills[use[0]] += 1
                    copies[use[0]] += use[1]
                elif step == "pv":
                    uses[step, arg] = uses["pv", (arg[0], 0)]
            return uses, before, tuple(fills), tuple(copies)

        USES = {id(x): count_uses(x) for x in (FIRST, WITH_ATTENTION, SECOND, SECOND_WITH_ATTENTION, LAST, NORM, TWO_NORMS)}

        class Place:

            def __init__(self, steps, fills, copies, ffn=0, attn=0, norm=None, stats=None, loaded=0, x2=x2, y=yt, x=None):
                self.steps, self.ffn, self.attn, self.norm, self.stats = steps, ffn, attn, norm or {}, stats or {}
                self.uses, self.before, self.all_fills, self.all_copies = USES[id(steps)]
                self.fills, self.copies, self.x2, self.y = fills, copies, x2, y
                self.x, self.loaded = x, loaded
                self.which = "ffn1" if steps is FIRST or steps is WITH_ATTENTION else "ffn2"

            def filled(self, step, arg):
                b, n = self.uses[step, arg]
                return b, self.fills[b] + (n + 1)

            def copied(self, step, arg, b):
                return self.copies[b] + self.before[step, arg][b]

            def after(self):
                return ([a + n for a, n in zip(self.fills, self.all_fills)],
                        [a + n for a, n in zip(self.copies, self.all_copies)])

        def known_zero(v):
            return isinstance(v, int) and v <= 0

        def program(eng, run):
            place = Place(NORM, [2 * WAVES, 2 * WAVES], [0, 0], norm={"ffn1": 0}, stats={"ffn1": 0}, loaded=0)
            run(place)
            place = Place(FIRST, *place.after(), ffn=0)
            run(place)
            place = Place(TWO_NORMS, *place.after(), ffn=1, norm={"ffn1": 1, "qkv": 2}, stats={"ffn1": 1, "qkv": 2}, loaded=1)
            run(place)
            fills, copies = place.after()
            in_a, in_b = USES[id(WITH_ATTENTION)], USES[id(SECOND)]
            per_fill = [in_a[2][b] + in_b[2][b] for b in range(2)]
            per_copy = [in_a[3][b] + in_b[3][b] for b in range(2)]

            def first_of(i):
                before = i - 1
                m, m_ln = before * 4 + 2, before * 3 + 2
                a = Place(WITH_ATTENTION, [fills[b] + before * per_fill[b] for b in range(2)],
                          [copies[b] + before * per_copy[b] for b in range(2)], ffn=2 * i - 1, attn=before,
                          norm={"qkv": m, "o": m + 1, "ffn2": m + 2}, stats={"qkv": m_ln, "ffn2": m_ln + 1})
                run(a)
                return a.after(), m + 2, m_ln + 1

            with eng.Fori(1, B - 1) as i:
                counts, m, m_ln = first_of(i)
                run(Place(SECOND, *counts, ffn=2 * i, attn=i, norm={"ffn1": m + 1, "qkv": m + 2},
                          stats={"ffn1": m_ln + 1, "qkv": m_ln + 2}, loaded=i + 1))
            counts, m, m_ln = first_of(B - 1)
            place = Place(SECOND_WITH_ATTENTION, *counts, ffn=2 * B - 2, attn=B - 1,
                          norm={"qkv": m + 1, "o": m + 2, "ffn2": m + 3}, stats={"qkv": m_ln + 1, "ffn2": m_ln + 2},
                          x=(xin, xt))
            run(place)
            run(Place(LAST, *place.after(), ffn=2 * B - 1, x2=xin, y=xt))

        def attention_buffers(place):
            return place.x or (place.x2, place.y)

        def norm_source(place, which):
            return {"ffn1": xin, "qkv": x1}.get(which) or attention_buffers(place)[0]

        def norm_target(place, which):
            return xt if which == "ffn1" else attention_buffers(place)[1]

        block = ctx.enter_context(nc.Block())

        @block.sync
        def _(sp):
            for dst, src in ((qnw_row, qkv_norm_w), (nw_row, norm_w), (pw_row, proj_norm_w), (s_row, s)):
                sp.dma_start(dst[:], src.rearrange("(a n) -> a n", a=1).partition_broadcast(P)).then_inc(rows_loaded, 16)
            for w in range(WAVES):
                if w >= 2:
                    sp.wait_ge(w_lo, 4 * (w - 1))
                for q, mat in enumerate((w1, w3)):
                    sp.dma_start(stage[:, w % 2, 2 * q:2 * q + 2, :],
                                 mat[2 * P * w:2 * P * (w + 1), :].rearrange("(c p) d -> p c d", p=P)).then_inc(w_loaded[w % 2], 16)
                if w < KT:
                    sp.dma_start(w2n[:, w, :], w2[P * w:P * (w + 1), :]).then_inc(w2_loaded[w], 16)
            sp.dma_start(xin[:], x[0].rearrange("(t p) d -> p t d", p=P)).then_inc(x_loaded, 16)
            sp.wait_ge(w2_tr, HT)
            for q in range(4):
                src = qkv_w[q * D:(q + 1) * D, :] if q < 3 else proj_w
                sp.dma_start(wst[:, 4 * q:4 * q + 4, :], src.rearrange("(c p) d -> p c d", p=P)).then_inc(wst_loaded[q], 16)
            sp.wait_ge(res_done, TT)
            sp.dma_start(xin[:], x[1].rearrange("(t p) d -> p t d", p=P)).then_inc(x_loaded, 16)
            x_tiles = x.rearrange("b (t p) d -> (b t) p d", p=P)
            out_tiles = out.rearrange("b (t p) d -> (b t) p d", p=P)
            with sp.Fori(1, B - 1) as i:
                sp.wait_ge(res_done, 2 * TT * i)
                sp.dma_start(xin[:], x_tiles[bass.ds((i + 1) * TT, TT)].rearrange("t p d -> p t d")).then_inc(x_loaded, 16)
                sp.wait_ge(res_done, TT * (2 * i + 1))
                sp.dma_start(out_tiles[bass.ds((i - 1) * TT, TT)].rearrange("t p d -> p t d"), x2).then_inc(y_stored, 16)
            sp.wait_ge(res_done, TT * (2 * B - 1))
            sp.dma_start(out_tiles[(B - 2) * TT:(B - 1) * TT].rearrange("t p d -> p t d"), x2).then_inc(y_stored, 16)
            sp.wait_ge(res_done, TT * 2 * B)
            sp.dma_start(out_tiles[(B - 1) * TT:B * TT].rearrange("t p d -> p t d"), xin[:]).then_inc(y_stored, 16)
            sp.wait_ge(y_stored, 16 * B)

        @block.gpsimd
        def _(pool):
            chain = [0]

            def link(ins):
                chain[0] += 1
                ins.then_inc(pool_chain, 1)
                pool.wait_ge(pool_chain, chain[0])

            nc.gpsimd.memset(half[:], -0.5).then_inc(pool_const, 1)
            link(nc.gpsimd.memset(ident[:], 0.0))
            nc.gpsimd.affine_select(out=ident[:], in_=ident[:], pattern=[[-1, P]], compare_op=ALU.not_equal, fill=1.0,
                                    base=0, channel_multiplier=1).then_inc(pool_const, 1)
            nc.gpsimd.iota(junk[:, 0:P], [[1, P]], base=0, channel_multiplier=-1,
                           allow_small_or_imprecise_dtypes=True).then_inc(pool_const, 1)
            nc.gpsimd.iota(junk[:, P:2 * P], [[1, P]], base=0, channel_multiplier=0,
                           allow_small_or_imprecise_dtypes=True).then_inc(pool_const, 1)
            nc.gpsimd.iota(tiny[:, 0:1], [[0, 1]], base=P, channel_multiplier=-1,
                           allow_small_or_imprecise_dtypes=True).then_inc(pool_const, 1)
            nc.gpsimd.iota(junk[:, 2 * P:3 * P].bitcast(I32), [[0, P]], base=0, channel_multiplier=1).then_inc(pool_const, 1)
            nc.gpsimd.iota(junk[:, 3 * P:4 * P].bitcast(I32), [[1, P]], base=0, channel_multiplier=0).then_inc(pool_const, 1)
            pool.wait_ge(act_const, 1)
            nc.gpsimd.affine_select(out=mask[:], in_=mask[:], pattern=[[0, HEADS], [1, P]], compare_op=ALU.is_ge, fill=0.0,
                                    base=0, channel_multiplier=-1).then_inc(pool_const, 1)

            def wave(w):
                pool.wait_ge(w_ss, 4 * (w + 1))
                nc.gpsimd.tensor_tensor(rows[:, 0, w, :], row_ss[:, w, :], half[:], ALU.pow).then_inc(w_pow, 1)

            def butterflies(t):
                pool.wait_ge(w2_ss, 4 * (t + 1))
                if t:
                    pool.wait_ge(w2_but, t)
                src, dst = w2n[:, t, :], w2p
                for st in range(BUTTERFLIES):
                    a = src.rearrange("p (a c m) -> p a c m", c=2, m=P << st)
                    b = dst.rearrange("p (a c m) -> p a c m", c=2, m=P << st)
                    nc.gpsimd.tensor_tensor(b[:, :, 0, :], a[:, :, 0, :], a[:, :, 1, :], ALU.add)
                    ins = nc.gpsimd.tensor_tensor(b[:, :, 1, :], a[:, :, 0, :], a[:, :, 1, :], ALU.subtract)
                    if st < BUTTERFLIES - 1:
                        link(ins)
                    src, dst = dst, src
                ins.then_inc(w2_but, 1)

            for w in range(WAVES):
                wave(w)
                if w >= 4:
                    butterflies(w - 4)
            pool.wait_ge(w2_tops, 1)
            nc.gpsimd.partition_all_reduce(top_all[:], tops[:], P, bass.bass_isa.ReduceOp.max).then_inc(w2_all, 1)
            pool.wait_ge(w2_all, 1)
            nc.gpsimd.tensor_tensor(tiny[:, 4:5], top_all[:, 1:2], half[:, 0:1], ALU.pow).then_inc(w2_pow, 1)

            def run(place):
                for step, arg in place.steps:
                    if step == "stat":
                        m = place.norm[arg]
                        pool.wait_ge(ln_veps, m + 1)
                        if not known_zero(m):
                            pool.wait_ge(ln_norm, TT * m)
                        nc.gpsimd.tensor_tensor(rstd[:], veps[:], half[:], ALU.pow).then_inc(ln_rstd, 1)
                    elif step == "q":
                        ag = place.attn * GROUPS + arg
                        b, _ = place.filled(step, arg)
                        pool.wait_ge(a_free[b], place.copied(step, arg, b) + 1)
                        nc.gpsimd.tensor_tensor(qdec.rearrange("p (c t) -> p c t", c=TT), qT[:].rearrange("p (c t) -> p c t", c=TT),
                                                lam_t[:, arg:arg + 1, :].to_broadcast([P, TT, P]), ALU.mult).then_inc(q_dec, 1)
                    elif step == "qturn":
                        for r in (2 * arg, 2 * arg + 1):
                            part = 6 if r < QKV_T else 7
                            pool.wait_ge(q_scales, 1)
                            pos, neg = hl[:, r % 2, 0, :], hl[:, r % 2, 1, :]
                            for b in range(2):
                                pool.wait_ge(a_free[b], place.copied(step, arg, b))
                            link(nc.gpsimd.tensor_scalar(pos, wst[:, r, :], tiny[:, part:part + 1], 0.5, ALU.mult, ALU.is_gt))
                            link(nc.gpsimd.tensor_scalar(neg, wst[:, r, :], tiny[:, part:part + 1], -0.5, ALU.mult, ALU.is_lt))
                            nc.gpsimd.tensor_tensor(pos, pos, neg, ALU.subtract).then_inc(q_tern, 1)
                    elif step == "qzero":
                        pool.wait_ge(q_tern, 16)
                        nc.gpsimd.memset(at["qblk"], 0.0).then_inc(qblk_zero, 1)

            program(pool, run)

        def copy_out_w(act, n):
            w, q = divmod(n, 4)
            j = 2 * w + q % 2
            dst = (w1t, w3t)[q // 2]
            nc.scalar.copy(dst[:, :, :, P * j:P * (j + 1)], a_bank16[n % 2]).then_inc(w_copied, 1)

        @block.scalar
        def _(act):
            act.wait_ge(dve_const, 3)
            for h in range(HEADS):
                ins = nc.scalar.activation(mask[:, h, :], junk[:, 0:P], ACT.Exp, scale=s_row[:, h:h + 1])
            ins.then_inc(act_const, 1)
            for g in range(GROUPS):
                nc.scalar.activation(lam_t[:, g, :], junk[:, P:2 * P], ACT.Exp, scale=s_col[:, g:g + 1])
            nc.scalar.activation(lam_rev[:], s_row[:], ACT.Exp, scale=tiny[:, 0:1])
            nc.scalar.activation(lam_T[:], s_col[:], ACT.Exp, scale=float(P))
            nc.scalar.copy(ident16[:], ident[:]).then_inc(act_const, 1)

            for w in range(WAVES):
                for q in range(4):
                    n = 4 * w + q
                    act.wait_ge(w_sc, w + 1)
                    if n >= 2:
                        act.wait_ge(a_ready[n % 2], (n - 2) // 2 + 1)
                        copy_out_w(act, n - 2)
                    nc.scalar.activation(hl[:, n % 2, 0, :], stage[:, w % 2, q, :], ACT.Copy,
                                         scale=row_sc[:, w, q:q + 1]).then_inc(w_hi, 1)
            for n in range(4 * WAVES - 2, 4 * WAVES):
                act.wait_ge(a_ready[n % 2], n // 2 + 1)
                copy_out_w(act, n)
            for j in range(HT + 1):
                if j < HT:
                    act.wait_ge(w2_tr, j + 1)
                    if j >= 2:
                        act.wait_ge(w2_had, j - 1)
                    nc.scalar.copy(w2c[:, j % 2, :], a_bank[j % 2][:]).then_inc(w2_c, 1)
                if j:
                    act.wait_ge(w2_had, j)
                    act.wait_ge(w2_f, 1)
                    nc.scalar.activation(w2t[:, 0, j - 1, :], d_bank[(j - 1) % 4][:], ACT.Copy,
                                         scale=f2[:, j - 1:j]).then_inc(w2_hi, 1)

            def run(place):
                n = place.ffn
                for step, arg in place.steps:
                    use = place.uses.get((step, arg))
                    if step == "gate":
                        j = arg
                        act.wait_ge(g_ready, n * HT + (j + 1))
                        if not known_zero(n * HT + j):
                            act.wait_ge(hfull_ready, n * HT + j)
                        nc.scalar.activation(gate, g_bank[:], ACT.Silu, scale=g_scale[:, j:j + 1]).then_inc(gate_ready, 1)
                    elif step == "lin":
                        j = arg
                        act.wait_ge(hfull_ready, n * HT + (j + 1))
                        if j == 1 and not known_zero(n):
                            act.wait_ge(d_ready, n * TT)
                        elif j != 1 and not known_zero(n * (HT - 1) + max(j - 1, 0)):
                            act.wait_ge(d_step, n * (HT - 1) + max(j - 1, 0))
                        nc.scalar.copy(hid[:, j % 2, 0, :], hfull).then_inc(hi_ready, 1)
                    elif step == "turn":
                        which, t = arg
                        b, fill = place.filled(step, arg)
                        act.wait_ge(a_ready[b], fill)
                        nc.scalar.copy(norm_target(place, which)[:, 0, :, P * t:P * (t + 1)],
                                       a_bank[b][:].rearrange("p (k t) -> p k t", k=KT)).then_inc(a_free[b], 1)
                    elif step == "qturn":
                        b, fill = place.filled(step, arg)
                        act.wait_ge(a_ready[b], fill)
                        dst, r = (wqkv, 2 * arg) if 2 * arg < QKV_T else (wproj, 2 * arg - QKV_T)
                        nc.scalar.copy(dst[:, :, P * r:P * (r + 2)].rearrange("p k (a t) -> p a k t", a=2),
                                       a_bank16[b]).then_inc(a_free[b], 1)
                    elif step == "q":
                        b, fill = place.filled(step, arg)
                        act.wait_ge(a_ready[b], fill)
                        ag = place.attn * GROUPS + arg
                        if not known_zero(ag):
                            act.wait_ge(q_spread, ag)
                            act.wait_ge(q_dec, ag)
                        nc.scalar.activation(qT[:], a_bank[b][:], ACT.Copy, scale=q_scale[:]).then_inc(a_free[b], 1)
                        act.wait_ge(a_free[b], place.copied(step, arg, b) + 1)
                        act.wait_ge(qblk_zero, 1)
                        for h in range(HG):
                            rows_h = slice(HD * h, HD * (h + 1))
                            ins = nc.scalar.copy(qblk[rows_h, :, h, :], qT[rows_h, :].rearrange("p (c t) -> p c t", c=TT))
                        ins.then_inc(q_spread, 1)
                    elif step == "k":
                        b, fill = place.filled(step, arg)
                        act.wait_ge(a_ready[b], fill)
                        nc.scalar.activation(kT, a_bank[b][:], ACT.Copy, scale=kv_scale[:]).then_inc(a_free[b], 1)
                    elif step == "vturn":
                        b, fill = place.filled(step, arg)
                        act.wait_ge(a_ready[b], fill)
                        nc.scalar.copy(at["vnat"], a_bank[b][:]).then_inc(a_free[b], 1)
                    elif step == "pv" and arg[1] == TT - 1:
                        g = arg[0]
                        b, fill = place.filled(step, arg)
                        act.wait_ge(a_ready[b], fill)
                        if g == 0 and not known_zero(place.attn) and place.x is None:
                            act.wait_ge(y_stored, 16 * place.attn)
                        nc.scalar.copy(attention_buffers(place)[0][:, :, P * g:P * (g + 1)],
                                       a_bank[b][:].rearrange("p (c e) -> p c e", c=TT)).then_inc(a_free[b], 1)

            program(act, run)

        @block.vector
        def _(dve):
            chain = [0]

            def link(ins):
                chain[0] += 1
                ins.then_inc(dve_chain, 1)
                dve.wait_ge(dve_chain, chain[0])

            def power(out, in_, flip):
                if flip:
                    return nc.vector.tensor_scalar(out.bitcast(I32), in_.bitcast(I32), EXPONENT, EXPONENT,
                                                   ALU.bitwise_and, ALU.bitwise_xor)
                return nc.vector.tensor_scalar(out.bitcast(I32), in_.bitcast(I32), EXPONENT, None, ALU.bitwise_and)

            dve.wait_ge(rows_loaded, 16 * 4)
            dve.wait_ge(pool_const, 7)
            nc.vector.tensor_scalar(s_row[:], s_row[:], -1.0, None, ALU.mult).then_inc(dve_const, 1)
            dve.wait_ge(dve_const, 1)
            for h in range(HG):
                rows_h = slice(HD * h, HD * (h + 1))
                ins = nc.vector.tensor_copy(s_col[rows_h, :], s_row[rows_h, :].rearrange("p (g h) -> p h g", h=HG)[:, h, :])
            ins.then_inc(dve_const, 1)
            nc.vector.tensor_scalar(junk[:, 0:P], junk[:, 0:P], 0.0, None, ALU.max).then_inc(dve_const, 1)
            nc.vector.memset(diag[:], 0.0)
            ip, ij = junk[:, 2 * P:3 * P].bitcast(I32), junk[:, 3 * P:4 * P].bitcast(I32)
            link(nc.vector.tensor_tensor(ip, ip, ij, ALU.bitwise_and))
            for shift in (4, 2, 1):
                link(nc.vector.tensor_scalar(ij, ip, shift, None, ALU.logical_shift_right))
                link(nc.vector.tensor_tensor(ip, ip, ij, ALU.bitwise_xor))
            link(nc.vector.tensor_scalar(ip, ip, 1, None, ALU.bitwise_and))
            link(nc.vector.tensor_copy(hadamard[:], ip))
            link(nc.vector.tensor_scalar(hadamard[:], hadamard[:], -2.0, 1.0, ALU.mult, ALU.add))
            for h in range(HG):
                nc.vector.memset(diag[HD * h:HD * (h + 1), HD * h:HD * (h + 1)], 1.0)
            for n, row in ((1, qnw_row), (2, pw_row)):
                link(nc.vector.tensor_reduce(tiny[:, n:n + 1], row[:], AX.X, ALU.max, apply_absolute_value=True))
                link(nc.vector.tensor_scalar(tiny[:, n:n + 1], tiny[:, n:n + 1], TINY, None, ALU.max))
                link(power(tiny[:, n:n + 1], tiny[:, n:n + 1], True))
                link(nc.vector.tensor_scalar(tiny[:, n:n + 1], tiny[:, n:n + 1], 0.25, None, ALU.mult))
                link(nc.vector.tensor_scalar(row[:], row[:], tiny[:, n:n + 1], None, ALU.mult))
                link(nc.vector.reciprocal(tiny[:, 8 + n:9 + n], tiny[:, n:n + 1]))
            dve.wait_ge(act_const, 2)

            def sums(w):
                dve.wait_ge(w_loaded[w % 2], 32 * (w // 2 + 1))
                for q in range(4):
                    t = stage[:, w % 2, q, :]
                    if q:
                        dve.wait_ge(w_ss, 4 * w + q)
                    elif w >= 2 and w - 1 <= KT:
                        dve.wait_ge(w2_ss, 4 * (w - 1))
                    elif w:
                        dve.wait_ge(w_ss, 4 * w)
                    nc.vector.tensor_tensor_reduce(out=junk[:], in0=t, in1=t, scale=1.0, scalar=TINY, op0=ALU.mult,
                                                   op1=ALU.add, accum_out=row_ss[:, w, q:q + 1]).then_inc(w_ss, 1)

            def scales(w):
                dve.wait_ge(w_pow, w + 1)
                link(power(rows[:, 0, w, :], rows[:, 0, w, :], False))
                nc.vector.tensor_scalar(row_sc[:, w, :], rows[:, 0, w, :], W_SCALE, None, ALU.mult).then_inc(w_sc, 1)
                link(power(rows[:, 1, w, :], rows[:, 0, w, :], True))

            def sums2(t):
                dve.wait_ge(w2_loaded[t], 16)
                for q in range(4):
                    v = w2n[:, t, 512 * q:512 * (q + 1)]
                    if q:
                        dve.wait_ge(w2_ss, 4 * t + q)
                    else:
                        dve.wait_ge(w_ss, 4 * (t + 2))
                    nc.vector.tensor_tensor_reduce(out=junk[:], in0=v, in1=v, scale=1.0, scalar=TINY, op0=ALU.mult,
                                                   op1=ALU.add, accum_out=ss2[:, t, q:q + 1]).then_inc(w2_ss, 1)

            sums(0)
            scales(0)
            for w in range(WAVES):
                if w + 1 < WAVES:
                    sums(w + 1)
                for q in range(4):
                    dve.wait_ge(w_hi, 4 * w + q + 1)
                    nc.vector.scalar_tensor_tensor(out=hl[:, q % 2, 1, :], in0=stage[:, w % 2, q, :],
                                                   scalar=row_sc[:, w, q:q + 1], in1=hl[:, q % 2, 0, :],
                                                   op0=ALU.mult, op1=ALU.subtract).then_inc(w_lo, 1)
                if w + 1 < WAVES:
                    scales(w + 1)
                if w < KT:
                    sums2(w)
            inv1 = rows[:, 1, :, 0:2]
            inv3 = rows[:, 1, :, 2:4]
            chunks = [v[:].rearrange("p (w c) -> p w c", c=2) for v in (g_scale, l_scale, f2)]
            nc.vector.tensor_scalar(chunks[0], inv1, 0.5 / (X_SCALE * W_SCALE), None, ALU.mult)
            nc.vector.tensor_scalar(chunks[1], rows[:, 0, :, 0:2], HID_SCALE / (X_SCALE * W_SCALE), None, ALU.mult)
            link(nc.vector.tensor_tensor(chunks[2], inv1, inv3, ALU.mult))
            nc.vector.tensor_reduce(tops[:, 0:1], f2[:], AX.X, ALU.max)
            dve.wait_ge(w2_ss, 4 * KT)
            link(nc.vector.tensor_reduce(tiny[:, 11:11 + KT], ss2[:], AX.X, ALU.add))
            nc.vector.tensor_reduce(tops[:, 1:2], tiny[:, 11:11 + KT], AX.X, ALU.max).then_inc(w2_tops, 1)
            dve.wait_ge(w2_pow, 1)
            link(power(tiny[:, 5:6], tiny[:, 4:5], False))
            link(power(tiny[:, 4:5], top_all[:, 0:1], True))
            link(nc.vector.tensor_tensor(tiny[:, 5:6], tiny[:, 5:6], tiny[:, 4:5], ALU.mult))
            link(nc.vector.tensor_scalar(tiny[:, 5:6], tiny[:, 5:6], 2.0 * HID_SCALE / 2.0 ** 6 * W_SCALE, None, ALU.mult))
            nc.vector.tensor_scalar(f2[:], f2[:], tiny[:, 5:6], 0.25 / HID_SCALE, ALU.mult, ALU.mult).then_inc(w2_f, 1)
            link(nc.vector.reciprocal(ffn_unscale[:], tiny[:, 5:6]))
            link(nc.vector.tensor_scalar(ffn_unscale[:], ffn_unscale[:], 0.5 / float(np.sqrt(H)), None, ALU.mult))
            for j in range(HT):
                dve.wait_ge(w2_hi, j + 1)
                nc.vector.scalar_tensor_tensor(out=w2t[:, 1, j, :], in0=d_bank[j % 4][:], scalar=f2[:, j:j + 1],
                                               in1=w2t[:, 0, j, :], op0=ALU.mult, op1=ALU.subtract).then_inc(w2_lo, 1)
            dve.wait_ge(w2_had, HT)
            nc.vector.memset(ones[:], 1.0).then_inc(q_ones, 1)

            def run(place):
                n, a = place.ffn, place.attn
                for step, arg in place.steps:
                    if step == "lin":
                        j = arg
                        dve.wait_ge(l_ready, n * HT + (j + 1))
                        dve.wait_ge(gate_ready, n * HT + (j + 1))
                        if not known_zero(n * HT + j):
                            dve.wait_ge(lo_ready, n * HT + j)
                        nc.vector.scalar_tensor_tensor(out=hfull, in0=l_bank[:], scalar=l_scale[:, j:j + 1], in1=gate,
                                                       op0=ALU.mult, op1=ALU.mult).then_inc(hfull_ready, 1)
                        dve.wait_ge(hi_ready, n * HT + (j + 1))
                        nc.vector.tensor_tensor(hid[:, j % 2, 1, :], hfull, hid[:, j % 2, 0, :],
                                                ALU.subtract).then_inc(lo_ready, 1)
                    elif step == "resid":
                        which, t = arg
                        src, dst = (xin, x1) if which == "ffn1" else (place.x2, place.x2)
                        dve.wait_ge(d_ready, n * TT + (t + 1))
                        nc.vector.scalar_tensor_tensor(out=dst[:, t, :], in0=d_bank[t][:], scalar=ffn_unscale[:],
                                                       in1=src[:, t, :], op0=ALU.mult, op1=ALU.add).then_inc(res_done, 1)
                    elif step == "stat" and arg != "o":
                        m, m_ln = place.norm[arg], place.stats[arg]
                        src = norm_source(place, arg)
                        if arg == "ffn1":
                            dve.wait_ge(x_loaded, 16 * (place.loaded + 1))
                        elif arg == "qkv":
                            dve.wait_ge(res_done, TT * n)
                        else:
                            for b in range(2):
                                dve.wait_ge(a_free[b], place.copied(step, arg, b))
                        for t in range(TT):
                            nc.vector.bn_stats(stat[:, t, :], src[:, t, :]).then_inc(ln_stats, 1)
                        dve.wait_ge(ln_stats, TT * (m_ln + 1))
                        even, odd = stat[:, 0:TT, 1], stat[:, 0:TT, 4]
                        nc.vector.tensor_tensor(mean[:], even, odd, ALU.add).then_inc(ln_small, 1)
                        nc.vector.tensor_tensor(ms[:, 0, 0:TT], even, odd, ALU.subtract).then_inc(ln_small, 1)
                        nc.vector.tensor_tensor(ms[:, 1, 0:TT], stat[:, 0:TT, 2], stat[:, 0:TT, 5], ALU.add).then_inc(ln_small, 1)
                        base = 5 * m_ln
                        dve.wait_ge(ln_small, base + 2)
                        nc.vector.tensor_tensor(ms[:, 0, 0:TT], ms[:, 0, 0:TT], ms[:, 0, 0:TT], ALU.mult).then_inc(ln_small, 1)
                        nc.vector.tensor_scalar(mean[:], mean[:], 0.5, None, ALU.mult)
                        dve.wait_ge(ln_small, base + 4)
                        nc.vector.scalar_tensor_tensor(out=ms[:, 0, 0:TT], in0=ms[:, 0, 0:TT], scalar=D / 4.0,
                                                       in1=ms[:, 1, 0:TT], op0=ALU.mult, op1=ALU.add).then_inc(ln_small, 1)
                        dve.wait_ge(ln_small, base + 5)
                        if not known_zero(m):
                            dve.wait_ge(ln_rstd, m)
                        mul, add = (1.0 + RMS_EPS, LN_EPS * RMS_EPS) if arg == "qkv" else (1.0, LN_EPS)
                        nc.vector.tensor_scalar(veps[:], ms[:, 0, 0:TT], mul / D / X_SCALE ** 2, add / X_SCALE ** 2,
                                                ALU.mult, ALU.add).then_inc(ln_veps, 1)
                    elif step == "ostat":
                        t = arg
                        src = attention_buffers(place)[0]
                        dve.wait_ge(a_free[1], place.copied(step, arg, 1))
                        nc.vector.bn_stats(stat[:, t, :], src[:, t, :]).then_inc(o_stats, 1)
                        nc.vector.tensor_tensor(src[:, t, :], src[:, t, :], nw_row[:], ALU.mult).then_inc(o_scaled, 1)
                        dve.wait_ge(o_scaled, TT * a + (t + 1))
                        nc.vector.bn_stats(stat[:, TT + t, :], src[:, t, :]).then_inc(o_stats, 1)
                    elif step == "stat":
                        m = place.norm[arg]
                        dve.wait_ge(o_stats, 2 * TT * (a + 1))
                        even, odd = stat[:, :, 1], stat[:, :, 4]
                        base = 6 * a
                        nc.vector.tensor_tensor(ms[:, 0, :], even, even, ALU.mult).then_inc(o_small, 1)
                        nc.vector.tensor_tensor(ms[:, 1, :], odd, odd, ALU.mult).then_inc(o_small, 1)
                        nc.vector.tensor_tensor(ms[:, 2, :], stat[:, :, 2], stat[:, :, 5], ALU.add).then_inc(o_small, 1)
                        dve.wait_ge(o_small, base + 2)
                        nc.vector.tensor_tensor(ms[:, 0, :], ms[:, 0, :], ms[:, 1, :], ALU.add).then_inc(o_small, 1)
                        dve.wait_ge(o_small, base + 4)
                        nc.vector.scalar_tensor_tensor(out=ms[:, 1, :], in0=ms[:, 0, :], scalar=D / 2.0,
                                                       in1=ms[:, 2, :], op0=ALU.mult, op1=ALU.add).then_inc(o_small, 1)
                        dve.wait_ge(o_small, base + 5)
                        nc.vector.scalar_tensor_tensor(out=ms[:, 0, 0:TT], in0=ms[:, 1, 0:TT], scalar=RMS_EPS,
                                                       in1=ms[:, 1, TT:2 * TT], op0=ALU.mult, op1=ALU.add).then_inc(o_small, 1)
                        dve.wait_ge(o_small, base + 6)
                        dve.wait_ge(ln_rstd, m)
                        nc.vector.tensor_scalar(veps[:], ms[:, 0, 0:TT], D * RMS_EPS * OUT_NORM_EPS, 1.0 / D / X_SCALE ** 2,
                                                ALU.add, ALU.mult).then_inc(ln_veps, 1)
                    elif step == "prep":
                        which, t = arg
                        m = place.norm[which]
                        src = norm_source(place, which)[:, t, :]
                        dve.wait_ge(ln_rstd, m + 1)
                        if place.steps is TWO_NORMS and t < 2:
                            for b in range(2):
                                dve.wait_ge(a_free[b], place.copied(step, arg, b))
                        if which == "qkv":
                            nc.vector.scalar_tensor_tensor(out=cent[:, t % 2], in0=src, scalar=mean[:, t:t + 1], in1=qnw_row[:],
                                                           op0=ALU.subtract, op1=ALU.mult).then_inc(ln_cent, 1)
                            dve.wait_ge(ln_cent, TT * a + (t + 1))
                            ins = nc.vector.tensor_scalar(cent[:, t % 2], cent[:, t % 2], rstd[:, t:t + 1], None, ALU.mult)
                        elif which == "o":
                            ins = nc.vector.scalar_tensor_tensor(out=cent[:, t % 2], in0=src, scalar=rstd[:, t:t + 1],
                                                                 in1=pw_row[:], op0=ALU.mult, op1=ALU.mult)
                        else:
                            ins = nc.vector.tensor_scalar(cent[:, t % 2], src, mean[:, t:t + 1], rstd[:, t:t + 1],
                                                          ALU.subtract, ALU.mult)
                        ins.then_inc(ln_norm, 1)
                    elif step == "turn":
                        which, t = arg
                        b, fill = place.filled(step, arg)
                        dst = norm_target(place, which)[:, :, :, P * t:P * (t + 1)]
                        dve.wait_ge(a_ready[b], fill)
                        dve.wait_ge(a_free[b], place.copied(step, arg, b) + 1)
                        nc.vector.tensor_tensor(dst[:, 1], a_bank[b][:].rearrange("p (k t) -> p k t", k=KT), dst[:, 0],
                                                ALU.subtract).then_inc(a_free[b], 1)
                    elif step == "qsum":
                        dve.wait_ge(wst_loaded[arg], 16)
                        nc.vector.tensor_reduce(asum[:, 4 * arg:4 * arg + 4], wst[:, 4 * arg:4 * arg + 4, :], AX.X, ALU.add,
                                                apply_absolute_value=True).then_inc(q_sum, 1)
                    elif step == "qtot":
                        b, fill = place.filled(step, arg)
                        dve.wait_ge(a_ready[b], fill)
                        nc.vector.tensor_reduce(tiny[:, 3:4], a_bank[b][:, 0:QKV_T], AX.X, ALU.add)
                        nc.vector.tensor_reduce(tiny[:, 4:5], a_bank[b][:, QKV_T:16], AX.X, ALU.add).then_inc(a_free[b], 1)
                        dve.wait_ge(a_free[b], place.copied(step, arg, b) + 1)
                        nc.vector.tensor_scalar(tiny[:, 3:4], tiny[:, 3:4], 1.0 / (3 * D * D), 1e-5, ALU.mult, ALU.max)
                        link(nc.vector.tensor_scalar(tiny[:, 4:5], tiny[:, 4:5], 1.0 / (D * D), 1e-5, ALU.mult, ALU.max))
                        link(nc.vector.reciprocal(tiny[:, 6:8], tiny[:, 3:5]))
                        link(nc.vector.tensor_scalar(kv_scale[:], tiny[:, 3:4], tiny[:, 9:10], 1.0 / X_SCALE, ALU.mult, ALU.mult))
                        nc.vector.tensor_scalar(proj_scale[:], tiny[:, 4:5], tiny[:, 10:11], 1.0 / X_SCALE, ALU.mult, ALU.mult)
                        nc.vector.tensor_scalar(q_scale[:], kv_scale[:], QK_SCALE, None, ALU.mult).then_inc(q_scales, 1)
                    elif step == "v":
                        b, fill = place.filled(step, arg)
                        dve.wait_ge(a_ready[b], fill)
                        nc.vector.tensor_scalar(vT, a_bank[b][:], kv_scale[:], None, ALU.mult).then_inc(a_free[b], 1)
                    elif step == "kturn":
                        g = arg
                        b, fill = place.filled(step, arg)
                        dve.wait_ge(a_ready[b], fill)
                        n_c = TT - 1
                        dec = lam_rev[:, HG * g:HG * (g + 1)]
                        for c in range(n_c):
                            ins = nc.vector.tensor_tensor(
                                kdec[:, c, :].rearrange("p (h d) -> p h d", h=HG),
                                a_bank[b][:, P * c:P * (c + 1)].rearrange("p (h d) -> p h d", h=HG),
                                dec.rearrange("p (h a) -> p h a", a=1).to_broadcast([P, HG, HD]), ALU.mult)
                        ins.then_inc(a_free[b], 1)
                    elif step == "score":
                        g, c = arg
                        b, fill = place.filled(step, arg)
                        dve.wait_ge(a_ready[b], fill)
                        nc.vector.tensor_tensor(sc[:, c % 2], a_bank[b][:].rearrange("p (h t) -> p h t", h=HG),
                                                mask[:, HG * g:HG * (g + 1), :], ALU.mult).then_inc(a_free[b], 1)
                    elif step == "kv":
                        g = arg
                        b, fill = place.filled(step, arg)
                        dve.wait_ge(a_ready[b], fill)
                        for c in range(TT - 1):
                            ins = nc.vector.tensor_tensor(state[:, c, :], a_bank[b][:, P * c:P * (c + 1)], diag[:], ALU.mult)
                            if c < TT - 2:
                                ins.then_inc(state_part, 1)
                            else:
                                ins.then_inc(a_free[b], 1)
                        ag = a * GROUPS + g
                        for c in range(1, TT - 1):
                            dve.wait_ge(state_part, (TT - 2) * (ag + 1))
                            if c == TT - 2:
                                dve.wait_ge(a_free[b], place.copied(step, arg, b) + 1)
                                dve.wait_ge(state_done, (TT - 2) * ag + (c - 1))
                            nc.vector.scalar_tensor_tensor(out=state[:, c, :], in0=state[:, c - 1, :], scalar=lam_T[:, g:g + 1],
                                                           in1=state[:, c, :], op0=ALU.mult, op1=ALU.add).then_inc(state_done, 1)
                    elif step == "proj":
                        t = arg
                        b, fill = place.filled(step, arg)
                        dve.wait_ge(a_ready[b], fill)
                        nc.vector.scalar_tensor_tensor(out=attention_buffers(place)[0][:, t, :], in0=a_bank[b][:],
                                                       scalar=proj_scale[:], in1=x1[:, t, :], op0=ALU.mult,
                                                       op1=ALU.add).then_inc(a_free[b], 1)

            program(dve, run)

        @block.tensor
        def _(pe):
            pe.wait_ge(act_const, 2)
            for n in range(4 * WAVES):
                pe.wait_ge(w_lo, n + 1)
                if n >= 2:
                    pe.wait_ge(w_copied, n - 1)
                for part in range(2):
                    for k in range(KT):
                        ins = nc.tensor.transpose(a_bank16[n % 2][:, part, k, :], hl[:, n % 2, part, P * k:P * (k + 1)], ident16[:])
                ins.then_inc(a_ready[n % 2], 1)
            pe.wait_ge(w2_but, KT)
            for j in range(HT + 1):
                if j < HT:
                    if j >= 2:
                        pe.wait_ge(w2_c, j - 1)
                    else:
                        pe.wait_ge(w_copied, 4 * WAVES)
                    for t in range(KT):
                        ins = nc.tensor.transpose(a_bank[j % 2][:, P * t:P * (t + 1)], w2n[:, t, P * j:P * (j + 1)], ident[:])
                    ins.then_inc(w2_tr, 1)
                if j:
                    pe.wait_ge(w2_c, j)
                    if j - 1 >= 4:
                        pe.wait_ge(w2_lo, j - 4)
                    nc.tensor.matmul(d_bank[(j - 1) % 4][:], hadamard[:], w2c[:, (j - 1) % 2, :], start=True,
                                     stop=True).then_inc(w2_had, 1)
            pe.wait_ge(w2_lo, HT)
            def take(place, step, arg):
                b, _ = place.uses[step, arg]
                free = place.copied(step, arg, b)
                if not known_zero(free):
                    pe.wait_ge(a_free[b], free)
                return b

            def landed(place, step, arg, b):
                free = place.copied(step, arg, b)
                if not known_zero(free):
                    pe.wait_ge(a_free[b], free)

            def run(place):
                n = place.ffn
                for step, arg in place.steps:
                    if step in ("gate", "lin"):
                        j = arg
                        src = xt if place.which == "ffn1" else place.y
                        wt, dst, done = (w1t, g_bank, g_ready) if step == "gate" else (w3t, l_bank, l_ready)
                        if step == "gate" and j == 0:
                            for b in range(2):
                                landed(place, step, arg, b)
                        if not known_zero(n * HT + j):
                            pe.wait_ge(gate_ready if step == "gate" else hfull_ready, n * HT + j)
                        for k in range(KT):
                            for wp, xp in ((0, 0), (0, 1), (1, 0)):
                                ins = nc.tensor.matmul(dst[:], wt[:, wp, k, P * j:P * (j + 1)], src[:, xp, k, :],
                                                       start=(k == 0 and wp == xp), stop=(k == KT - 1 and wp == 1))
                        ins.then_inc(done, 1)
                    elif step == "down":
                        j = arg
                        pe.wait_ge(lo_ready, n * HT + (j + 1))
                        if j == 0 and not known_zero(n):
                            pe.wait_ge(res_done, n * TT)
                        for t in range(TT):
                            for hp, wp in ((0, 0), (0, 1), (1, 0)):
                                ins = nc.tensor.matmul(d_bank[t][:], hid[:, j % 2, hp, P * t:P * (t + 1)], w2t[:, wp, j, :],
                                                       start=(j == 0 and hp == wp), stop=(j == HT - 1 and hp == 1))
                            if j == HT - 1:
                                ins.then_inc(d_ready, 1)
                        if j < HT - 1:
                            ins.then_inc(d_step, 1)
                    elif step == "turn":
                        which, t = arg
                        m = place.norm[which]
                        b = take(place, step, arg)
                        pe.wait_ge(ln_norm, TT * m + (t + 1))
                        for k in range(KT):
                            ins = nc.tensor.transpose(a_bank[b][:, P * k:P * (k + 1)], cent[:, t % 2, P * k:P * (k + 1)], ident[:])
                        ins.then_inc(a_ready[b], 1)
                    elif step == "qtot":
                        b = take(place, step, arg)
                        pe.wait_ge(q_ones, 1)
                        pe.wait_ge(q_sum, 4)
                        nc.tensor.matmul(a_bank[b][:, 0:16], ones[:], asum[:], start=True, stop=True).then_inc(a_ready[b], 1)
                    elif step == "qturn":
                        b = take(place, step, arg)
                        pe.wait_ge(q_tern, 2 * (arg + 1))
                        for r in range(2):
                            for k in range(KT):
                                ins = nc.tensor.transpose(a_bank16[b][:, r, k, :], hl[:, r, 0, P * k:P * (k + 1)], ident16[:])
                        ins.then_inc(a_ready[b], 1)
                    elif step in ("q", "k", "v"):
                        g = arg
                        b = take(place, step, arg)
                        if g == 0:
                            for other in range(2):
                                landed(place, step, arg, other)
                        src = attention_buffers(place)[1]
                        col = "qkv".index(step) * D + P * g
                        for k in range(KT):
                            for part in range(2):
                                ins = nc.tensor.matmul(a_bank[b][:], wqkv[:, k, col:col + P], src[:, part, k, :],
                                                       start=(k == 0 and part == 0), stop=(k == KT - 1 and part == 1))
                        ins.then_inc(a_ready[b], 1)
                    elif step in ("vturn", "kturn"):
                        b = take(place, step, arg)
                        src, n_c = (vT, TT) if step == "vturn" else (kT, TT - 1)
                        for c in range(n_c):
                            ins = nc.tensor.transpose(a_bank[b][:, P * c:P * (c + 1)], src[:, P * c:P * (c + 1)], ident[:])
                        ins.then_inc(a_ready[b], 1)
                    elif step == "score":
                        g, c = arg
                        b = take(place, step, arg)
                        if c == 0:
                            pe.wait_ge(q_spread, place.attn * GROUPS + (g + 1))
                            landed(place, step, arg, 1)
                        nc.tensor.matmul(a_bank[b][:], kT[:, P * c:P * (c + 1)], qblk[:, c].rearrange("p h t -> p (h t)"),
                                         start=True, stop=True).then_inc(a_ready[b], 1)
                    elif step == "kv":
                        g = arg
                        b = take(place, step, arg)
                        pe.wait_ge(a_free[0], place.copied("score", (g, 0), 0))
                        for c in range(TT - 1):
                            ins = nc.tensor.matmul(a_bank[b][:, P * c:P * (c + 1)], kdec[:, c, :], vnat[:, c, :],
                                                   start=True, stop=True)
                        ins.then_inc(a_ready[b], 1)
                    elif step == "pv":
                        g, c = arg
                        b = place.uses[step, arg][0]
                        if c == 0:
                            take(place, step, arg)
                        pe.wait_ge(a_free[0], place.copied("score", arg, 0) + 1)
                        if c:
                            if c == 1:
                                pe.wait_ge(q_dec, place.attn * GROUPS + (g + 1))
                            if c >= 2:
                                pe.wait_ge(state_done, (TT - 2) * (place.attn * GROUPS + g) + (c - 1))
                            nc.tensor.matmul(a_bank[b][:, P * c:P * (c + 1)], qdec[:, P * c:P * (c + 1)], state[:, c - 1, :],
                                             start=False, stop=False, skip_group_check=True)
                        for h in range(HG):
                            col = P * c + HD * h
                            ins = nc.tensor.matmul(a_bank[b][:, col:col + HD], sc[:, c % 2, h, :], vnat[:, c, HD * h:HD * (h + 1)],
                                                   start=(c == 0 and h == 0), stop=True, skip_group_check=True)
                        if c == TT - 1:
                            ins.then_inc(a_ready[b], 1)
                    elif step == "proj":
                        t = arg
                        b = take(place, step, arg)
                        if t == 0:
                            for other in range(2):
                                landed(place, step, arg, other)
                        src = attention_buffers(place)[1]
                        for k in range(KT):
                            for part in range(2):
                                ins = nc.tensor.matmul(a_bank[b][:], src[:, part, k, P * t:P * (t + 1)], wproj[:, k, :],
                                                       start=(k == 0 and part == 0), stop=(k == KT - 1 and part == 1))
                        ins.then_inc(a_ready[b], 1)

            program(pe, run)


_INS = ["L0_attn_x", "L0_attn_qkv_w", "L0_attn_qkv_norm_w", "L0_attn_proj_w", "L0_attn_proj_norm_w", "L0_attn_norm_w",
        "L0_attn_s", "L0_ffn_W1", "L0_ffn_W2", "L0_ffn_W3"]


def kernel(**inputs):
    import numpy as _np
    import concourse.bacc as _bacc
    from concourse import mybir as _mybir
    from concourse.bass_utils import run_bass_kernel_spmd as _run

    nc = _bacc.Bacc("TRN2", target_bir_lowering=False, num_devices=1)
    arrays, args = {}, []
    for name in _INS:
        a = _np.ascontiguousarray(inputs[name])
        arrays[f"in_{name}_dram"] = a
        args.append(nc.dram_tensor(f"in_{name}_dram", a.shape, _mybir.dt.from_np(a.dtype), kind="ExternalInput").ap())
    args.append(nc.dram_tensor("out_0_dram", inputs["L0_attn_x"].shape, _mybir.dt.float32, kind="ExternalOutput").ap())
    macaron_kernel(nc, *args)
    return _run(nc, [arrays], core_ids=[0]).results[0]["out_0_dram"]
```

```python
from contextlib import ExitStack

import numpy as np

import concourse.bass as bass
from concourse import mybir

ALU = mybir.AluOpType
ACT = mybir.ActivationFunctionType
AX = mybir.AxisListType
F32 = mybir.dt.float32
F16 = mybir.dt.float16
I32 = mybir.dt.int32

P = 128
EXPONENT = 0x7F800000
LN_EPS = 1e-5
RMS_EPS = float(np.finfo(np.float32).eps)
OUT_NORM_EPS = 1e-6
TINY = 1e-30
X_SCALE = 2.0 ** 11
W_SCALE = 2.0 ** 15


def macaron_kernel(nc, x, qkv_w, qkv_norm_w, proj_w, proj_norm_w, norm_w, s, w1, w2, w3, out):
    B, T, D = x.shape
    H = w1.shape[0]
    HEADS = s.shape[0]
    HD = D // HEADS
    TT = T // P
    KT = D // P
    HT = H // P
    HG = P // HD
    GROUPS = HEADS // HG
    QKV_T = 3 * D // P
    PROJ_T = D // P
    QK_SCALE = float(HD) ** -0.5
    STAGES = 4
    FOURTHS = 4
    BUTTERFLIES = HT.bit_length() - 1
    assert (D, T, HG, QKV_T, PROJ_T, HT) == (512, 512, 4, 12, 4, 16)

    HID_SCALE = W_SCALE / D

    ctx = ExitStack()
    with ctx:
        def sb(name, shape, dt=F32):
            return ctx.enter_context(nc.sbuf_tensor(name, shape, dt))

        def sem(name):
            return ctx.enter_context(nc.semaphore(name))

        w1t = sb("w1t", [P, 2, KT, H], F16)
        w3t = sb("w3t", [P, 2, KT, H], F16)
        w2t = sb("w2t", [P, 2, HT, D], F16)
        wqkv = sb("wqkv", [P, KT, 3 * D], F16)
        wproj = sb("wproj", [P, KT, D], F16)
        mask = sb("mask", [P, HEADS, P])
        xin = sb("xin", [P, TT, D])
        xt = sb("xt", [P, 2, KT, T], F16)
        cent = sb("cent", [P, 2, D])
        tern = cent[:].bitcast(F16).rearrange("p b (a d) -> p b a d", a=2)
        qT = sb("qT", [P, T])
        junk = qT
        sizes = dict(x1=TT * D, hid=2 * D, gate=D, hfull=D, x2=TT * D, yt=KT * T, qblk=TT * HG * P, qdec=T, kT=T,
                     vnat=T, kdec=(TT - 1) * P, sc=2 * HG * P, state=(TT - 1) * P)
        work = sb("work", [P, sum(sizes.values())])
        at, start = {}, 0
        for name, n in sizes.items():
            at[name] = work[:, start:start + n]
            start += n
        x1 = at["x1"].rearrange("p (t d) -> p t d", t=TT)
        x2 = at["x2"].rearrange("p (t d) -> p t d", t=TT)
        yt = at["yt"].bitcast(F16).rearrange("p (a k t) -> p a k t", a=2, k=KT)
        hid = at["hid"].bitcast(F16).rearrange("p (b a t) -> p b a t", b=2, a=2)
        gate, hfull, qdec, kT = at["gate"], at["hfull"], at["qdec"], at["kT"]
        qblk = at["qblk"].rearrange("p (c h t) -> p c h t", c=TT, h=HG)
        vnat = at["vnat"].rearrange("p (c e) -> p c e", c=TT)
        kdec = at["kdec"].rearrange("p (c e) -> p c e", c=TT - 1)
        sc = at["sc"].rearrange("p (b h t) -> p b h t", b=2, h=HG)
        vT = at["sc"][:, 0:T]
        state = at["state"].rearrange("p (c e) -> p c e", c=TT - 1)
        first = sizes["x1"] + sizes["hid"] + sizes["gate"] + sizes["hfull"]
        w2n = work[:, first:first + KT * H].rearrange("p (t h) -> p t h", t=KT)
        wst = work[:, first:first + 16 * D].rearrange("p (r d) -> p r d", r=16)
        w2c = [gate, hfull]
        early = w2t[:].rearrange("p a j d -> p (a j d)").bitcast(F32)
        n_stage = STAGES * 2 * D
        stage = early[:, 0:n_stage].rearrange("p (b m d) -> p b m d", b=STAGES, m=2)
        w2p = early[:, n_stage:n_stage + H]
        qst = early[:, n_stage + H:n_stage + H + 4 * D].rearrange("p (r d) -> p r d", r=4)
        x_next = mask[:].rearrange("p h t -> p (h t)").rearrange("p (t d) -> p t d", t=TT)
        keep = ([wqkv[:].rearrange("p k d -> p (k d)")[:, 2 * T * i:2 * T * (i + 1)] for i in range(6)]
                + [wproj[:].rearrange("p k d -> p (k d)")[:, 2 * T * i:2 * T * (i + 1)] for i in range(2)]
                + [at["x1"].bitcast(F16)[:, 2 * T * i:2 * T * (i + 1)] for i in range(4)]
                + [work[:, first + KT * H + T * i:first + KT * H + T * (i + 1)].bitcast(F16) for i in range(2)])
        first_hid = [v.rearrange("p (a t) -> p a t", a=2) for v in keep] + [hid[:, 0], hid[:, 1]]
        ident = sb("ident", [P, P])
        ident16 = sb("ident16", [P, P], F16)
        hadamard = sb("hadamard", [P, P])
        lam_t = sb("lam_t", [P, GROUPS, P])
        lam_rev = sb("lam_rev", [P, HEADS])
        lam_T = sb("lam_T", [P, GROUPS])
        diag = sb("diag", [P, P])
        qnw_row = sb("qnw_row", [P, D])
        nw_row = sb("nw_row", [P, D])
        pw_row = sb("pw_row", [P, D])
        s_row = sb("s_row", [P, HEADS])
        s_col = sb("s_col", [P, GROUPS])
        rows = sb("rows", [P, 2, HT, 2])
        row_ss = sb("row_ss", [P, HT, 2])
        row_sc = sb("row_sc", [P, HT, 2])
        g_scale = sb("g_scale", [P, HT])
        l_scale = sb("l_scale", [P, HT])
        f2 = sb("f2", [P, HT])
        ss2 = sb("ss2", [P, KT, 4])
        tops = sb("tops", [P, 2])
        top_all = sb("top_all", [P, 2])
        half = sb("half", [P, 4])
        asum = sb("asum", [P, 16])
        asum_all = sb("asum_all", [P, 16])
        tiny = sb("tiny", [P, 16])
        ffn_unscale = sb("ffn_unscale", [P, 1])
        q_scale = sb("q_scale", [P, 1])
        kv_scale = sb("kv_scale", [P, 1])
        proj_scale = sb("proj_scale", [P, 1])
        stat = sb("stat", [P, 2 * TT, 6])
        mean = sb("mean", [P, TT])
        ms = sb("ms", [P, 3, 2 * TT])
        veps = sb("veps", [P, TT])
        rstd = sb("rstd", [P, TT])

        def bank(name):
            return ctx.enter_context(nc.psum_tensor(name, [P, 512], F32))

        g_bank, l_bank = bank("g_bank"), bank("l_bank")
        d_bank = [bank(f"d_bank{t}") for t in range(TT)]
        a_bank = [bank("a_bank0"), bank("a_bank1")]
        had_bank = [g_bank, l_bank]
        a_bank16 = [b[:].bitcast(F16).rearrange("p (a k t) -> p a k t", a=2, k=KT) for b in a_bank]

        x_loaded, y_stored = sem("x_loaded"), sem("y_stored")
        g_ready, l_ready, d_ready = sem("g_ready"), sem("l_ready"), sem("d_ready")
        d_step = sem("d_step")
        gate_ready, hfull_ready = sem("gate_ready"), sem("hfull_ready")
        hi_ready, lo_ready = sem("hi_ready"), sem("lo_ready")
        res_done = sem("res_done")
        a_ready = [sem("a_ready0"), sem("a_ready1")]
        a_free = [sem("a_free0"), sem("a_free1")]
        ln_stats, ln_small, ln_veps, ln_rstd = sem("ln_stats"), sem("ln_small"), sem("ln_veps"), sem("ln_rstd")
        ln_cent, ln_norm = sem("ln_cent"), sem("ln_norm")
        q_spread, q_dec = sem("q_spread"), sem("q_dec")
        o_stats, o_scaled, o_small = sem("o_stats"), sem("o_scaled"), sem("o_small")
        state_part, state_done = sem("state_part"), sem("state_done")
        rows_loaded, x_next_loaded = sem("rows_loaded"), sem("x_next_loaded")
        w_loaded = [sem(f"w_loaded{b}") for b in range(STAGES)]
        w2_loaded = [sem(f"w2_loaded{t}") for t in range(KT)]
        qst_loaded = sem("qst_loaded")
        wst_loaded = [sem(f"wst_loaded{q}") for q in range(FOURTHS)]
        pool_const, dve_const, act_const = sem("pool_const"), sem("dve_const"), sem("act_const")
        pool_chain, dve_chain = sem("pool_chain"), sem("dve_chain")
        w_ss, w_sc, w_norm = sem("w_ss"), sem("w_sc"), sem("w_norm")
        w2_ss, w2_but, w2_tops, w2_all, w2_f = sem("w2_ss"), sem("w2_but"), sem("w2_tops"), sem("w2_all"), sem("w2_f")
        w2_had, w2_hi, w2_lo = sem("w2_had"), sem("w2_hi"), sem("w2_lo")
        q_sum, q_all, q_scales, q_scaled, q_tern, qblk_zero = (sem("q_sum"), sem("q_all"), sem("q_scales"), sem("q_scaled"),
                                                               sem("q_tern"), sem("q_zero"))
        decay_numbers, decay_rates, decay_exp = sem("decay_numbers"), sem("decay_rates"), sem("decay_exp")

        def feed_forward(which, slots):
            steps = []
            for j in range(HT):
                steps += [("gate", j)] + slots.get(3 * j, []) + [("lin", j)] + slots.get(3 * j + 1, [])
                if j:
                    steps += [("down", j - 1)]
                steps += slots.get(3 * j + 2, [])
            return steps + [("down", HT - 1)] + slots.get(3 * HT, []) + [("resid", (which, t)) for t in range(TT)]

        def norm_steps(which):
            pre = [("stat", which), ("prep", (which, 0)), ("prep", (which, 1))]
            tr0 = [("turn", (which, 0)), ("prep", (which, 2)), ("turn", (which, 1)), ("prep", (which, 3))]
            tr1 = [("turn", (which, 2)), ("turn", (which, 3))]
            return pre, tr0, tr1

        def add(slots, at, steps):
            slots.setdefault(at, []).extend(steps)

        def attention_slots(at):
            slots = {}
            pre, tr0, tr1 = norm_steps("qkv")
            add(slots, at, tr0)
            add(slots, at + 1, tr1)
            at += 2
            for g in range(GROUPS):
                add(slots, at, [("q", g)])
                add(slots, at + 1, [("v", g), ("k", g)])
                add(slots, at + 2, [("vturn", g), ("kturn", g)])
                add(slots, at + 3, [("score", (g, 0)), ("kv", g)])
                for c in range(1, TT):
                    add(slots, at + 3 + c, [("score", (g, c)), ("pv", (g, c - 1))])
                at += 3 + TT
                add(slots, at, [("pv", (g, TT - 1))])
            pre, tr0, tr1 = norm_steps("o")
            add(slots, at + 1, [("ostat", 0), ("ostat", 1)])
            add(slots, at + 4, [("ostat", 2), ("ostat", 3)])
            add(slots, at + 6, pre)
            add(slots, at + 8, tr0)
            add(slots, at + 9, tr1)
            add(slots, at + 10, [("proj", 0), ("proj", 1)])
            add(slots, at + 11, [("proj", 2), ("proj", 3)])
            pre, tr0, tr1 = norm_steps("ffn2")
            add(slots, at + 12, pre[:1])
            add(slots, at + 13, pre[1:])
            add(slots, at + 15, tr0)
            add(slots, at + 16, tr1)
            assert at + 16 <= 3 * HT
            return slots

        def second_slots():
            slots = {}
            pre, tr0, tr1 = norm_steps("ffn1")
            add(slots, 10, pre)
            add(slots, 14, tr0)
            add(slots, 15, tr1)
            add(slots, 40, norm_steps("qkv")[0])
            return slots

        def last_attention_slots():
            slots = attention_slots(2)
            return {**slots, 0: norm_steps("qkv")[0]}

        def first_steps():
            pre, tr0, tr1 = norm_steps("ffn1")
            steps = [("wsum", 0), ("wsum", 1), pre[0], ("wscale", 0)] + pre[1:] + tr0 + [("wsum", 2), ("wsum", 3)]
            steps += [("turn", ("ffn1", 2)), ("wprep", 0), ("turn", ("ffn1", 3)), ("wprep", 1)]
            steps += [("wturn", 0), ("wprep", 2), ("wturn", 1), ("wprep", 3), ("wscale", 1)]
            flies = [(t, st) for t in range(KT) for st in range(BUTTERFLIES)]
            n_pre, n_tr0, n_tr1 = norm_steps("next")
            for j in range(HT):
                steps += [("gate", j)]
                if j < HT - 4:
                    steps += [("wsum", j + 4)]
                if j < HT - 1:
                    steps += [("wturn", 2 * j + 2)]
                if j < HT - 2:
                    steps += [("wprep", 2 * j + 4)]
                steps += [("lin", j)]
                if j < HT - 1:
                    steps += [("wturn", 2 * j + 3)]
                if j < HT - 2:
                    steps += [("wprep", 2 * j + 5)]
                if j < HT - 4 and j % 2:
                    steps += [("wscale", (j + 3) // 2)]
                if j < KT:
                    steps += [("w2sum", j)]
                steps += [("fly", f) for f in flies[2 * j:2 * j + 2]]
                if j >= 3 and j % 3 == 0 and j <= 3 * FOURTHS:
                    steps += [("qsum", j // 3 - 1)]
                if j == HT - 3:
                    steps += [("wtop", 0), ("qmean", 0)]
                if j == HT - 1:
                    steps += n_pre
            for j in range(HT + 1):
                if j < HT:
                    steps += [("w2turn", j)]
                if j:
                    steps += [("w2had", j - 1)]
            slots = {0: n_tr0, 1: n_tr1, 2: [("decay", 0)], HT // 2 - 2: [("qprep", 0)]}
            for r in range(8):
                slots[HT // 2 - 1 + r] = [("qturn", r)] + ([("qprep", r + 1)] if r < 7 else [("qzero", 0)])
            for j in range(HT):
                steps += [("down", j)] + slots.get(j, [])
            return steps + [("resid", ("ffn1", t)) for t in range(TT)]

        FIRST = first_steps()
        WITH_ATTENTION = feed_forward("ffn1", attention_slots(0))
        SECOND = feed_forward("ffn2", second_slots())
        SECOND_WITH_ATTENTION = feed_forward("ffn2", last_attention_slots())
        LAST = feed_forward("ffn2", {})
        NORM = norm_steps("qkv")[0]

        def bank_use(step, arg):
            if step == "turn":
                return arg[1] % 2, 2
            if step == "proj":
                return arg % 2, 1
            if step == "wturn":
                return arg % 2, 2
            if step in ("w2turn", "qturn"):
                return arg % 2, 1
            if step == "pv":
                return (1, 1) if arg[1] == 0 else None
            return {"q": (0, 1), "v": (0, 1), "vturn": (0, 1), "score": (0, 1),
                    "k": (1, 1), "kturn": (1, 1), "kv": (1, 1)}.get(step)

        def count_uses(steps):
            fills, copies, uses, before = [0, 0], [0, 0], {}, {}
            for step, arg in steps:
                before[step, arg] = tuple(copies)
                use = bank_use(step, arg)
                if use:
                    uses[step, arg] = (use[0], fills[use[0]])
                    fills[use[0]] += 1
                    copies[use[0]] += use[1]
                elif step == "pv":
                    uses[step, arg] = uses["pv", (arg[0], 0)]
            return uses, before, tuple(fills), tuple(copies)

        USES = {id(x): count_uses(x) for x in (FIRST, WITH_ATTENTION, SECOND, SECOND_WITH_ATTENTION, LAST, NORM)}

        class Place:

            def __init__(self, steps, fills, copies, ffn=0, attn=0, norm=None, stats=None, loaded=0, x2=x2, y=yt, x=None):
                self.steps, self.ffn, self.attn, self.norm, self.stats = steps, ffn, attn, norm or {}, stats or {}
                self.uses, self.before, self.all_fills, self.all_copies = USES[id(steps)]
                self.fills, self.copies, self.x2, self.y = fills, copies, x2, y
                self.x, self.loaded = x, loaded
                self.which = "ffn1" if steps is FIRST or steps is WITH_ATTENTION else "ffn2"

            def filled(self, step, arg):
                b, n = self.uses[step, arg]
                return b, self.fills[b] + (n + 1)

            def copied(self, step, arg, b):
                return self.copies[b] + self.before[step, arg][b]

            def after(self):
                return ([a + n for a, n in zip(self.fills, self.all_fills)],
                        [a + n for a, n in zip(self.copies, self.all_copies)])

        def known_zero(v):
            return isinstance(v, int) and v <= 0

        def program(eng, run):
            place = Place(FIRST, [0, 0], [0, 0], norm={"ffn1": 0, "next": 1}, stats={"ffn1": 0, "next": 1})
            run(place)
            place = Place(NORM, *place.after(), ffn=1, norm={"qkv": 2}, stats={"qkv": 2})
            run(place)
            fills, copies = place.after()
            in_a, in_b = USES[id(WITH_ATTENTION)], USES[id(SECOND)]
            per_fill = [in_a[2][b] + in_b[2][b] for b in range(2)]
            per_copy = [in_a[3][b] + in_b[3][b] for b in range(2)]

            def first_of(i):
                before = i - 1
                m, m_ln = before * 4 + 2, before * 3 + 2
                a = Place(WITH_ATTENTION, [fills[b] + before * per_fill[b] for b in range(2)],
                          [copies[b] + before * per_copy[b] for b in range(2)], ffn=2 * i - 1, attn=before,
                          norm={"qkv": m, "o": m + 1, "ffn2": m + 2}, stats={"qkv": m_ln, "ffn2": m_ln + 1}, loaded=i)
                run(a)
                return a.after(), m + 2, m_ln + 1

            with eng.Fori(1, B - 1) as i:
                counts, m, m_ln = first_of(i)
                run(Place(SECOND, *counts, ffn=2 * i, attn=i, norm={"ffn1": m + 1, "qkv": m + 2},
                          stats={"ffn1": m_ln + 1, "qkv": m_ln + 2}, loaded=i + 1))
            counts, m, m_ln = first_of(B - 1)
            place = Place(SECOND_WITH_ATTENTION, *counts, ffn=2 * B - 2, attn=B - 1,
                          norm={"qkv": m + 1, "o": m + 2, "ffn2": m + 3}, stats={"qkv": m_ln + 1, "ffn2": m_ln + 2},
                          x=(xin, xt))
            run(place)
            run(Place(LAST, *place.after(), ffn=2 * B - 1, x2=xin, y=xt))

        def attention_buffers(place):
            return place.x or (place.x2, place.y)

        def norm_source(place, which):
            return {"ffn1": xin, "next": x_next, "qkv": x1}.get(which) or attention_buffers(place)[0]

        def norm_target(place, which):
            return xt if which in ("ffn1", "next") else attention_buffers(place)[1]

        def hidden(place, j):
            return first_hid[j] if place.steps is FIRST else hid[:, j % 2]

        block = ctx.enter_context(nc.Block())

        @block.sync
        def _(sp):
            def load_chunk(j):
                for m, mat in enumerate((w1, w3)):
                    sp.dma_start(stage[:, j % STAGES, m, :], mat[P * j:P * (j + 1), :]).then_inc(w_loaded[j % STAGES], 16)

            def load_quarter(q, dst, done):
                src = qkv_w[q * D:(q + 1) * D, :] if q < 3 else proj_w
                sp.dma_start(dst, src.rearrange("(c p) d -> p c d", p=P)).then_inc(done, 16)

            load_chunk(0)
            sp.dma_start(xin[:], x[0].rearrange("(t p) d -> p t d", p=P)).then_inc(x_loaded, 16)
            for j in range(1, STAGES):
                load_chunk(j)
            for t in range(KT):
                sp.dma_start(w2n[:, t, :], w2[P * t:P * (t + 1), :]).then_inc(w2_loaded[t], 16)
            load_quarter(0, qst, qst_loaded)
            sp.dma_start(x_next, x[1].rearrange("(t p) d -> p t d", p=P)).then_inc(x_next_loaded, 16)
            for dst, src in ((qnw_row, qkv_norm_w), (nw_row, norm_w), (pw_row, proj_norm_w), (s_row, s)):
                sp.dma_start(dst[:], src.rearrange("(a n) -> a n", a=1).partition_broadcast(P)).then_inc(rows_loaded, 16)
            for j in range(STAGES, HT):
                sp.wait_ge(w_norm, 2 * (j - STAGES + 1))
                load_chunk(j)
                if j >= 9 and j % 3 == 0:
                    q = j // 3 - 2
                    sp.wait_ge(q_sum, q)
                    load_quarter(q, qst, qst_loaded)
            sp.wait_ge(w2_had, HT)
            for q in range(FOURTHS):
                load_quarter(q, wst[:, 4 * q:4 * q + 4, :], wst_loaded[q])
            sp.wait_ge(res_done, TT)
            sp.dma_start(xin[:], x[1].rearrange("(t p) d -> p t d", p=P)).then_inc(x_loaded, 16)
            x_tiles = x.rearrange("b (t p) d -> (b t) p d", p=P)
            out_tiles = out.rearrange("b (t p) d -> (b t) p d", p=P)
            with sp.Fori(1, B - 1) as i:
                sp.wait_ge(res_done, 2 * TT * i)
                sp.dma_start(xin[:], x_tiles[bass.ds((i + 1) * TT, TT)].rearrange("t p d -> p t d")).then_inc(x_loaded, 16)
                sp.wait_ge(res_done, TT * (2 * i + 1))
                sp.dma_start(out_tiles[bass.ds((i - 1) * TT, TT)].rearrange("t p d -> p t d"), x2).then_inc(y_stored, 16)
            sp.wait_ge(res_done, TT * (2 * B - 1))
            sp.dma_start(out_tiles[(B - 2) * TT:(B - 1) * TT].rearrange("t p d -> p t d"), x2).then_inc(y_stored, 16)
            sp.wait_ge(res_done, TT * 2 * B)
            sp.dma_start(out_tiles[(B - 1) * TT:B * TT].rearrange("t p d -> p t d"), xin[:]).then_inc(y_stored, 16)
            sp.wait_ge(y_stored, 16 * B)

        @block.gpsimd
        def _(pool):
            chain = [0]

            def link(ins):
                chain[0] += 1
                ins.then_inc(pool_chain, 1)
                pool.wait_ge(pool_chain, chain[0])

            link(nc.gpsimd.memset(ident[:], 0.0))
            nc.gpsimd.affine_select(out=ident[:], in_=ident[:], pattern=[[-1, P]], compare_op=ALU.not_equal, fill=1.0,
                                    base=0, channel_multiplier=1).then_inc(pool_const, 1)
            nc.gpsimd.memset(half[:], -0.5).then_inc(pool_const, 1)
            nc.gpsimd.iota(junk[:, 2 * P:3 * P].bitcast(I32), [[0, P]], base=0, channel_multiplier=1).then_inc(pool_const, 1)
            nc.gpsimd.iota(junk[:, 3 * P:4 * P].bitcast(I32), [[1, P]], base=0, channel_multiplier=0).then_inc(pool_const, 1)
            pool.wait_ge(pool_const, 4)

            def run(place):
                for step, arg in place.steps:
                    if step == "stat":
                        m = place.norm[arg]
                        pool.wait_ge(ln_veps, m + 1)
                        if not known_zero(m):
                            pool.wait_ge(ln_norm, TT * m)
                        nc.gpsimd.tensor_tensor(rstd[:], veps[:], half[:], ALU.pow).then_inc(ln_rstd, 1)
                    elif step == "q":
                        ag = place.attn * GROUPS + arg
                        b, _ = place.filled(step, arg)
                        pool.wait_ge(a_free[b], place.copied(step, arg, b) + 1)
                        nc.gpsimd.tensor_tensor(qdec.rearrange("p (c t) -> p c t", c=TT), qT[:].rearrange("p (c t) -> p c t", c=TT),
                                                lam_t[:, arg:arg + 1, :].to_broadcast([P, TT, P]), ALU.mult).then_inc(q_dec, 1)
                    elif step == "fly":
                        t, st = arg
                        src, dst = (w2n[:, t, :], w2p) if st % 2 == 0 else (w2p, w2n[:, t, :])
                        if st == 0:
                            pool.wait_ge(w2_loaded[t], 16)
                            if t:
                                pool.wait_ge(w2_but, t)
                        elif st == 1:
                            pool.wait_ge(w2_ss, 4 * (t + 1))
                        a = src.rearrange("p (a c m) -> p a c m", c=2, m=P << st)
                        b = dst.rearrange("p (a c m) -> p a c m", c=2, m=P << st)
                        nc.gpsimd.tensor_tensor(b[:, :, 0, :], a[:, :, 0, :], a[:, :, 1, :], ALU.add)
                        ins = nc.gpsimd.tensor_tensor(b[:, :, 1, :], a[:, :, 0, :], a[:, :, 1, :], ALU.subtract)
                        if st < BUTTERFLIES - 1:
                            link(ins)
                        else:
                            ins.then_inc(w2_but, 1)
                    elif step == "wtop":
                        pool.wait_ge(w2_tops, 1)
                        nc.gpsimd.partition_all_reduce(top_all[:], tops[:], P, bass.bass_isa.ReduceOp.max).then_inc(w2_all, 1)
                    elif step == "qmean":
                        pool.wait_ge(q_sum, FOURTHS)
                        nc.gpsimd.partition_all_reduce(asum_all[:], asum[:], P, bass.bass_isa.ReduceOp.add).then_inc(q_all, 1)
                    elif step == "decay":
                        pool.wait_ge(w_ss, 2 * HT)
                        pool.wait_ge(w2_ss, 4 * KT)
                        nc.gpsimd.iota(junk[:, 0:P], [[1, P]], base=0, channel_multiplier=-1,
                                       allow_small_or_imprecise_dtypes=True).then_inc(decay_numbers, 1)
                        nc.gpsimd.iota(junk[:, P:2 * P], [[1, P]], base=0, channel_multiplier=0,
                                       allow_small_or_imprecise_dtypes=True).then_inc(decay_numbers, 1)
                        nc.gpsimd.iota(tiny[:, 0:1], [[0, 1]], base=P, channel_multiplier=-1,
                                       allow_small_or_imprecise_dtypes=True).then_inc(decay_numbers, 1)
                        pool.wait_ge(decay_exp, 1)
                        nc.gpsimd.affine_select(out=mask[:], in_=mask[:], pattern=[[0, HEADS], [1, P]], compare_op=ALU.is_ge,
                                                fill=0.0, base=0, channel_multiplier=-1).then_inc(decay_exp, 1)
                    elif step == "qzero":
                        pool.wait_ge(q_tern, QKV_T + PROJ_T)
                        nc.gpsimd.memset(at["qblk"], 0.0).then_inc(qblk_zero, 1)

            program(pool, run)

        @block.scalar
        def _(act):
            act.wait_ge(pool_const, 1)
            nc.scalar.copy(ident16[:], ident[:]).then_inc(act_const, 1)
            act.wait_ge(dve_const, 1)
            squares = [(act_const, 1)]

            def sum_squares(v, out, done):
                act.wait_ge(*squares[-1])
                nc.scalar.activation(junk[:], v, ACT.Square, accum_out=out).then_inc(done, 1)
                squares.append((done, 1 + sum(1 for d, _ in squares if d is done)))

            def run(place):
                n = place.ffn
                for step, arg in place.steps:
                    if step == "wsum":
                        j = arg
                        act.wait_ge(w_loaded[j % STAGES], 32 * (j // STAGES + 1))
                        for m in range(2):
                            sum_squares(stage[:, j % STAGES, m, :], row_ss[:, j, m:m + 1], w_ss)
                    elif step == "w2sum":
                        t = arg
                        act.wait_ge(w2_loaded[t], 16)
                        for q in range(4):
                            sum_squares(w2n[:, t, D * q:D * (q + 1)], ss2[:, t, q:q + 1], w2_ss)
                    elif step == "wturn":
                        j, m = divmod(arg, 2)
                        b, fill = place.filled(step, arg)
                        act.wait_ge(a_ready[b], fill)
                        nc.scalar.copy((w1t, w3t)[m][:, 0, :, P * j:P * (j + 1)],
                                       a_bank[b][:].rearrange("p (k h) -> p k h", k=KT)).then_inc(a_free[b], 1)
                    elif step == "w2turn":
                        j = arg
                        b, fill = place.filled(step, arg)
                        act.wait_ge(a_ready[b], fill)
                        if j >= 2:
                            act.wait_ge(w2_had, j - 1)
                        else:
                            act.wait_ge((hfull_ready, lo_ready)[j], HT)
                        nc.scalar.copy(w2c[j % 2], a_bank[b][:]).then_inc(a_free[b], 1)
                    elif step == "w2had":
                        j = arg
                        act.wait_ge(w2_had, j + 1)
                        act.wait_ge(w2_f, 1)
                        nc.scalar.activation(w2t[:, 0, j, :], had_bank[j % 2][:], ACT.Copy, scale=f2[:, j:j + 1]).then_inc(w2_hi, 1)
                    elif step == "decay":
                        act.wait_ge(decay_rates, 3)
                        act.wait_ge(ln_norm, 2 * TT)
                        for h in range(HEADS):
                            ins = nc.scalar.activation(mask[:, h, :], junk[:, 0:P], ACT.Exp, scale=s_row[:, h:h + 1])
                        ins.then_inc(decay_exp, 1)
                        for g in range(GROUPS):
                            nc.scalar.activation(lam_t[:, g, :], junk[:, P:2 * P], ACT.Exp, scale=s_col[:, g:g + 1])
                        nc.scalar.activation(lam_rev[:], s_row[:], ACT.Exp, scale=tiny[:, 0:1])
                        nc.scalar.activation(lam_T[:], s_col[:], ACT.Exp, scale=float(P)).then_inc(act_const, 1)
                    elif step == "qprep":
                        act.wait_ge(q_scales, 1)
                        for r in (2 * arg, 2 * arg + 1):
                            act.wait_ge(wst_loaded[r // 4], 16)
                            part = 6 if r < QKV_T else 7
                            nc.scalar.activation(wst[:, r, :], wst[:, r, :], ACT.Copy, scale=tiny[:, part:part + 1]).then_inc(q_scaled, 1)
                    elif step == "gate":
                        j = arg
                        if place.steps is FIRST:
                            act.wait_ge(w_sc, j // 2 + 1)
                        act.wait_ge(g_ready, n * HT + (j + 1))
                        if not known_zero(n * HT + j):
                            act.wait_ge(hfull_ready, n * HT + j)
                        nc.scalar.activation(gate, g_bank[:], ACT.Silu, scale=g_scale[:, j:j + 1]).then_inc(gate_ready, 1)
                    elif step == "lin":
                        j = arg
                        act.wait_ge(hfull_ready, n * HT + (j + 1))
                        if place.steps is FIRST:
                            pass
                        elif j == 1 and not known_zero(n):
                            act.wait_ge(d_ready, n * TT)
                        elif j != 1 and not known_zero(n * (HT - 1) + max(j - 1, 0)):
                            act.wait_ge(d_step, n * (HT - 1) + max(j - 1, 0))
                        nc.scalar.copy(hidden(place, j)[:, 0, :], hfull).then_inc(hi_ready, 1)
                    elif step == "turn":
                        which, t = arg
                        b, fill = place.filled(step, arg)
                        act.wait_ge(a_ready[b], fill)
                        nc.scalar.copy(norm_target(place, which)[:, 0, :, P * t:P * (t + 1)],
                                       a_bank[b][:].rearrange("p (k t) -> p k t", k=KT)).then_inc(a_free[b], 1)
                    elif step == "qturn":
                        b, fill = place.filled(step, arg)
                        act.wait_ge(a_ready[b], fill)
                        dst, r = (wqkv, 2 * arg) if 2 * arg < QKV_T else (wproj, 2 * arg - QKV_T)
                        nc.scalar.copy(dst[:, :, P * r:P * (r + 2)].rearrange("p k (a t) -> p a k t", a=2),
                                       a_bank16[b]).then_inc(a_free[b], 1)
                    elif step == "q":
                        b, fill = place.filled(step, arg)
                        act.wait_ge(a_ready[b], fill)
                        ag = place.attn * GROUPS + arg
                        if not known_zero(ag):
                            act.wait_ge(q_spread, ag)
                            act.wait_ge(q_dec, ag)
                        nc.scalar.activation(qT[:], a_bank[b][:], ACT.Copy, scale=q_scale[:]).then_inc(a_free[b], 1)
                        act.wait_ge(a_free[b], place.copied(step, arg, b) + 1)
                        act.wait_ge(qblk_zero, 1)
                        for h in range(HG):
                            rows_h = slice(HD * h, HD * (h + 1))
                            ins = nc.scalar.copy(qblk[rows_h, :, h, :], qT[rows_h, :].rearrange("p (c t) -> p c t", c=TT))
                        ins.then_inc(q_spread, 1)
                    elif step == "k":
                        b, fill = place.filled(step, arg)
                        act.wait_ge(a_ready[b], fill)
                        nc.scalar.activation(kT, a_bank[b][:], ACT.Copy, scale=kv_scale[:]).then_inc(a_free[b], 1)
                    elif step == "vturn":
                        b, fill = place.filled(step, arg)
                        act.wait_ge(a_ready[b], fill)
                        nc.scalar.copy(at["vnat"], a_bank[b][:]).then_inc(a_free[b], 1)
                    elif step == "pv" and arg[1] == TT - 1:
                        g = arg[0]
                        b, fill = place.filled(step, arg)
                        act.wait_ge(a_ready[b], fill)
                        if g == 0 and not known_zero(place.attn) and place.x is None:
                            act.wait_ge(y_stored, 16 * place.attn)
                        nc.scalar.copy(attention_buffers(place)[0][:, :, P * g:P * (g + 1)],
                                       a_bank[b][:].rearrange("p (c e) -> p c e", c=TT)).then_inc(a_free[b], 1)

            program(act, run)

        @block.vector
        def _(dve):
            chain = [0]

            def link(ins):
                chain[0] += 1
                ins.then_inc(dve_chain, 1)
                dve.wait_ge(dve_chain, chain[0])

            def power(out, in_, flip):
                if flip:
                    return nc.vector.tensor_scalar(out.bitcast(I32), in_.bitcast(I32), EXPONENT, EXPONENT,
                                                   ALU.bitwise_and, ALU.bitwise_xor)
                return nc.vector.tensor_scalar(out.bitcast(I32), in_.bitcast(I32), EXPONENT, None, ALU.bitwise_and)

            def inverse_norm(out, ss):
                link(nc.vector.tensor_scalar(out.bitcast(I32), ss.bitcast(I32), 24, None, ALU.logical_shift_right))
                return nc.vector.tensor_scalar(out.bitcast(I32), out.bitcast(I32), -float(1 << 23), float(189 << 23),
                                               ALU.mult, ALU.add)

            dve.wait_ge(pool_const, 4)
            ip, ij = junk[:, 2 * P:3 * P].bitcast(I32), junk[:, 3 * P:4 * P].bitcast(I32)
            link(nc.vector.tensor_tensor(ip, ip, ij, ALU.bitwise_and))
            for shift in (4, 2, 1):
                link(nc.vector.tensor_scalar(ij, ip, shift, None, ALU.logical_shift_right))
                link(nc.vector.tensor_tensor(ip, ip, ij, ALU.bitwise_xor))
            link(nc.vector.tensor_scalar(ip, ip, 1, None, ALU.bitwise_and))
            nc.vector.tensor_copy(hadamard[:], ip).then_inc(dve_const, 1)
            dve.wait_ge(dve_const, 1)
            nc.vector.tensor_scalar(hadamard[:], hadamard[:], -2.0, 1.0, ALU.mult, ALU.add).then_inc(dve_const, 1)
            link(nc.vector.memset(diag[:], 0.0))
            for h in range(HG):
                nc.vector.memset(diag[HD * h:HD * (h + 1), HD * h:HD * (h + 1)], 1.0)

            def run(place):
                n, a = place.ffn, place.attn
                for step, arg in place.steps:
                    if step == "wscale":
                        js = slice(2 * arg, 2 * arg + 2)
                        dve.wait_ge(w_ss, 4 * (arg + 1))
                        scale, inverse = rows[:, 0, js, :], rows[:, 1, js, :]
                        link(inverse_norm(scale, row_ss[:, js, :]))
                        link(power(inverse, scale, True))
                        nc.vector.tensor_scalar(row_sc[:, js, :], scale, W_SCALE, None, ALU.mult)
                        nc.vector.tensor_scalar(g_scale[:, js], inverse[:, :, 0], 0.5 / (X_SCALE * W_SCALE), None, ALU.mult)
                        nc.vector.tensor_scalar(l_scale[:, js], scale[:, :, 0], HID_SCALE / (X_SCALE * W_SCALE), None,
                                                ALU.mult).then_inc(w_sc, 1)
                    elif step == "wprep":
                        j, m = divmod(arg, 2)
                        dve.wait_ge(w_sc, j // 2 + 1)
                        nc.vector.tensor_scalar(cent[:, arg % 2], stage[:, j % STAGES, m, :], row_sc[:, j, m:m + 1], None,
                                                ALU.mult).then_inc(w_norm, 1)
                    elif step == "wturn":
                        j, m = divmod(arg, 2)
                        b, fill = place.filled(step, arg)
                        dst = (w1t, w3t)[m][:, :, :, P * j:P * (j + 1)]
                        dve.wait_ge(a_ready[b], fill)
                        dve.wait_ge(a_free[b], place.copied(step, arg, b) + 1)
                        nc.vector.tensor_tensor(dst[:, 1], a_bank[b][:].rearrange("p (k h) -> p k h", k=KT), dst[:, 0],
                                                ALU.subtract).then_inc(a_free[b], 1)
                    elif step == "wtop":
                        dve.wait_ge(w_sc, HT // 2)
                        link(nc.vector.tensor_tensor(f2[:], rows[:, 1, :, 0], rows[:, 1, :, 1], ALU.mult))
                        nc.vector.tensor_reduce(tops[:, 0:1], f2[:], AX.X, ALU.max)
                        dve.wait_ge(w2_ss, 4 * KT)
                        link(nc.vector.tensor_reduce(tiny[:, 11:11 + KT], ss2[:], AX.X, ALU.add))
                        nc.vector.tensor_reduce(tops[:, 1:2], tiny[:, 11:11 + KT], AX.X, ALU.max).then_inc(w2_tops, 1)
                        dve.wait_ge(w2_all, 1)
                        link(inverse_norm(tiny[:, 5:6], top_all[:, 1:2]))
                        link(power(tiny[:, 4:5], top_all[:, 0:1], True))
                        link(nc.vector.tensor_tensor(tiny[:, 5:6], tiny[:, 5:6], tiny[:, 4:5], ALU.mult))
                        link(nc.vector.tensor_scalar(tiny[:, 5:6], tiny[:, 5:6], 2.0 * HID_SCALE / 2.0 ** 6 * W_SCALE, None, ALU.mult))
                        nc.vector.tensor_scalar(f2[:], f2[:], tiny[:, 5:6], 0.25 / HID_SCALE, ALU.mult, ALU.mult).then_inc(w2_f, 1)
                        link(nc.vector.reciprocal(ffn_unscale[:], tiny[:, 5:6]))
                        link(nc.vector.tensor_scalar(ffn_unscale[:], ffn_unscale[:], 0.5 / float(np.sqrt(H)), None, ALU.mult))
                    elif step == "w2had":
                        j = arg
                        dve.wait_ge(w2_hi, j + 1)
                        nc.vector.scalar_tensor_tensor(out=w2t[:, 1, j, :], in0=had_bank[j % 2][:], scalar=f2[:, j:j + 1],
                                                       in1=w2t[:, 0, j, :], op0=ALU.mult, op1=ALU.subtract).then_inc(w2_lo, 1)
                    elif step == "decay":
                        dve.wait_ge(rows_loaded, 16 * 4)
                        nc.vector.tensor_scalar(s_row[:], s_row[:], -1.0, None, ALU.mult).then_inc(decay_rates, 1)
                        dve.wait_ge(decay_rates, 1)
                        for h in range(HG):
                            rows_h = slice(HD * h, HD * (h + 1))
                            ins = nc.vector.tensor_copy(s_col[rows_h, :], s_row[rows_h, :].rearrange("p (g h) -> p h g", h=HG)[:, h, :])
                        ins.then_inc(decay_rates, 1)
                        dve.wait_ge(decay_numbers, 3)
                        nc.vector.tensor_scalar(junk[:, 0:P], junk[:, 0:P], 0.0, None, ALU.max).then_inc(decay_rates, 1)
                        for i, row in ((1, qnw_row), (2, pw_row)):
                            link(nc.vector.tensor_reduce(tiny[:, i:i + 1], row[:], AX.X, ALU.max, apply_absolute_value=True))
                            link(nc.vector.tensor_scalar(tiny[:, i:i + 1], tiny[:, i:i + 1], TINY, None, ALU.max))
                            link(power(tiny[:, i:i + 1], tiny[:, i:i + 1], True))
                            link(nc.vector.tensor_scalar(tiny[:, i:i + 1], tiny[:, i:i + 1], 0.25, None, ALU.mult))
                            link(nc.vector.tensor_scalar(row[:], row[:], tiny[:, i:i + 1], None, ALU.mult))
                            link(nc.vector.reciprocal(tiny[:, 8 + i:9 + i], tiny[:, i:i + 1]))
                        dve.wait_ge(q_scales, 1)
                        link(nc.vector.tensor_scalar(kv_scale[:], tiny[:, 3:4], tiny[:, 9:10], 1.0 / X_SCALE, ALU.mult, ALU.mult))
                        nc.vector.tensor_scalar(proj_scale[:], tiny[:, 4:5], tiny[:, 10:11], 1.0 / X_SCALE, ALU.mult, ALU.mult)
                        nc.vector.tensor_scalar(q_scale[:], kv_scale[:], QK_SCALE, None, ALU.mult).then_inc(q_scales, 1)
                    elif step == "qprep":
                        if arg:
                            b, fill = place.filled("qturn", arg - 1)
                            dve.wait_ge(a_ready[b], fill)
                        for r in (2 * arg, 2 * arg + 1):
                            dve.wait_ge(q_scaled, r + 1)
                            signs, negative = tern[:, r % 2, 0, :], tern[:, r % 2, 1, :]
                            link(nc.vector.tensor_scalar(negative, wst[:, r, :], -0.5, None, ALU.is_lt))
                            nc.vector.scalar_tensor_tensor(out=signs, in0=wst[:, r, :], scalar=0.5, in1=negative, op0=ALU.is_gt,
                                                           op1=ALU.subtract).then_inc(q_tern, 1)
                    elif step == "lin":
                        j = arg
                        dve.wait_ge(l_ready, n * HT + (j + 1))
                        dve.wait_ge(gate_ready, n * HT + (j + 1))
                        if not known_zero(n * HT + j):
                            dve.wait_ge(lo_ready, n * HT + j)
                        nc.vector.scalar_tensor_tensor(out=hfull, in0=l_bank[:], scalar=l_scale[:, j:j + 1], in1=gate,
                                                       op0=ALU.mult, op1=ALU.mult).then_inc(hfull_ready, 1)
                        dve.wait_ge(hi_ready, n * HT + (j + 1))
                        parts = hidden(place, j)
                        nc.vector.tensor_tensor(parts[:, 1, :], hfull, parts[:, 0, :], ALU.subtract).then_inc(lo_ready, 1)
                    elif step == "resid":
                        which, t = arg
                        src, dst = (xin, x1) if which == "ffn1" else (place.x2, place.x2)
                        dve.wait_ge(d_ready, n * TT + (t + 1))
                        if which == "ffn1" and t == 0:
                            dve.wait_ge(x_loaded, 16 * (place.loaded + 1))
                        nc.vector.scalar_tensor_tensor(out=dst[:, t, :], in0=d_bank[t][:], scalar=ffn_unscale[:],
                                                       in1=src[:, t, :], op0=ALU.mult, op1=ALU.add).then_inc(res_done, 1)
                    elif step == "stat" and arg != "o":
                        m, m_ln = place.norm[arg], place.stats[arg]
                        src = norm_source(place, arg)
                        if arg == "ffn1":
                            dve.wait_ge(x_loaded, 16 * (place.loaded + 1))
                        elif arg == "next":
                            dve.wait_ge(x_next_loaded, 16)
                        elif arg == "qkv":
                            dve.wait_ge(res_done, TT * n)
                        else:
                            for b in range(2):
                                dve.wait_ge(a_free[b], place.copied(step, arg, b))
                        for t in range(TT):
                            nc.vector.bn_stats(stat[:, t, :], src[:, t, :]).then_inc(ln_stats, 1)
                        dve.wait_ge(ln_stats, TT * (m_ln + 1))
                        even, odd = stat[:, 0:TT, 1], stat[:, 0:TT, 4]
                        nc.vector.tensor_tensor(mean[:], even, odd, ALU.add).then_inc(ln_small, 1)
                        nc.vector.tensor_tensor(ms[:, 0, 0:TT], even, odd, ALU.subtract).then_inc(ln_small, 1)
                        nc.vector.tensor_tensor(ms[:, 1, 0:TT], stat[:, 0:TT, 2], stat[:, 0:TT, 5], ALU.add).then_inc(ln_small, 1)
                        base = 5 * m_ln
                        dve.wait_ge(ln_small, base + 2)
                        nc.vector.tensor_tensor(ms[:, 0, 0:TT], ms[:, 0, 0:TT], ms[:, 0, 0:TT], ALU.mult).then_inc(ln_small, 1)
                        nc.vector.tensor_scalar(mean[:], mean[:], 0.5, None, ALU.mult)
                        dve.wait_ge(ln_small, base + 4)
                        nc.vector.scalar_tensor_tensor(out=ms[:, 0, 0:TT], in0=ms[:, 0, 0:TT], scalar=D / 4.0,
                                                       in1=ms[:, 1, 0:TT], op0=ALU.mult, op1=ALU.add).then_inc(ln_small, 1)
                        dve.wait_ge(ln_small, base + 5)
                        if not known_zero(m):
                            dve.wait_ge(ln_rstd, m)
                        mul, add = (1.0 + RMS_EPS, LN_EPS * RMS_EPS) if arg == "qkv" else (1.0, LN_EPS)
                        nc.vector.tensor_scalar(veps[:], ms[:, 0, 0:TT], mul / D / X_SCALE ** 2, add / X_SCALE ** 2,
                                                ALU.mult, ALU.add).then_inc(ln_veps, 1)
                    elif step == "ostat":
                        t = arg
                        src = attention_buffers(place)[0]
                        dve.wait_ge(a_free[1], place.copied(step, arg, 1))
                        nc.vector.bn_stats(stat[:, t, :], src[:, t, :]).then_inc(o_stats, 1)
                        nc.vector.tensor_tensor(src[:, t, :], src[:, t, :], nw_row[:], ALU.mult).then_inc(o_scaled, 1)
                        dve.wait_ge(o_scaled, TT * a + (t + 1))
                        nc.vector.bn_stats(stat[:, TT + t, :], src[:, t, :]).then_inc(o_stats, 1)
                    elif step == "stat":
                        m = place.norm[arg]
                        dve.wait_ge(o_stats, 2 * TT * (a + 1))
                        even, odd = stat[:, :, 1], stat[:, :, 4]
                        base = 6 * a
                        nc.vector.tensor_tensor(ms[:, 0, :], even, even, ALU.mult).then_inc(o_small, 1)
                        nc.vector.tensor_tensor(ms[:, 1, :], odd, odd, ALU.mult).then_inc(o_small, 1)
                        nc.vector.tensor_tensor(ms[:, 2, :], stat[:, :, 2], stat[:, :, 5], ALU.add).then_inc(o_small, 1)
                        dve.wait_ge(o_small, base + 2)
                        nc.vector.tensor_tensor(ms[:, 0, :], ms[:, 0, :], ms[:, 1, :], ALU.add).then_inc(o_small, 1)
                        dve.wait_ge(o_small, base + 4)
                        nc.vector.scalar_tensor_tensor(out=ms[:, 1, :], in0=ms[:, 0, :], scalar=D / 2.0,
                                                       in1=ms[:, 2, :], op0=ALU.mult, op1=ALU.add).then_inc(o_small, 1)
                        dve.wait_ge(o_small, base + 5)
                        nc.vector.scalar_tensor_tensor(out=ms[:, 0, 0:TT], in0=ms[:, 1, 0:TT], scalar=RMS_EPS,
                                                       in1=ms[:, 1, TT:2 * TT], op0=ALU.mult, op1=ALU.add).then_inc(o_small, 1)
                        dve.wait_ge(o_small, base + 6)
                        dve.wait_ge(ln_rstd, m)
                        nc.vector.tensor_scalar(veps[:], ms[:, 0, 0:TT], D * RMS_EPS * OUT_NORM_EPS, 1.0 / D / X_SCALE ** 2,
                                                ALU.add, ALU.mult).then_inc(ln_veps, 1)
                    elif step == "prep":
                        which, t = arg
                        m = place.norm[which]
                        src = norm_source(place, which)[:, t, :]
                        dve.wait_ge(ln_rstd, m + 1)
                        if place.steps is NORM:
                            for b in range(2):
                                dve.wait_ge(a_free[b], place.copied(step, arg, b))
                        if which == "qkv":
                            nc.vector.scalar_tensor_tensor(out=cent[:, t % 2], in0=src, scalar=mean[:, t:t + 1], in1=qnw_row[:],
                                                           op0=ALU.subtract, op1=ALU.mult).then_inc(ln_cent, 1)
                            dve.wait_ge(ln_cent, TT * a + (t + 1))
                            ins = nc.vector.tensor_scalar(cent[:, t % 2], cent[:, t % 2], rstd[:, t:t + 1], None, ALU.mult)
                        elif which == "o":
                            ins = nc.vector.scalar_tensor_tensor(out=cent[:, t % 2], in0=src, scalar=rstd[:, t:t + 1],
                                                                 in1=pw_row[:], op0=ALU.mult, op1=ALU.mult)
                        else:
                            ins = nc.vector.tensor_scalar(cent[:, t % 2], src, mean[:, t:t + 1], rstd[:, t:t + 1],
                                                          ALU.subtract, ALU.mult)
                        ins.then_inc(ln_norm, 1)
                    elif step == "turn":
                        which, t = arg
                        b, fill = place.filled(step, arg)
                        dst = norm_target(place, which)[:, :, :, P * t:P * (t + 1)]
                        dve.wait_ge(a_ready[b], fill)
                        dve.wait_ge(a_free[b], place.copied(step, arg, b) + 1)
                        nc.vector.tensor_tensor(dst[:, 1], a_bank[b][:].rearrange("p (k t) -> p k t", k=KT), dst[:, 0],
                                                ALU.subtract).then_inc(a_free[b], 1)
                    elif step == "qsum":
                        dve.wait_ge(qst_loaded, 16 * (arg + 1))
                        nc.vector.tensor_reduce(asum[:, 4 * arg:4 * arg + 4], qst, AX.X, ALU.add,
                                                apply_absolute_value=True).then_inc(q_sum, 1)
                    elif step == "qmean":
                        dve.wait_ge(q_all, 1)
                        nc.vector.tensor_reduce(tiny[:, 3:4], asum_all[:, 0:QKV_T], AX.X, ALU.add)
                        link(nc.vector.tensor_reduce(tiny[:, 4:5], asum_all[:, QKV_T:QKV_T + PROJ_T], AX.X, ALU.add))
                        nc.vector.tensor_scalar(tiny[:, 3:4], tiny[:, 3:4], 1.0 / (3 * D * D), 1e-5, ALU.mult, ALU.max)
                        link(nc.vector.tensor_scalar(tiny[:, 4:5], tiny[:, 4:5], 1.0 / (D * D), 1e-5, ALU.mult, ALU.max))
                        nc.vector.reciprocal(tiny[:, 6:8], tiny[:, 3:5]).then_inc(q_scales, 1)
                    elif step == "v":
                        b, fill = place.filled(step, arg)
                        dve.wait_ge(a_ready[b], fill)
                        nc.vector.tensor_scalar(vT, a_bank[b][:], kv_scale[:], None, ALU.mult).then_inc(a_free[b], 1)
                    elif step == "kturn":
                        g = arg
                        b, fill = place.filled(step, arg)
                        dve.wait_ge(a_ready[b], fill)
                        n_c = TT - 1
                        dec = lam_rev[:, HG * g:HG * (g + 1)]
                        for c in range(n_c):
                            ins = nc.vector.tensor_tensor(
                                kdec[:, c, :].rearrange("p (h d) -> p h d", h=HG),
                                a_bank[b][:, P * c:P * (c + 1)].rearrange("p (h d) -> p h d", h=HG),
                                dec.rearrange("p (h a) -> p h a", a=1).to_broadcast([P, HG, HD]), ALU.mult)
                        ins.then_inc(a_free[b], 1)
                    elif step == "score":
                        g, c = arg
                        b, fill = place.filled(step, arg)
                        dve.wait_ge(a_ready[b], fill)
                        nc.vector.tensor_tensor(sc[:, c % 2], a_bank[b][:].rearrange("p (h t) -> p h t", h=HG),
                                                mask[:, HG * g:HG * (g + 1), :], ALU.mult).then_inc(a_free[b], 1)
                    elif step == "kv":
                        g = arg
                        b, fill = place.filled(step, arg)
                        dve.wait_ge(a_ready[b], fill)
                        for c in range(TT - 1):
                            ins = nc.vector.tensor_tensor(state[:, c, :], a_bank[b][:, P * c:P * (c + 1)], diag[:], ALU.mult)
                            if c < TT - 2:
                                ins.then_inc(state_part, 1)
                            else:
                                ins.then_inc(a_free[b], 1)
                        ag = a * GROUPS + g
                        for c in range(1, TT - 1):
                            dve.wait_ge(state_part, (TT - 2) * (ag + 1))
                            if c == TT - 2:
                                dve.wait_ge(a_free[b], place.copied(step, arg, b) + 1)
                                dve.wait_ge(state_done, (TT - 2) * ag + (c - 1))
                            nc.vector.scalar_tensor_tensor(out=state[:, c, :], in0=state[:, c - 1, :], scalar=lam_T[:, g:g + 1],
                                                           in1=state[:, c, :], op0=ALU.mult, op1=ALU.add).then_inc(state_done, 1)
                    elif step == "proj":
                        t = arg
                        b, fill = place.filled(step, arg)
                        dve.wait_ge(a_ready[b], fill)
                        nc.vector.scalar_tensor_tensor(out=attention_buffers(place)[0][:, t, :], in0=a_bank[b][:],
                                                       scalar=proj_scale[:], in1=x1[:, t, :], op0=ALU.mult,
                                                       op1=ALU.add).then_inc(a_free[b], 1)

            program(dve, run)

        @block.tensor
        def _(pe):
            pe.wait_ge(pool_const, 1)
            pe.wait_ge(act_const, 1)

            def take(place, step, arg):
                b, _ = place.uses[step, arg]
                free = place.copied(step, arg, b)
                if not known_zero(free):
                    pe.wait_ge(a_free[b], free)
                return b

            def landed(place, step, arg, b):
                free = place.copied(step, arg, b)
                if not known_zero(free):
                    pe.wait_ge(a_free[b], free)

            def run(place):
                n = place.ffn
                for step, arg in place.steps:
                    if step == "wturn":
                        b = take(place, step, arg)
                        pe.wait_ge(w_norm, arg + 1)
                        for k in range(KT):
                            ins = nc.tensor.transpose(a_bank[b][:, P * k:P * (k + 1)], cent[:, arg % 2, P * k:P * (k + 1)], ident[:])
                        ins.then_inc(a_ready[b], 1)
                    elif step == "w2turn":
                        j = arg
                        b = take(place, step, arg)
                        pe.wait_ge(w2_but, KT)
                        for t in range(KT):
                            ins = nc.tensor.transpose(a_bank[b][:, P * t:P * (t + 1)], w2n[:, t, P * j:P * (j + 1)], ident[:])
                        ins.then_inc(a_ready[b], 1)
                    elif step == "w2had":
                        j = arg
                        b, _ = place.uses["w2turn", j]
                        pe.wait_ge(a_free[b], place.copied("w2turn", j, b) + 1)
                        pe.wait_ge(dve_const, 2)
                        if j >= 2:
                            pe.wait_ge(w2_lo, j - 1)
                        else:
                            pe.wait_ge((gate_ready, hfull_ready)[j], HT)
                        nc.tensor.matmul(had_bank[j % 2][:], hadamard[:], w2c[j % 2], start=True, stop=True).then_inc(w2_had, 1)
                    elif step in ("gate", "lin"):
                        j = arg
                        src = xt if place.which == "ffn1" else place.y
                        wt, dst, done = (w1t, g_bank, g_ready) if step == "gate" else (w3t, l_bank, l_ready)
                        if step == "gate" and j == 0:
                            for b in range(2):
                                landed(place, step, arg, b)
                        if place.steps is FIRST:
                            tile = 2 * j + (step == "lin")
                            pe.wait_ge(a_free[tile % 2], place.copied("wturn", tile, tile % 2) + 2)
                        if not known_zero(n * HT + j):
                            pe.wait_ge(gate_ready if step == "gate" else hfull_ready, n * HT + j)
                        for k in range(KT):
                            for wp, xp in ((0, 0), (0, 1), (1, 0)):
                                ins = nc.tensor.matmul(dst[:], wt[:, wp, k, P * j:P * (j + 1)], src[:, xp, k, :],
                                                       start=(k == 0 and wp == xp), stop=(k == KT - 1 and wp == 1))
                        ins.then_inc(done, 1)
                    elif step == "down":
                        j = arg
                        parts = hidden(place, j)
                        pe.wait_ge(lo_ready, n * HT + (j + 1))
                        if place.steps is FIRST:
                            pe.wait_ge(w2_lo, j + 1)
                        if j == 0 and not known_zero(n):
                            pe.wait_ge(res_done, n * TT)
                        for t in range(TT):
                            for hp, wp in ((0, 0), (0, 1), (1, 0)):
                                ins = nc.tensor.matmul(d_bank[t][:], parts[:, hp, P * t:P * (t + 1)], w2t[:, wp, j, :],
                                                       start=(j == 0 and hp == wp), stop=(j == HT - 1 and hp == 1))
                            if j == HT - 1:
                                ins.then_inc(d_ready, 1)
                        if j < HT - 1:
                            ins.then_inc(d_step, 1)
                    elif step == "turn":
                        which, t = arg
                        m = place.norm[which]
                        b = take(place, step, arg)
                        pe.wait_ge(ln_norm, TT * m + (t + 1))
                        for k in range(KT):
                            ins = nc.tensor.transpose(a_bank[b][:, P * k:P * (k + 1)], cent[:, t % 2, P * k:P * (k + 1)], ident[:])
                        ins.then_inc(a_ready[b], 1)
                    elif step == "qturn":
                        b = take(place, step, arg)
                        pe.wait_ge(q_tern, 2 * (arg + 1))
                        for r in range(2):
                            for k in range(KT):
                                ins = nc.tensor.transpose(a_bank16[b][:, r, k, :], tern[:, r, 0, P * k:P * (k + 1)], ident16[:])
                        ins.then_inc(a_ready[b], 1)
                    elif step in ("q", "k", "v"):
                        g = arg
                        b = take(place, step, arg)
                        if g == 0:
                            for other in range(2):
                                landed(place, step, arg, other)
                        src = attention_buffers(place)[1]
                        col = "qkv".index(step) * D + P * g
                        for k in range(KT):
                            for part in range(2):
                                ins = nc.tensor.matmul(a_bank[b][:], wqkv[:, k, col:col + P], src[:, part, k, :],
                                                       start=(k == 0 and part == 0), stop=(k == KT - 1 and part == 1))
                        ins.then_inc(a_ready[b], 1)
                    elif step in ("vturn", "kturn"):
                        b = take(place, step, arg)
                        src, n_c = (vT, TT) if step == "vturn" else (kT, TT - 1)
                        for c in range(n_c):
                            ins = nc.tensor.transpose(a_bank[b][:, P * c:P * (c + 1)], src[:, P * c:P * (c + 1)], ident[:])
                        ins.then_inc(a_ready[b], 1)
                    elif step == "score":
                        g, c = arg
                        b = take(place, step, arg)
                        if c == 0:
                            pe.wait_ge(q_spread, place.attn * GROUPS + (g + 1))
                            landed(place, step, arg, 1)
                        nc.tensor.matmul(a_bank[b][:], kT[:, P * c:P * (c + 1)], qblk[:, c].rearrange("p h t -> p (h t)"),
                                         start=True, stop=True).then_inc(a_ready[b], 1)
                    elif step == "kv":
                        g = arg
                        b = take(place, step, arg)
                        pe.wait_ge(a_free[0], place.copied("score", (g, 0), 0))
                        for c in range(TT - 1):
                            ins = nc.tensor.matmul(a_bank[b][:, P * c:P * (c + 1)], kdec[:, c, :], vnat[:, c, :],
                                                   start=True, stop=True)
                        ins.then_inc(a_ready[b], 1)
                    elif step == "pv":
                        g, c = arg
                        b = place.uses[step, arg][0]
                        if c == 0:
                            take(place, step, arg)
                        pe.wait_ge(a_free[0], place.copied("score", arg, 0) + 1)
                        if c:
                            if c == 1:
                                pe.wait_ge(q_dec, place.attn * GROUPS + (g + 1))
                            if c >= 2:
                                pe.wait_ge(state_done, (TT - 2) * (place.attn * GROUPS + g) + (c - 1))
                            nc.tensor.matmul(a_bank[b][:, P * c:P * (c + 1)], qdec[:, P * c:P * (c + 1)], state[:, c - 1, :],
                                             start=False, stop=False, skip_group_check=True)
                        for h in range(HG):
                            col = P * c + HD * h
                            ins = nc.tensor.matmul(a_bank[b][:, col:col + HD], sc[:, c % 2, h, :], vnat[:, c, HD * h:HD * (h + 1)],
                                                   start=(c == 0 and h == 0), stop=True, skip_group_check=True)
                        if c == TT - 1:
                            ins.then_inc(a_ready[b], 1)
                    elif step == "proj":
                        t = arg
                        b = take(place, step, arg)
                        if t == 0:
                            for other in range(2):
                                landed(place, step, arg, other)
                        src = attention_buffers(place)[1]
                        for k in range(KT):
                            for part in range(2):
                                ins = nc.tensor.matmul(a_bank[b][:], src[:, part, k, P * t:P * (t + 1)], wproj[:, k, :],
                                                       start=(k == 0 and part == 0), stop=(k == KT - 1 and part == 1))
                        ins.then_inc(a_ready[b], 1)

            program(pe, run)


_INS = ["L0_attn_x", "L0_attn_qkv_w", "L0_attn_qkv_norm_w", "L0_attn_proj_w", "L0_attn_proj_norm_w", "L0_attn_norm_w",
        "L0_attn_s", "L0_ffn_W1", "L0_ffn_W2", "L0_ffn_W3"]


def kernel(**inputs):
    import numpy as _np
    import concourse.bacc as _bacc
    from concourse import mybir as _mybir
    from concourse.bass_utils import run_bass_kernel_spmd as _run

    nc = _bacc.Bacc("TRN2", target_bir_lowering=False, num_devices=1)
    arrays, args = {}, []
    for name in _INS:
        a = _np.ascontiguousarray(inputs[name])
        arrays[f"in_{name}_dram"] = a
        args.append(nc.dram_tensor(f"in_{name}_dram", a.shape, _mybir.dt.from_np(a.dtype), kind="ExternalInput").ap())
    args.append(nc.dram_tensor("out_0_dram", inputs["L0_attn_x"].shape, _mybir.dt.float32, kind="ExternalOutput").ap())
    macaron_kernel(nc, *args)
    return _run(nc, [arrays], core_ids=[0]).results[0]["out_0_dram"]
```

```python
from contextlib import ExitStack

import numpy as np

import concourse.bass as bass
from concourse import mybir

ALU = mybir.AluOpType
ACT = mybir.ActivationFunctionType
AX = mybir.AxisListType
F32 = mybir.dt.float32
F16 = mybir.dt.float16
I32 = mybir.dt.int32

P = 128
EXPONENT = 0x7F800000
LN_EPS = 1e-5
RMS_EPS = float(np.finfo(np.float32).eps)
OUT_NORM_EPS = 1e-6
TINY = 1e-30
X_SCALE = 2.0 ** 11
W_SCALE = 2.0 ** 15
QKV_SCALE = 2.0 ** 6
SCORE_SCALE = 2.0 ** -20


def macaron_kernel(nc, x, qkv_w, qkv_norm_w, proj_w, proj_norm_w, norm_w, s, w1, w2, w3, out):
    B, T, D = x.shape
    H = w1.shape[0]
    HEADS = s.shape[0]
    HD = D // HEADS
    TT = T // P
    KT = D // P
    HT = H // P
    HG = P // HD
    GROUPS = HEADS // HG
    QKV_T = 3 * D // P
    PROJ_T = D // P
    QK_SCALE = float(HD) ** -0.5
    STAGES = 4
    FOURTHS = 4
    BUTTERFLIES = HT.bit_length() - 1
    assert (D, T, HG, QKV_T, PROJ_T, HT) == (512, 512, 4, 12, 4, 16)

    HID_SCALE = W_SCALE / D

    ctx = ExitStack()
    with ctx:
        def sb(name, shape, dt=F32):
            return ctx.enter_context(nc.sbuf_tensor(name, shape, dt))

        def sem(name):
            return ctx.enter_context(nc.semaphore(name))

        w1t = sb("w1t", [P, 2, KT, H], F16)
        w3t = sb("w3t", [P, 2, KT, H], F16)
        w2t = sb("w2t", [P, 2, HT, D], F16)
        wqkv = sb("wqkv", [P, KT, 3 * D], F16)
        wproj = sb("wproj", [P, KT, D], F16)
        mask = sb("mask", [P, HEADS, P])
        xin = sb("xin", [P, TT, D])
        xt = sb("xt", [P, 2, KT, T], F16)
        cent = sb("cent", [P, 3, D])
        tern = cent[:, 0:2].bitcast(F16).rearrange("p b (a d) -> p b a d", a=2)
        qT = sb("qT", [P, T])
        junk = qT
        sizes = dict(x1=TT * D, hid=2 * D, gate=D, hfull=D, x2=TT * D, yt=KT * T, qs=HG * T // 2, ks=HG * T // 2, qdec=T,
                     kdec=(TT - 1) * P, flow=T, sc=2 * HG * P, state=(TT - 1) * P)
        early_use = sizes["x1"] + sizes["hid"] + sizes["gate"] + sizes["hfull"] + KT * H + 2 * T
        work = sb("work", [P, max(sum(sizes.values()), early_use)])
        at, start = {}, 0
        for name, n in sizes.items():
            at[name] = work[:, start:start + n]
            start += n
        x1 = at["x1"].rearrange("p (t d) -> p t d", t=TT)
        x2 = at["x2"].rearrange("p (t d) -> p t d", t=TT)
        yt = at["yt"].bitcast(F16).rearrange("p (a k t) -> p a k t", a=2, k=KT)
        hid = at["hid"].bitcast(F16).rearrange("p (b a t) -> p b a t", b=2, a=2)
        gate, hfull, qdec, flow = at["gate"], at["hfull"], at["qdec"], at["flow"]
        BLOCKS = 3
        qs = at["qs"].bitcast(F16).rearrange("p (h t) -> p h t", h=HG)
        ks = at["ks"].bitcast(F16).rearrange("p (h t) -> p h t", h=HG)
        kdec = at["kdec"].bitcast(F16).rearrange("p (a e) -> p a e", a=2)
        sc = at["sc"].bitcast(F16).rearrange("p (b a h t) -> p b a h t", b=2, a=2, h=HG)

        q_parts = sc[:, 0].rearrange("p a h t -> p a (h t)")
        k_parts = sc[:, 1].rearrange("p a h t -> p a (h t)")

        def values(buffer):
            return buffer.rearrange("p t d -> p (t d)").bitcast(F16).rearrange("p (t g a e) -> p t g a e", t=TT, g=GROUPS, a=2)

        state = at["state"].rearrange("p (c e) -> p c e", c=TT - 1)
        first = sizes["x1"] + sizes["hid"] + sizes["gate"] + sizes["hfull"]
        w2n = work[:, first:first + KT * H].rearrange("p (t h) -> p t h", t=KT)
        wst = work[:, first:first + 16 * D].rearrange("p (r d) -> p r d", r=16)
        w2c = [gate, hfull]
        early = w2t[:].rearrange("p a j d -> p (a j d)").bitcast(F32)
        n_stage = STAGES * 2 * D
        stage = early[:, 0:n_stage].rearrange("p (b m d) -> p b m d", b=STAGES, m=2)
        w2p = early[:, n_stage:n_stage + H]
        qst = early[:, n_stage + H:n_stage + H + 4 * D].rearrange("p (r d) -> p r d", r=4)
        x_next = mask[:].rearrange("p h t -> p (h t)").rearrange("p (t d) -> p t d", t=TT)
        w_parts = [hid[:, 0], hid[:, 1]] + [cent[:, b].bitcast(F16).rearrange("p (a d) -> p a d", a=2) for b in (1, 2)]
        keep = ([wqkv[:].rearrange("p k d -> p (k d)")[:, 2 * T * i:2 * T * (i + 1)] for i in range(6)]
                + [wproj[:].rearrange("p k d -> p (k d)")[:, 2 * T * i:2 * T * (i + 1)] for i in range(2)]
                + [at["x1"].bitcast(F16)[:, 2 * T * i:2 * T * (i + 1)] for i in range(4)]
                + [work[:, first + KT * H + T * i:first + KT * H + T * (i + 1)].bitcast(F16) for i in range(2)])
        first_hid = [v.rearrange("p (a t) -> p a t", a=2) for v in keep] + [hid[:, 0], hid[:, 1]]
        ident = sb("ident", [P, P])
        ident16 = sb("ident16", [P, P], F16)
        hadamard = sb("hadamard", [P, P])
        lam_t = sb("lam_t", [P, GROUPS, P])
        lam_rev = sb("lam_rev", [P, HEADS])
        lam_T = sb("lam_T", [P, GROUPS])
        diag = sb("diag", [P, P])
        qnw_row = sb("qnw_row", [P, D])
        nw_row = sb("nw_row", [P, D])
        pw_row = sb("pw_row", [P, D])
        s_row = sb("s_row", [P, HEADS])
        s_col = sb("s_col", [P, GROUPS])
        rows = sb("rows", [P, 2, HT, 2])
        row_ss = sb("row_ss", [P, HT, 2])
        row_sc = sb("row_sc", [P, HT, 2])
        g_scale = sb("g_scale", [P, HT])
        l_scale = sb("l_scale", [P, HT])
        f2 = sb("f2", [P, HT])
        ss2 = sb("ss2", [P, KT, 4])
        tops = sb("tops", [P, 2])
        top_all = sb("top_all", [P, 2])
        half = sb("half", [P, 4])
        asum = sb("asum", [P, 16])
        asum_all = sb("asum_all", [P, 16])
        tiny = sb("tiny", [P, 16])
        ffn_unscale = sb("ffn_unscale", [P, 1])
        o_scale = sb("o_scale", [P, 1])
        proj_scale = sb("proj_scale", [P, 1])
        stat = sb("stat", [P, 2 * TT, 6])
        mean = sb("mean", [P, TT])
        ms = sb("ms", [P, 3, 2 * TT])
        veps = sb("veps", [P, TT])
        decay_bound = sb("decay_bound", [P, 1])
        rstd = sb("rstd", [P, TT])

        def bank(name):
            return ctx.enter_context(nc.psum_tensor(name, [P, 512], F32))

        g_bank, l_bank = bank("g_bank"), bank("l_bank")
        d_bank = [bank(f"d_bank{t}") for t in range(TT)]
        a_bank = [bank("a_bank0"), bank("a_bank1")]
        had_bank = [g_bank, l_bank]
        a_bank16 = [b[:].bitcast(F16).rearrange("p (a k t) -> p a k t", a=2, k=KT) for b in a_bank]

        x_loaded, y_stored = sem("x_loaded"), sem("y_stored")
        g_ready, l_ready, d_ready = sem("g_ready"), sem("l_ready"), sem("d_ready")
        d_step = sem("d_step")
        gate_ready, hfull_ready = sem("gate_ready"), sem("hfull_ready")
        hi_ready, lo_ready = sem("hi_ready"), sem("lo_ready")
        res_done = sem("res_done")
        a_ready = [sem("a_ready0"), sem("a_ready1")]
        a_free = [sem("a_free0"), sem("a_free1")]
        ln_stats, ln_small, ln_veps, ln_rstd = sem("ln_stats"), sem("ln_small"), sem("ln_veps"), sem("ln_rstd")
        ln_cent, ln_norm = sem("ln_cent"), sem("ln_norm")
        q_hi, q_lo, q_dec = sem("q_hi"), sem("q_lo"), sem("q_dec")
        q_moved, k_moved = sem("q_moved"), sem("k_moved")
        k_hi, k_lo, kd_hi, kd_lo = sem("k_hi"), sem("k_lo"), sem("kd_hi"), sem("kd_lo")
        sc_hi, sc_lo = sem("sc_hi"), sem("sc_lo")
        o_stats, o_scaled, o_small = sem("o_stats"), sem("o_scaled"), sem("o_small")
        state_done = sem("state_done")
        rows_loaded, x_next_loaded = sem("rows_loaded"), sem("x_next_loaded")
        w_loaded = [sem(f"w_loaded{b}") for b in range(STAGES)]
        w2_loaded = [sem(f"w2_loaded{t}") for t in range(KT)]
        qst_loaded = sem("qst_loaded")
        wst_loaded = [sem(f"wst_loaded{q}") for q in range(FOURTHS)]
        pool_const, dve_const, act_const = sem("pool_const"), sem("dve_const"), sem("act_const")
        pool_chain, dve_chain = sem("pool_chain"), sem("dve_chain")
        w_ss, w_sc = sem("w_ss"), sem("w_sc")
        w_hi, w_lo = sem("w_hi"), sem("w_lo")
        w_turned = [sem(f"w_turned{b}") for b in range(4)]
        w2_ss, w2_but, w2_tops, w2_all, w2_f = sem("w2_ss"), sem("w2_but"), sem("w2_tops"), sem("w2_all"), sem("w2_f")
        w2_had, w2_hi, w2_lo = sem("w2_had"), sem("w2_hi"), sem("w2_lo")
        q_sum, q_all, q_scales, q_scaled, q_tern = (sem("q_sum"), sem("q_all"), sem("q_scales"), sem("q_scaled"),
                                                    sem("q_tern"))
        decay_numbers, decay_rates, decay_exp = sem("decay_numbers"), sem("decay_rates"), sem("decay_exp")
        decay_top, decay_fit = sem("decay_top"), sem("decay_fit")

        def feed_forward(which, slots):
            steps = []
            for j in range(HT):
                steps += [("gate", j)] + slots.get(3 * j, []) + [("lin", j)] + slots.get(3 * j + 1, [])
                if j:
                    steps += [("down", j - 1)]
                steps += [("low", j)] + slots.get(3 * j + 2, [])
            return steps + [("down", HT - 1)] + slots.get(3 * HT, []) + [("resid", (which, t)) for t in range(TT)]

        def norm_steps(which):
            pre = [("stat", which)] + [("prep", (which, t)) for t in range(3)]
            tr0 = [("turn", (which, 0)), ("prep", (which, 3)), ("turn", (which, 1))]
            tr1 = [("turn", (which, 2)), ("turn", (which, 3))]
            return pre, tr0, tr1

        def add(slots, at, steps):
            slots.setdefault(at, []).extend(steps)

        def attention_slots(at):
            slots = {}
            pre, tr0, tr1 = norm_steps("qkv")
            add(slots, at, tr0)
            add(slots, at + 1, tr1)
            for t in range(TT):
                add(slots, at + 3 + t // 2, [("v", t)])
            at += 7
            for g in range(GROUPS):
                b = at + (3 + TT) * g
                add(slots, b - 3, [("q", g)])
                add(slots, b - 2, [("qlow", g), ("k", g)])
                add(slots, b - 1, [("klow", g), ("kturn", g)])
                add(slots, b, [("score", (g, 0))])
                add(slots, b + 1, [("kv", g), ("score", (g, 1)), ("state", g)])
                for c in range(TT):
                    add(slots, b + 2 + c, [("pv", (g, c))] + ([("score", (g, c + 2))] if c < TT - 2 else []))
            at += (3 + TT) * (GROUPS - 1) + 1 + TT
            pre, tr0, tr1 = norm_steps("o")
            add(slots, at + 1, [("ostat", 0), ("ostat", 1)])
            add(slots, at + 3, [("ostat", 2), ("ostat", 3)])
            add(slots, at + 5, pre)
            add(slots, at + 7, tr0)
            add(slots, at + 8, tr1)
            add(slots, at + 9, [("proj", 0), ("proj", 1)])
            add(slots, at + 10, [("proj", 2), ("proj", 3)])
            pre, tr0, tr1 = norm_steps("ffn2")
            add(slots, at + 11, pre)
            add(slots, at + 13, tr0)
            add(slots, at + 14, tr1)
            assert at + 14 <= 3 * HT
            return slots

        def second_slots():
            slots = {}
            pre, tr0, tr1 = norm_steps("ffn1")
            add(slots, 10, pre)
            add(slots, 14, tr0)
            add(slots, 15, tr1)
            pre = norm_steps("qkv")[0]
            add(slots, 35, pre[:1])
            add(slots, 38, pre[1:2])
            add(slots, 41, pre[2:3])
            add(slots, 44, pre[3:])
            return slots

        def last_attention_slots():
            slots = attention_slots(1)
            return {**slots, 0: norm_steps("qkv")[0]}

        SCALED = [slice(0, 1), slice(1, 2)] + [slice(j, j + 2) for j in range(2, HT, 2)]

        def scaled(j):
            return 1 + next(n for n, js in enumerate(SCALED) if j < js.stop)

        W2_SUMS, Q_SUMS = (0, 1, 3, 4, 6, 7, 9, 10), (4, 8, 11, 14)

        def first_steps():
            pre, tr0, tr1 = norm_steps("ffn1")
            steps = [("wsum", 0), ("wscale", 0), pre[0], ("wprep", 0), ("wprep", 1)]
            steps += pre[1:] + [("wsum", 1)] + tr0 + tr1 + [("wscale", 1), ("wprep", 2), ("wprep", 3)]
            steps += [("wsum", 2), ("wsum", 3), ("wscale", 2)]
            flies = [(t, st) for t in range(KT) for st in range(BUTTERFLIES)]
            n_pre, n_tr0, n_tr1 = norm_steps("next")
            for j in range(HT):
                steps += [("gate", j)]
                if j < HT - 2:
                    steps += [("wprep", 2 * j + 4)]
                if j < HT - 4:
                    steps += [("wsum", j + 4)]
                steps += [("lin", j)]
                if j < HT - 2:
                    steps += [("wprep", 2 * j + 5)]
                if j < HT - 4 and j % 2:
                    steps += [("wscale", (j + 5) // 2)]
                if j in W2_SUMS:
                    steps += [("w2sum", W2_SUMS.index(j))]
                steps += [("fly", f) for f in flies[2 * j:2 * j + 2]]
                if j in Q_SUMS:
                    steps += [("qsum", Q_SUMS.index(j))]
                if j == HT - 3:
                    steps += [("wtop", 0)]
                if j == HT - 1:
                    steps += [("wfit", 0), ("qmean", 0)]
                steps += [("low", j)]
            for j in range(HT + 1):
                if j < HT:
                    steps += [("w2turn", j)]
                if j:
                    steps += [("w2had", j - 1)]
            slots = {0: n_pre, 2: n_tr0, 3: n_tr1, 4: [("decay", 0)], 5: [("qscale", 0)],
                     6: [("qprep", 0), ("qscale", 1)]}
            for r in range(8):
                slots[7 + r] = [("qturn", r)]
                if r < 6:
                    slots[7 + r] = [("qscale", r + 2)] + slots[7 + r]
                if r < 7:
                    slots[7 + r] += [("qprep", r + 1)]
            add(slots, 10, [("fit", 0)])
            for j in range(HT):
                steps += [("down", j)] + slots.get(j, [])
            return steps + [("resid", ("ffn1", t)) for t in range(TT)]

        FIRST = first_steps()
        WITH_ATTENTION = feed_forward("ffn1", attention_slots(0))
        SECOND = feed_forward("ffn2", second_slots())
        SECOND_WITH_ATTENTION = feed_forward("ffn2", last_attention_slots())
        LAST = feed_forward("ffn2", {})
        NORM = norm_steps("qkv")[0]

        def bank_use(step, arg):
            if step == "turn":
                return arg[1] % 2, 2
            if step == "v":
                return arg % 2, 2
            if step == "proj":
                return arg % 2, 1
            if step in ("w2turn", "qturn"):
                return arg % 2, 1
            if step == "pv":
                return (1, 1) if arg[1] == 0 else None
            return {"q": (0, 1), "k": (0, 1), "score": (0, 1), "kturn": (1, 1), "kv": (1, 1)}.get(step)

        def count_uses(steps):
            fills, copies, uses, before = [0, 0], [0, 0], {}, {}
            for step, arg in steps:
                before[step, arg] = tuple(copies)
                use = bank_use(step, arg)
                if use:
                    uses[step, arg] = (use[0], fills[use[0]])
                    fills[use[0]] += 1
                    copies[use[0]] += use[1]
                elif step == "pv":
                    uses[step, arg] = uses["pv", (arg[0], 0)]
            return uses, before, tuple(fills), tuple(copies)

        USES = {id(x): count_uses(x) for x in (FIRST, WITH_ATTENTION, SECOND, SECOND_WITH_ATTENTION, LAST, NORM)}

        class Place:

            def __init__(self, steps, fills, copies, ffn=0, attn=0, norm=None, stats=None, block=0, loaded=0, x2=x2, y=yt, x=None):
                self.steps, self.ffn, self.attn, self.norm, self.stats = steps, ffn, attn, norm or {}, stats or {}
                self.uses, self.before, self.all_fills, self.all_copies = USES[id(steps)]
                self.fills, self.copies, self.x2, self.y = fills, copies, x2, y
                self.x, self.block, self.loaded = x, block, loaded
                self.which = "ffn1" if steps is FIRST or steps is WITH_ATTENTION else "ffn2"

            def filled(self, step, arg):
                b, n = self.uses[step, arg]
                return b, self.fills[b] + (n + 1)

            def copied(self, step, arg, b):
                return self.copies[b] + self.before[step, arg][b]

            def after(self):
                return ([a + n for a, n in zip(self.fills, self.all_fills)],
                        [a + n for a, n in zip(self.copies, self.all_copies)])

        def known_zero(v):
            return isinstance(v, int) and v <= 0

        def program(eng, run):
            place = Place(FIRST, [0, 0], [0, 0], norm={"ffn1": 0, "next": 1}, stats={"ffn1": 0, "next": 1})
            run(place)
            place = Place(NORM, *place.after(), ffn=1, norm={"qkv": 2}, stats={"qkv": 2})
            run(place)
            fills, copies = place.after()
            in_a, in_b = USES[id(WITH_ATTENTION)], USES[id(SECOND)]
            per_fill = [in_a[2][b] + in_b[2][b] for b in range(2)]
            per_copy = [in_a[3][b] + in_b[3][b] for b in range(2)]

            def first_of(i):
                before = i - 1
                m, m_ln = before * 4 + 2, before * 3 + 2
                a = Place(WITH_ATTENTION, [fills[b] + before * per_fill[b] for b in range(2)],
                          [copies[b] + before * per_copy[b] for b in range(2)], ffn=2 * i - 1, attn=before,
                          norm={"qkv": m, "o": m + 1, "ffn2": m + 2}, stats={"qkv": m_ln, "ffn2": m_ln + 1},
                          block=i, loaded=i)
                run(a)
                return a.after(), m + 2, m_ln + 1

            with eng.Fori(1, B - 1) as i:
                counts, m, m_ln = first_of(i)
                run(Place(SECOND, *counts, ffn=2 * i, attn=i, norm={"ffn1": m + 1, "qkv": m + 2},
                          stats={"ffn1": m_ln + 1, "qkv": m_ln + 2}, block=i - 1, loaded=i + 1))
            counts, m, m_ln = first_of(B - 1)
            place = Place(SECOND_WITH_ATTENTION, *counts, ffn=2 * B - 2, attn=B - 1,
                          norm={"qkv": m + 1, "o": m + 2, "ffn2": m + 3}, stats={"qkv": m_ln + 1, "ffn2": m_ln + 2},
                          block=B - 2, x=(xin, xt))
            run(place)
            run(Place(LAST, *place.after(), ffn=2 * B - 1, block=B - 1, x2=xin, y=xt))

        def attention_buffers(place):
            return place.x or (place.x2, place.y)

        def norm_source(place, which):
            return {"ffn1": xin, "next": x_next, "qkv": x1}.get(which) or attention_buffers(place)[0]

        def norm_target(place, which):
            return xt if which in ("ffn1", "next") else attention_buffers(place)[1]

        def hidden(place, j):
            return first_hid[j] if place.steps is FIRST else hid[:, j % 2]

        block = ctx.enter_context(nc.Block())

        @block.sync
        def _(sp):
            def load_chunk(j):
                for m, mat in enumerate((w1, w3)):
                    sp.dma_start(stage[:, j % STAGES, m, :], mat[P * j:P * (j + 1), :]).then_inc(w_loaded[j % STAGES], 16)

            def quarter(q):
                src = qkv_w[q * D:(q + 1) * D, :] if q < 3 else proj_w
                return src.rearrange("(c p) d -> p c d", p=P)

            def load_half(q, half):
                rows_h = slice(2 * half, 2 * half + 2)
                sp.dma_start(qst[:, rows_h, :], quarter(q)[:, rows_h, :]).then_inc(qst_loaded, 16)

            def load_w2(t, half):
                cols = slice(half * H // 2, (half + 1) * H // 2)
                sp.dma_start(w2n[:, t, cols], w2[P * t:P * (t + 1), cols]).then_inc(w2_loaded[t], 16)

            load_chunk(0)
            sp.dma_start(xin[:], x[0].rearrange("(t p) d -> p t d", p=P)).then_inc(x_loaded, 16)
            for j in range(1, STAGES):
                load_chunk(j)
            for half in range(2):
                load_w2(0, half)
            w2_loads = {0: (1, 0), 1: (1, 1), 4: (2, 0), 5: (2, 1), 8: (3, 0), 9: (3, 1)}
            q_loads = {2: (0, 0), 3: (0, 1), 6: (1, 0), 7: (1, 1), 10: (2, 0), 11: (2, 1), 13: (3, 0), 14: (3, 1)}
            for c in range(HT):
                for m in range(2):
                    n = 2 * c + m
                    sp.wait_ge(w_lo, n + 1)
                    sp.dma_start_transpose((w1t, w3t)[m][:, :, :, P * c:P * (c + 1)].rearrange("p a k h -> p (a k) h"),
                                           w_parts[n % 4].rearrange("p a d -> p (a d)")).then_inc(w_turned[n % 4], 16)
                if c + STAGES < HT:
                    load_chunk(c + STAGES)
                if c in w2_loads:
                    load_w2(*w2_loads[c])
                if c in q_loads:
                    q, half = q_loads[c]
                    if q and half == 0:
                        sp.wait_ge(q_sum, q)
                    load_half(q, half)
                if c == 12:
                    sp.dma_start(x_next, x[1].rearrange("(t p) d -> p t d", p=P)).then_inc(x_next_loaded, 16)
                if c == HT - 1:
                    for dst, src in ((qnw_row, qkv_norm_w), (nw_row, norm_w), (pw_row, proj_norm_w), (s_row, s)):
                        sp.dma_start(dst[:], src.rearrange("(a n) -> a n", a=1).partition_broadcast(P)).then_inc(rows_loaded, 16)
            sp.wait_ge(w2_had, HT)
            for q in range(FOURTHS):
                sp.dma_start(wst[:, 4 * q:4 * q + 4, :], quarter(q)).then_inc(wst_loaded[q], 16)
            x_tiles = x.rearrange("b (t p) d -> (b t) p d", p=P)
            out_tiles = out.rearrange("b (t p) d -> (b t) p d", p=P)

            def run(place):
                for step, arg in place.steps:
                    if step == "resid" and arg == ("ffn1", TT - 1):
                        if not (isinstance(place.block, int) and place.block == B - 1):
                            sp.wait_ge(res_done, TT * (place.ffn + 1))
                            sp.dma_start(xin[:], x_tiles[bass.ds((place.block + 1) * TT, TT)].rearrange("t p d -> p t d")
                                         ).then_inc(x_loaded, 16)
                    elif step == "resid" and place.steps is LAST:
                        t = arg[1]
                        sp.wait_ge(res_done, TT * place.ffn + t + 1)
                        sp.dma_start(out_tiles[place.block * TT + t], xin[:, t, :]).then_inc(y_stored, 16)
                    elif step == "resid" and arg == ("ffn2", TT - 1):
                        sp.wait_ge(res_done, TT * (place.ffn + 1))
                        sp.dma_start(out_tiles[bass.ds(place.block * TT, TT)].rearrange("t p d -> p t d"), x2).then_inc(y_stored, 16)

            program(sp, run)
            sp.wait_ge(y_stored, 16 * (B - 1 + TT))

        @block.gpsimd
        def _(pool):
            chain = [0]

            def link(ins):
                chain[0] += 1
                ins.then_inc(pool_chain, 1)
                pool.wait_ge(pool_chain, chain[0])

            link(nc.gpsimd.memset(ident[:], 0.0))
            nc.gpsimd.affine_select(out=ident[:], in_=ident[:], pattern=[[-1, P]], compare_op=ALU.not_equal, fill=1.0,
                                    base=0, channel_multiplier=1).then_inc(pool_const, 1)
            nc.gpsimd.memset(half[:], -0.5).then_inc(pool_const, 1)
            nc.gpsimd.iota(junk[:, 2 * P:3 * P].bitcast(I32), [[0, P]], base=0, channel_multiplier=1).then_inc(pool_const, 1)
            nc.gpsimd.iota(junk[:, 3 * P:4 * P].bitcast(I32), [[1, P]], base=0, channel_multiplier=0).then_inc(pool_const, 1)
            pool.wait_ge(pool_const, 4)

            def run(place):
                for step, arg in place.steps:
                    if step == "stat":
                        m = place.norm[arg]
                        pool.wait_ge(ln_veps, m + 1)
                        if not known_zero(m):
                            pool.wait_ge(ln_norm, TT * m)
                        nc.gpsimd.tensor_tensor(rstd[:], veps[:], half[:], ALU.pow).then_inc(ln_rstd, 1)
                    elif step == "q":
                        ag = place.attn * GROUPS + arg
                        if arg:
                            b, fill = place.filled("pv", (arg - 1, 0))
                            pool.wait_ge(a_ready[b], fill)
                        b, _ = place.filled(step, arg)
                        pool.wait_ge(a_free[b], place.copied(step, arg, b) + 1)
                        nc.gpsimd.tensor_tensor(qdec.rearrange("p (c t) -> p c t", c=TT), qT[:].rearrange("p (c t) -> p c t", c=TT),
                                                lam_t[:, arg:arg + 1, :].to_broadcast([P, TT, P]), ALU.mult).then_inc(q_dec, 1)
                    elif step == "fly":
                        t, st = arg
                        src, dst = (w2n[:, t, :], w2p) if st % 2 == 0 else (w2p, w2n[:, t, :])
                        if st == 0:
                            pool.wait_ge(w2_loaded[t], 32)
                            if t:
                                pool.wait_ge(w2_but, t)
                        elif st == 1:
                            pool.wait_ge(w2_ss, 4 * (t + 1))
                        a = src.rearrange("p (a c m) -> p a c m", c=2, m=P << st)
                        b = dst.rearrange("p (a c m) -> p a c m", c=2, m=P << st)
                        nc.gpsimd.tensor_tensor(b[:, :, 0, :], a[:, :, 0, :], a[:, :, 1, :], ALU.add)
                        ins = nc.gpsimd.tensor_tensor(b[:, :, 1, :], a[:, :, 0, :], a[:, :, 1, :], ALU.subtract)
                        if st < BUTTERFLIES - 1:
                            link(ins)
                        else:
                            ins.then_inc(w2_but, 1)
                    elif step == "wtop":
                        pool.wait_ge(w2_tops, 1)
                        nc.gpsimd.partition_all_reduce(top_all[:], tops[:], P, bass.bass_isa.ReduceOp.max).then_inc(w2_all, 1)
                    elif step == "qmean":
                        pool.wait_ge(q_sum, FOURTHS)
                        nc.gpsimd.partition_all_reduce(asum_all[:], asum[:], P, bass.bass_isa.ReduceOp.add).then_inc(q_all, 1)
                    elif step == "decay":
                        pool.wait_ge(w_ss, 2 * HT)
                        pool.wait_ge(w2_ss, 4 * KT)
                        nc.gpsimd.iota(junk[:, 0:P], [[1, P]], base=0, channel_multiplier=-1,
                                       allow_small_or_imprecise_dtypes=True).then_inc(decay_numbers, 1)
                        nc.gpsimd.iota(junk[:, P:2 * P], [[1, P]], base=0, channel_multiplier=0,
                                       allow_small_or_imprecise_dtypes=True).then_inc(decay_numbers, 1)
                        nc.gpsimd.iota(tiny[:, 0:1], [[0, 1]], base=P, channel_multiplier=-1,
                                       allow_small_or_imprecise_dtypes=True).then_inc(decay_numbers, 1)
                        pool.wait_ge(decay_exp, 1)
                        nc.gpsimd.affine_select(out=mask[:], in_=mask[:], pattern=[[0, HEADS], [1, P]], compare_op=ALU.is_ge,
                                                fill=0.0, base=0, channel_multiplier=-1).then_inc(decay_exp, 1)

            program(pool, run)

        @block.scalar
        def _(act):
            act.wait_ge(pool_const, 1)
            nc.scalar.copy(ident16[:], ident[:]).then_inc(act_const, 1)
            act.wait_ge(dve_const, 1)
            squares = [(act_const, 1)]

            def move_high(parts, dst):
                for h in range(HG):
                    ins = nc.scalar.copy(dst[0:HD, h, :], parts[HD * h:HD * (h + 1), 0, :])
                return ins

            def sum_squares(v, out, done):
                act.wait_ge(*squares[-1])
                nc.scalar.activation(junk[:], v, ACT.Square, accum_out=out).then_inc(done, 1)
                squares.append((done, 1 + sum(1 for d, _ in squares if d is done)))

            def run(place):
                n = place.ffn
                for step, arg in place.steps:
                    if step == "wsum":
                        j = arg
                        act.wait_ge(w_loaded[j % STAGES], 32 * (j // STAGES + 1))
                        for m in range(2):
                            sum_squares(stage[:, j % STAGES, m, :], row_ss[:, j, m:m + 1], w_ss)
                    elif step == "w2sum":
                        t, part = divmod(arg, 2)
                        act.wait_ge(w2_loaded[t], 32)
                        for q in (2 * part, 2 * part + 1):
                            sum_squares(w2n[:, t, D * q:D * (q + 1)], ss2[:, t, q:q + 1], w2_ss)
                    elif step == "wprep":
                        j, m = divmod(arg, 2)
                        act.wait_ge(w_sc, scaled(j))
                        if arg >= 4:
                            act.wait_ge(w_turned[arg % 4], 16 * (arg // 4))
                        nc.scalar.activation(w_parts[arg % 4][:, 0, :], stage[:, j % STAGES, m, :], ACT.Copy,
                                             scale=row_sc[:, j, m:m + 1]).then_inc(w_hi, 1)
                    elif step == "w2turn":
                        j = arg
                        b, fill = place.filled(step, arg)
                        act.wait_ge(a_ready[b], fill)
                        if j >= 2:
                            act.wait_ge(w2_had, j - 1)
                        else:
                            act.wait_ge((hfull_ready, lo_ready)[j], HT)
                        nc.scalar.copy(w2c[j % 2], a_bank[b][:]).then_inc(a_free[b], 1)
                    elif step == "w2had":
                        j = arg
                        act.wait_ge(w2_had, j + 1)
                        act.wait_ge(w2_f, 1)
                        nc.scalar.activation(w2t[:, 0, j, :], had_bank[j % 2][:], ACT.Copy, scale=f2[:, j:j + 1]).then_inc(w2_hi, 1)
                    elif step == "decay":
                        act.wait_ge(decay_rates, 3)
                        act.wait_ge(ln_norm, 2 * TT)
                        for h in range(HEADS):
                            ins = nc.scalar.activation(mask[:, h, :], junk[:, 0:P], ACT.Exp, scale=s_row[:, h:h + 1])
                        ins.then_inc(decay_exp, 1)
                        for g in range(GROUPS):
                            nc.scalar.activation(lam_t[:, g, :], junk[:, P:2 * P], ACT.Exp, scale=s_col[:, g:g + 1])
                        nc.scalar.activation(decay_bound[:], decay_bound[:], ACT.Exp, scale=float(P)).then_inc(decay_top, 1)
                        nc.scalar.activation(lam_rev[:], s_row[:], ACT.Exp, scale=tiny[:, 0:1])
                        nc.scalar.activation(lam_T[:], s_col[:], ACT.Exp, scale=float(P)).then_inc(act_const, 1)
                    elif step == "fit":
                        act.wait_ge(decay_fit, 2)
                        act.wait_ge(decay_exp, 2)
                        nc.scalar.activation(mask[:], mask[:], ACT.Copy, scale=decay_bound[:]).then_inc(decay_fit, 1)
                    elif step == "qscale":
                        act.wait_ge(q_scales, 1)
                        for r in (2 * arg, 2 * arg + 1):
                            act.wait_ge(wst_loaded[r // 4], 16)
                            part = 6 if r < QKV_T else 7
                            nc.scalar.activation(wst[:, r, :], wst[:, r, :], ACT.Copy, scale=tiny[:, part:part + 1]).then_inc(q_scaled, 1)
                    elif step == "gate":
                        j = arg
                        if place.steps is FIRST:
                            act.wait_ge(w_sc, scaled(j))
                        act.wait_ge(g_ready, n * HT + (j + 1))
                        if not known_zero(n * HT + j):
                            act.wait_ge(hfull_ready, n * HT + j)
                        nc.scalar.activation(gate, g_bank[:], ACT.Silu, scale=g_scale[:, j:j + 1]).then_inc(gate_ready, 1)
                    elif step == "lin":
                        j = arg
                        act.wait_ge(hfull_ready, n * HT + (j + 1))
                        if place.steps is FIRST:
                            if j >= HT - 2:
                                act.wait_ge(w_turned[j - (HT - 2)], 16 * 2 * HT // 4)
                        elif j == 1 and not known_zero(n):
                            act.wait_ge(d_ready, n * TT)
                        elif j != 1 and not known_zero(n * (HT - 1) + max(j - 1, 0)):
                            act.wait_ge(d_step, n * (HT - 1) + max(j - 1, 0))
                        nc.scalar.copy(hidden(place, j)[:, 0, :], hfull).then_inc(hi_ready, 1)
                    elif step == "turn":
                        which, t = arg
                        b, fill = place.filled(step, arg)
                        act.wait_ge(a_ready[b], fill)
                        nc.scalar.copy(norm_target(place, which)[:, 0, :, P * t:P * (t + 1)],
                                       a_bank[b][:].rearrange("p (k t) -> p k t", k=KT)).then_inc(a_free[b], 1)
                    elif step == "qturn":
                        b, fill = place.filled(step, arg)
                        act.wait_ge(a_ready[b], fill)
                        dst, r = (wqkv, 2 * arg) if 2 * arg < QKV_T else (wproj, 2 * arg - QKV_T)
                        nc.scalar.copy(dst[:, :, P * r:P * (r + 2)].rearrange("p k (a t) -> p a k t", a=2),
                                       a_bank16[b]).then_inc(a_free[b], 1)
                    elif step == "q":
                        b, fill = place.filled(step, arg)
                        act.wait_ge(a_ready[b], fill)
                        ag = place.attn * GROUPS + arg
                        if not known_zero(ag):
                            act.wait_ge(q_lo, ag)
                            act.wait_ge(q_dec, ag)
                        nc.scalar.mul(qT[:], a_bank[b][:], QKV_SCALE / X_SCALE).then_inc(a_free[b], 1)
                        act.wait_ge(a_free[b], place.copied(step, arg, b) + 1)
                        nc.scalar.copy(q_parts[:, 0, :], qT[:]).then_inc(q_hi, 1)
                        act.wait_ge(q_hi, ag + 1)
                        move_high(q_parts, qs).then_inc(q_moved, 1)
                    elif step == "k":
                        b, fill = place.filled(step, arg)
                        ag = place.attn * GROUPS + arg
                        act.wait_ge(a_ready[b], fill)
                        if not known_zero(ag):
                            act.wait_ge(sc_lo, TT * ag)
                        nc.scalar.mul(flow, a_bank[b][:], QKV_SCALE / X_SCALE).then_inc(a_free[b], 1)
                        act.wait_ge(a_free[b], place.copied(step, arg, b) + 1)
                        nc.scalar.copy(k_parts[:, 0, :], flow).then_inc(k_hi, 1)
                        act.wait_ge(k_hi, ag + 1)
                        move_high(k_parts, ks).then_inc(k_moved, 1)
                    elif step == "v":
                        t = arg
                        b, fill = place.filled(step, arg)
                        act.wait_ge(a_ready[b], fill)
                        if t == 0 and not known_zero(place.attn) and place.x is None:
                            act.wait_ge(y_stored, 16 * place.attn)
                        nc.scalar.mul(values(attention_buffers(place)[0])[:, t, :, 0, :],
                                      a_bank[b][:].rearrange("p (g e) -> p g e", g=GROUPS), QKV_SCALE / X_SCALE).then_inc(a_free[b], 1)
                    elif step == "kturn":
                        b, _ = place.filled(step, arg)
                        act.wait_ge(a_free[b], place.copied(step, arg, b) + 1)
                        nc.scalar.copy(kdec[:, 0, :], flow[:, 0:(TT - 1) * P]).then_inc(kd_hi, 1)
                    elif step == "score":
                        g, c = arg
                        b, _ = place.filled(step, arg)
                        act.wait_ge(a_free[b], place.copied(step, arg, b) + 1)
                        nc.scalar.copy(sc[:, c % 2, 0], flow.rearrange("p (h t) -> p h t", h=HG)).then_inc(sc_hi, 1)
                    elif step == "pv" and arg[1] == TT - 1:
                        g = arg[0]
                        b, fill = place.filled(step, arg)
                        act.wait_ge(a_ready[b], fill)
                        nc.scalar.activation(attention_buffers(place)[0][:, :, P * g:P * (g + 1)],
                                             a_bank[b][:].rearrange("p (c e) -> p c e", c=TT), ACT.Copy,
                                             scale=o_scale[:]).then_inc(a_free[b], 1)

            program(act, run)

        @block.vector
        def _(dve):
            chain = [0]

            def link(ins):
                chain[0] += 1
                ins.then_inc(dve_chain, 1)
                dve.wait_ge(dve_chain, chain[0])

            def power(out, in_, flip):
                if flip:
                    return nc.vector.tensor_scalar(out.bitcast(I32), in_.bitcast(I32), EXPONENT, EXPONENT,
                                                   ALU.bitwise_and, ALU.bitwise_xor)
                return nc.vector.tensor_scalar(out.bitcast(I32), in_.bitcast(I32), EXPONENT, None, ALU.bitwise_and)

            def move(parts, dst, i, part):
                for h in range(HG):
                    ins = nc.vector.tensor_copy(dst[HD * i:HD * (i + 1), h, :], parts[HD * h:HD * (h + 1), part, :])
                return ins

            def inverse_norm(out, ss):
                link(nc.vector.tensor_scalar(out.bitcast(I32), ss.bitcast(I32), 24, None, ALU.logical_shift_right))
                return nc.vector.tensor_scalar(out.bitcast(I32), out.bitcast(I32), -float(1 << 23), float(189 << 23),
                                               ALU.mult, ALU.add)

            dve.wait_ge(pool_const, 4)
            ip, ij = junk[:, 2 * P:3 * P].bitcast(I32), junk[:, 3 * P:4 * P].bitcast(I32)
            link(nc.vector.tensor_tensor(ip, ip, ij, ALU.bitwise_and))
            for shift in (4, 2, 1):
                link(nc.vector.tensor_scalar(ij, ip, shift, None, ALU.logical_shift_right))
                link(nc.vector.tensor_tensor(ip, ip, ij, ALU.bitwise_xor))
            link(nc.vector.tensor_scalar(ip, ip, 1, None, ALU.bitwise_and))
            nc.vector.tensor_copy(hadamard[:], ip).then_inc(dve_const, 1)
            dve.wait_ge(dve_const, 1)
            nc.vector.tensor_scalar(hadamard[:], hadamard[:], -2.0, 1.0, ALU.mult, ALU.add).then_inc(dve_const, 1)
            link(nc.vector.memset(diag[:], 0.0))
            for h in range(HG):
                nc.vector.memset(diag[HD * h:HD * (h + 1), HD * h:HD * (h + 1)], SCORE_SCALE)

            def run(place):
                n, a = place.ffn, place.attn
                for step, arg in place.steps:
                    if step == "wscale":
                        js = SCALED[arg]
                        dve.wait_ge(w_ss, 2 * js.stop)
                        scale, inverse = rows[:, 0, js, :], rows[:, 1, js, :]
                        link(inverse_norm(scale, row_ss[:, js, :]))
                        link(power(inverse, scale, True))
                        nc.vector.tensor_scalar(row_sc[:, js, :], scale, W_SCALE, None, ALU.mult)
                        nc.vector.tensor_scalar(g_scale[:, js], inverse[:, :, 0], 0.5 / (X_SCALE * W_SCALE), None, ALU.mult)
                        nc.vector.tensor_scalar(l_scale[:, js], scale[:, :, 0], HID_SCALE / (X_SCALE * W_SCALE), None,
                                                ALU.mult).then_inc(w_sc, 1)
                    elif step == "wprep":
                        j, m = divmod(arg, 2)
                        dve.wait_ge(w_hi, arg + 1)
                        parts = w_parts[arg % 4]
                        nc.vector.scalar_tensor_tensor(out=parts[:, 1, :], in0=stage[:, j % STAGES, m, :], scalar=row_sc[:, j, m:m + 1],
                                                       in1=parts[:, 0, :], op0=ALU.mult, op1=ALU.subtract).then_inc(w_lo, 1)
                    elif step == "wtop":
                        dve.wait_ge(w_sc, len(SCALED))
                        link(nc.vector.tensor_tensor(f2[:], rows[:, 1, :, 0], rows[:, 1, :, 1], ALU.mult))
                        nc.vector.tensor_reduce(tops[:, 0:1], f2[:], AX.X, ALU.max)
                        dve.wait_ge(w2_ss, 4 * KT)
                        link(nc.vector.tensor_reduce(tiny[:, 11:11 + KT], ss2[:], AX.X, ALU.add))
                        nc.vector.tensor_reduce(tops[:, 1:2], tiny[:, 11:11 + KT], AX.X, ALU.max).then_inc(w2_tops, 1)
                    elif step == "wfit":
                        dve.wait_ge(w2_all, 1)
                        link(inverse_norm(tiny[:, 5:6], top_all[:, 1:2]))
                        link(power(tiny[:, 4:5], top_all[:, 0:1], True))
                        link(nc.vector.tensor_tensor(tiny[:, 5:6], tiny[:, 5:6], tiny[:, 4:5], ALU.mult))
                        link(nc.vector.tensor_scalar(tiny[:, 5:6], tiny[:, 5:6], 2.0 * HID_SCALE / 2.0 ** 6 * W_SCALE, None, ALU.mult))
                        nc.vector.tensor_scalar(f2[:], f2[:], tiny[:, 5:6], 0.25 / HID_SCALE, ALU.mult, ALU.mult).then_inc(w2_f, 1)
                        link(nc.vector.reciprocal(ffn_unscale[:], tiny[:, 5:6]))
                        link(nc.vector.tensor_scalar(ffn_unscale[:], ffn_unscale[:], 0.5 / float(np.sqrt(H)), None, ALU.mult))
                    elif step == "w2had":
                        j = arg
                        dve.wait_ge(w2_hi, j + 1)
                        nc.vector.scalar_tensor_tensor(out=w2t[:, 1, j, :], in0=had_bank[j % 2][:], scalar=f2[:, j:j + 1],
                                                       in1=w2t[:, 0, j, :], op0=ALU.mult, op1=ALU.subtract).then_inc(w2_lo, 1)
                    elif step == "decay":
                        dve.wait_ge(rows_loaded, 16 * 4)
                        nc.vector.tensor_scalar(s_row[:], s_row[:], -1.0, None, ALU.mult).then_inc(decay_rates, 1)
                        dve.wait_ge(decay_rates, 1)
                        for h in range(HG):
                            rows_h = slice(HD * h, HD * (h + 1))
                            ins = nc.vector.tensor_copy(s_col[rows_h, :], s_row[rows_h, :].rearrange("p (g h) -> p h g", h=HG)[:, h, :])
                        ins.then_inc(decay_rates, 1)
                        nc.vector.tensor_reduce(decay_bound[:], s_row[:], AX.X, ALU.max).then_inc(decay_fit, 1)
                        dve.wait_ge(decay_fit, 1)
                        nc.vector.tensor_scalar(decay_bound[:], decay_bound[:], 0.0, None, ALU.max)
                        dve.wait_ge(decay_numbers, 3)
                        nc.vector.tensor_scalar(junk[:, 0:P], junk[:, 0:P], 0.0, None, ALU.max).then_inc(decay_rates, 1)
                        for i, row in ((1, qnw_row), (2, pw_row)):
                            link(nc.vector.tensor_reduce(tiny[:, i:i + 1], row[:], AX.X, ALU.max, apply_absolute_value=True))
                            link(nc.vector.tensor_scalar(tiny[:, i:i + 1], tiny[:, i:i + 1], TINY, None, ALU.max))
                            link(power(tiny[:, i:i + 1], tiny[:, i:i + 1], True))
                            link(nc.vector.tensor_scalar(tiny[:, i:i + 1], tiny[:, i:i + 1], 0.25, None, ALU.mult))
                            link(nc.vector.tensor_scalar(row[:], row[:], tiny[:, i:i + 1], None, ALU.mult))
                            link(nc.vector.reciprocal(tiny[:, 8 + i:9 + i], tiny[:, i:i + 1]))
                    elif step == "fit":
                        dve.wait_ge(decay_top, 1)
                        link(power(decay_bound[:], decay_bound[:], True))
                        nc.vector.tensor_scalar(decay_bound[:], decay_bound[:], 0.25, None, ALU.mult).then_inc(decay_fit, 1)
                        dve.wait_ge(decay_fit, 2)
                        dve.wait_ge(act_const, 2)
                        nc.vector.tensor_scalar(lam_rev[:], lam_rev[:], decay_bound[:], None, ALU.mult)
                        dve.wait_ge(q_scales, 1)
                        nc.vector.tensor_scalar(proj_scale[:], tiny[:, 4:5], tiny[:, 10:11], 1.0 / X_SCALE, ALU.mult, ALU.mult)
                        link(nc.vector.tensor_scalar(tiny[:, 8:9], tiny[:, 3:4], tiny[:, 9:10], None, ALU.mult))
                        link(nc.vector.reciprocal(o_scale[:], decay_bound[:]))
                        link(nc.vector.tensor_scalar(o_scale[:], o_scale[:], QK_SCALE / (QKV_SCALE ** 3 * SCORE_SCALE), None, ALU.mult))
                        link(nc.vector.tensor_scalar(o_scale[:], o_scale[:], tiny[:, 8:9], tiny[:, 8:9], ALU.mult, ALU.mult))
                        nc.vector.tensor_scalar(o_scale[:], o_scale[:], tiny[:, 8:9], None, ALU.mult).then_inc(q_scales, 1)
                    elif step == "qprep":
                        if arg:
                            b, fill = place.filled("qturn", arg - 1)
                            dve.wait_ge(a_ready[b], fill)
                        for r in (2 * arg, 2 * arg + 1):
                            dve.wait_ge(q_scaled, r + 1)
                            signs, negative = tern[:, r % 2, 0, :], tern[:, r % 2, 1, :]
                            link(nc.vector.tensor_scalar(negative, wst[:, r, :], -0.5, None, ALU.is_lt))
                            nc.vector.scalar_tensor_tensor(out=signs, in0=wst[:, r, :], scalar=0.5, in1=negative, op0=ALU.is_gt,
                                                           op1=ALU.subtract).then_inc(q_tern, 1)
                    elif step == "lin":
                        j = arg
                        dve.wait_ge(l_ready, n * HT + (j + 1))
                        dve.wait_ge(gate_ready, n * HT + (j + 1))
                        if not known_zero(n * HT + j):
                            dve.wait_ge(lo_ready, n * HT + j)
                        nc.vector.scalar_tensor_tensor(out=hfull, in0=l_bank[:], scalar=l_scale[:, j:j + 1], in1=gate,
                                                       op0=ALU.mult, op1=ALU.mult).then_inc(hfull_ready, 1)
                    elif step == "low":
                        j = arg
                        dve.wait_ge(hi_ready, n * HT + (j + 1))
                        parts = hidden(place, j)
                        nc.vector.tensor_tensor(parts[:, 1, :], hfull, parts[:, 0, :], ALU.subtract).then_inc(lo_ready, 1)
                    elif step == "resid":
                        which, t = arg
                        src, dst = (xin, x1) if which == "ffn1" else (place.x2, place.x2)
                        dve.wait_ge(d_ready, n * TT + (t + 1))
                        if which == "ffn1" and t == 0:
                            dve.wait_ge(x_loaded, 16 * (place.loaded + 1))
                        nc.vector.scalar_tensor_tensor(out=dst[:, t, :], in0=d_bank[t][:], scalar=ffn_unscale[:],
                                                       in1=src[:, t, :], op0=ALU.mult, op1=ALU.add).then_inc(res_done, 1)
                    elif step == "stat" and arg != "o":
                        m, m_ln = place.norm[arg], place.stats[arg]
                        src = norm_source(place, arg)
                        if arg == "ffn1":
                            dve.wait_ge(x_loaded, 16 * (place.loaded + 1))
                        elif arg == "next":
                            dve.wait_ge(x_next_loaded, 16)
                        elif arg == "qkv":
                            dve.wait_ge(res_done, TT * n)
                        else:
                            for b in range(2):
                                dve.wait_ge(a_free[b], place.copied(step, arg, b))
                        for t in range(TT):
                            nc.vector.bn_stats(stat[:, t, :], src[:, t, :]).then_inc(ln_stats, 1)
                        dve.wait_ge(ln_stats, TT * (m_ln + 1))
                        even, odd = stat[:, 0:TT, 1], stat[:, 0:TT, 4]
                        nc.vector.tensor_tensor(mean[:], even, odd, ALU.add).then_inc(ln_small, 1)
                        nc.vector.tensor_tensor(ms[:, 0, 0:TT], even, odd, ALU.subtract).then_inc(ln_small, 1)
                        nc.vector.tensor_tensor(ms[:, 1, 0:TT], stat[:, 0:TT, 2], stat[:, 0:TT, 5], ALU.add).then_inc(ln_small, 1)
                        base = 5 * m_ln
                        dve.wait_ge(ln_small, base + 2)
                        nc.vector.tensor_tensor(ms[:, 0, 0:TT], ms[:, 0, 0:TT], ms[:, 0, 0:TT], ALU.mult).then_inc(ln_small, 1)
                        nc.vector.tensor_scalar(mean[:], mean[:], 0.5, None, ALU.mult)
                        dve.wait_ge(ln_small, base + 4)
                        nc.vector.scalar_tensor_tensor(out=ms[:, 0, 0:TT], in0=ms[:, 0, 0:TT], scalar=D / 4.0,
                                                       in1=ms[:, 1, 0:TT], op0=ALU.mult, op1=ALU.add).then_inc(ln_small, 1)
                        dve.wait_ge(ln_small, base + 5)
                        if not known_zero(m):
                            dve.wait_ge(ln_rstd, m)
                        mul, add = (1.0 + RMS_EPS, LN_EPS * RMS_EPS) if arg == "qkv" else (1.0, LN_EPS)
                        nc.vector.tensor_scalar(veps[:], ms[:, 0, 0:TT], mul / D / X_SCALE ** 2, add / X_SCALE ** 2,
                                                ALU.mult, ALU.add).then_inc(ln_veps, 1)
                    elif step == "ostat":
                        t = arg
                        src = attention_buffers(place)[0]
                        dve.wait_ge(a_free[1], place.copied(step, arg, 1))
                        nc.vector.bn_stats(stat[:, t, :], src[:, t, :]).then_inc(o_stats, 1)
                        nc.vector.tensor_tensor(src[:, t, :], src[:, t, :], nw_row[:], ALU.mult).then_inc(o_scaled, 1)
                        dve.wait_ge(o_scaled, TT * a + (t + 1))
                        nc.vector.bn_stats(stat[:, TT + t, :], src[:, t, :]).then_inc(o_stats, 1)
                    elif step == "stat":
                        m = place.norm[arg]
                        dve.wait_ge(o_stats, 2 * TT * (a + 1))
                        even, odd = stat[:, :, 1], stat[:, :, 4]
                        base = 6 * a
                        nc.vector.tensor_tensor(ms[:, 0, :], even, even, ALU.mult).then_inc(o_small, 1)
                        nc.vector.tensor_tensor(ms[:, 1, :], odd, odd, ALU.mult).then_inc(o_small, 1)
                        nc.vector.tensor_tensor(ms[:, 2, :], stat[:, :, 2], stat[:, :, 5], ALU.add).then_inc(o_small, 1)
                        dve.wait_ge(o_small, base + 2)
                        nc.vector.tensor_tensor(ms[:, 0, :], ms[:, 0, :], ms[:, 1, :], ALU.add).then_inc(o_small, 1)
                        dve.wait_ge(o_small, base + 4)
                        nc.vector.scalar_tensor_tensor(out=ms[:, 1, :], in0=ms[:, 0, :], scalar=D / 2.0,
                                                       in1=ms[:, 2, :], op0=ALU.mult, op1=ALU.add).then_inc(o_small, 1)
                        dve.wait_ge(o_small, base + 5)
                        nc.vector.scalar_tensor_tensor(out=ms[:, 0, 0:TT], in0=ms[:, 1, 0:TT], scalar=RMS_EPS,
                                                       in1=ms[:, 1, TT:2 * TT], op0=ALU.mult, op1=ALU.add).then_inc(o_small, 1)
                        dve.wait_ge(o_small, base + 6)
                        dve.wait_ge(ln_rstd, m)
                        nc.vector.tensor_scalar(veps[:], ms[:, 0, 0:TT], D * RMS_EPS * OUT_NORM_EPS, 1.0 / D / X_SCALE ** 2,
                                                ALU.add, ALU.mult).then_inc(ln_veps, 1)
                    elif step == "prep":
                        which, t = arg
                        m = place.norm[which]
                        src = norm_source(place, which)[:, t, :]
                        dve.wait_ge(ln_rstd, m + 1)
                        if place.steps is NORM:
                            for b in range(2):
                                dve.wait_ge(a_free[b], place.copied(step, arg, b))
                        if which == "qkv":
                            nc.vector.scalar_tensor_tensor(out=cent[:, t % 3], in0=src, scalar=mean[:, t:t + 1], in1=qnw_row[:],
                                                           op0=ALU.subtract, op1=ALU.mult).then_inc(ln_cent, 1)
                            dve.wait_ge(ln_cent, TT * a + (t + 1))
                            ins = nc.vector.tensor_scalar(cent[:, t % 3], cent[:, t % 3], rstd[:, t:t + 1], None, ALU.mult)
                        elif which == "o":
                            ins = nc.vector.scalar_tensor_tensor(out=cent[:, t % 3], in0=src, scalar=rstd[:, t:t + 1],
                                                                 in1=pw_row[:], op0=ALU.mult, op1=ALU.mult)
                        else:
                            ins = nc.vector.tensor_scalar(cent[:, t % 3], src, mean[:, t:t + 1], rstd[:, t:t + 1],
                                                          ALU.subtract, ALU.mult)
                        ins.then_inc(ln_norm, 1)
                    elif step == "turn":
                        which, t = arg
                        b, fill = place.filled(step, arg)
                        dst = norm_target(place, which)[:, :, :, P * t:P * (t + 1)]
                        dve.wait_ge(a_ready[b], fill)
                        dve.wait_ge(a_free[b], place.copied(step, arg, b) + 1)
                        nc.vector.tensor_tensor(dst[:, 1], a_bank[b][:].rearrange("p (k t) -> p k t", k=KT), dst[:, 0],
                                                ALU.subtract).then_inc(a_free[b], 1)
                    elif step == "qsum":
                        dve.wait_ge(qst_loaded, 32 * (arg + 1))
                        nc.vector.tensor_reduce(asum[:, 4 * arg:4 * arg + 4], qst, AX.X, ALU.add,
                                                apply_absolute_value=True).then_inc(q_sum, 1)
                    elif step == "qmean":
                        dve.wait_ge(q_all, 1)
                        nc.vector.tensor_reduce(tiny[:, 3:4], asum_all[:, 0:QKV_T], AX.X, ALU.add)
                        link(nc.vector.tensor_reduce(tiny[:, 4:5], asum_all[:, QKV_T:QKV_T + PROJ_T], AX.X, ALU.add))
                        nc.vector.tensor_scalar(tiny[:, 3:4], tiny[:, 3:4], 1.0 / (3 * D * D), 1e-5, ALU.mult, ALU.max)
                        link(nc.vector.tensor_scalar(tiny[:, 4:5], tiny[:, 4:5], 1.0 / (D * D), 1e-5, ALU.mult, ALU.max))
                        nc.vector.reciprocal(tiny[:, 6:8], tiny[:, 3:5]).then_inc(q_scales, 1)
                    elif step == "qlow":
                        ag = a * GROUPS + arg
                        dve.wait_ge(q_hi, ag + 1)
                        nc.vector.tensor_tensor(q_parts[:, 1, :], qT[:], q_parts[:, 0, :], ALU.subtract).then_inc(q_lo, 1)
                        move(q_parts, qs, 2, 0)
                        dve.wait_ge(q_lo, ag + 1)
                        move(q_parts, qs, 1, 1).then_inc(q_moved, 1)
                    elif step == "klow":
                        ag = a * GROUPS + arg
                        dve.wait_ge(k_hi, ag + 1)
                        nc.vector.tensor_tensor(k_parts[:, 1, :], flow, k_parts[:, 0, :], ALU.subtract).then_inc(k_lo, 1)
                        move(k_parts, ks, 1, 0)
                        dve.wait_ge(k_lo, ag + 1)
                        move(k_parts, ks, 2, 1).then_inc(k_moved, 1)
                    elif step == "v":
                        t = arg
                        b, fill = place.filled(step, arg)
                        dve.wait_ge(a_ready[b], fill)
                        dve.wait_ge(a_free[b], place.copied(step, arg, b) + 1)
                        v = values(attention_buffers(place)[0])[:, t]
                        nc.vector.scalar_tensor_tensor(out=v[:, :, 1, :], in0=a_bank[b][:].rearrange("p (g e) -> p g e", g=GROUPS),
                                                       scalar=QKV_SCALE / X_SCALE, in1=v[:, :, 0, :], op0=ALU.mult,
                                                       op1=ALU.subtract).then_inc(a_free[b], 1)
                    elif step == "kturn":
                        g = arg
                        ag = a * GROUPS + g
                        b, fill = place.filled(step, arg)
                        dve.wait_ge(a_ready[b], fill)
                        dve.wait_ge(k_lo, ag + 1)
                        dec = lam_rev[:, HG * g:HG * (g + 1)]
                        for c in range(TT - 1):
                            ins = nc.vector.tensor_tensor(
                                flow[:, P * c:P * (c + 1)].rearrange("p (h d) -> p h d", h=HG),
                                a_bank[b][:, P * c:P * (c + 1)].rearrange("p (h d) -> p h d", h=HG),
                                dec.rearrange("p (h a) -> p h a", a=1).to_broadcast([P, HG, HD]), ALU.mult)
                        ins.then_inc(a_free[b], 1)
                        dve.wait_ge(kd_hi, ag + 1)
                        nc.vector.tensor_tensor(kdec[:, 1, :], flow[:, 0:(TT - 1) * P], kdec[:, 0, :], ALU.subtract).then_inc(kd_lo, 1)
                    elif step == "score":
                        g, c = arg
                        n_sc = TT * (a * GROUPS + g) + c
                        b, fill = place.filled(step, arg)
                        dve.wait_ge(a_ready[b], fill)
                        if c:
                            dve.wait_ge(sc_lo, n_sc)
                        else:
                            dve.wait_ge(kd_lo, a * GROUPS + (g + 1))
                        masked = flow.rearrange("p (h t) -> p h t", h=HG)
                        nc.vector.scalar_tensor_tensor(out=masked, in0=a_bank[b][:].rearrange("p (h t) -> p h t", h=HG),
                                                       scalar=SCORE_SCALE, in1=mask[:, HG * g:HG * (g + 1), :], op0=ALU.mult,
                                                       op1=ALU.mult).then_inc(a_free[b], 1)
                        dve.wait_ge(sc_hi, n_sc + 1)
                        nc.vector.tensor_tensor(sc[:, c % 2, 1], masked, sc[:, c % 2, 0], ALU.subtract).then_inc(sc_lo, 1)
                    elif step == "kv":
                        g = arg
                        b, fill = place.filled(step, arg)
                        dve.wait_ge(a_ready[b], fill)
                        nc.vector.tensor_tensor(state, a_bank[b][:, 0:(TT - 1) * P].rearrange("p (c e) -> p c e", c=TT - 1),
                                                diag[:].rearrange("p (a e) -> p a e", a=1).to_broadcast([P, TT - 1, P]),
                                                ALU.mult).then_inc(a_free[b], 1)
                    elif step == "state":
                        g = arg
                        ag = a * GROUPS + g
                        b, _ = place.filled("kv", g)
                        dve.wait_ge(a_free[b], place.copied("kv", g, b) + 1)
                        for c in range(1, TT - 1):
                            if c > 1:
                                dve.wait_ge(state_done, (TT - 2) * ag + (c - 1))
                            nc.vector.scalar_tensor_tensor(out=state[:, c, :], in0=state[:, c - 1, :], scalar=lam_T[:, g:g + 1],
                                                           in1=state[:, c, :], op0=ALU.mult, op1=ALU.add).then_inc(state_done, 1)
                    elif step == "proj":
                        t = arg
                        b, fill = place.filled(step, arg)
                        dve.wait_ge(a_ready[b], fill)
                        nc.vector.scalar_tensor_tensor(out=attention_buffers(place)[0][:, t, :], in0=a_bank[b][:],
                                                       scalar=proj_scale[:], in1=x1[:, t, :], op0=ALU.mult,
                                                       op1=ALU.add).then_inc(a_free[b], 1)

            program(dve, run)

        @block.tensor
        def _(pe):
            pe.wait_ge(pool_const, 1)
            pe.wait_ge(act_const, 1)

            def take(place, step, arg):
                b, _ = place.uses[step, arg]
                free = place.copied(step, arg, b)
                if not known_zero(free):
                    pe.wait_ge(a_free[b], free)
                return b

            def landed(place, step, arg, b):
                free = place.copied(step, arg, b)
                if not known_zero(free):
                    pe.wait_ge(a_free[b], free)

            def run(place):
                n = place.ffn
                for step, arg in place.steps:
                    if step == "w2turn":
                        j = arg
                        b = take(place, step, arg)
                        pe.wait_ge(w2_but, KT)
                        for t in range(KT):
                            ins = nc.tensor.transpose(a_bank[b][:, P * t:P * (t + 1)], w2n[:, t, P * j:P * (j + 1)], ident[:])
                        ins.then_inc(a_ready[b], 1)
                    elif step == "w2had":
                        j = arg
                        b, _ = place.uses["w2turn", j]
                        pe.wait_ge(a_free[b], place.copied("w2turn", j, b) + 1)
                        pe.wait_ge(dve_const, 2)
                        if j >= 2:
                            pe.wait_ge(w2_lo, j - 1)
                        else:
                            pe.wait_ge((gate_ready, hfull_ready)[j], HT)
                        nc.tensor.matmul(had_bank[j % 2][:], hadamard[:], w2c[j % 2], start=True, stop=True).then_inc(w2_had, 1)
                    elif step in ("gate", "lin"):
                        j = arg
                        src = xt if place.which == "ffn1" else place.y
                        wt, dst, done = (w1t, g_bank, g_ready) if step == "gate" else (w3t, l_bank, l_ready)
                        if step == "gate" and j == 0:
                            for b in range(2):
                                landed(place, step, arg, b)
                        if place.steps is FIRST:
                            tile = 2 * j + (step == "lin")
                            pe.wait_ge(w_turned[tile % 4], 16 * (tile // 4 + 1))
                        if not known_zero(n * HT + j):
                            pe.wait_ge(gate_ready if step == "gate" else hfull_ready, n * HT + j)
                        for k in range(KT):
                            for wp, xp in ((0, 0), (0, 1), (1, 0)):
                                ins = nc.tensor.matmul(dst[:], wt[:, wp, k, P * j:P * (j + 1)], src[:, xp, k, :],
                                                       start=(k == 0 and wp == xp), stop=(k == KT - 1 and wp == 1))
                        ins.then_inc(done, 1)
                    elif step == "down":
                        j = arg
                        parts = hidden(place, j)
                        pe.wait_ge(lo_ready, n * HT + (j + 1))
                        if place.steps is FIRST:
                            pe.wait_ge(w2_lo, j + 1)
                        if j == 0 and not known_zero(n):
                            pe.wait_ge(res_done, n * TT)
                        for t in range(TT):
                            for hp, wp in ((0, 0), (0, 1), (1, 0)):
                                ins = nc.tensor.matmul(d_bank[t][:], parts[:, hp, P * t:P * (t + 1)], w2t[:, wp, j, :],
                                                       start=(j == 0 and hp == wp), stop=(j == HT - 1 and hp == 1))
                            if j == HT - 1:
                                ins.then_inc(d_ready, 1)
                        if j < HT - 1:
                            ins.then_inc(d_step, 1)
                    elif step == "turn":
                        which, t = arg
                        m = place.norm[which]
                        b = take(place, step, arg)
                        pe.wait_ge(ln_norm, TT * m + (t + 1))
                        for k in range(KT):
                            ins = nc.tensor.transpose(a_bank[b][:, P * k:P * (k + 1)], cent[:, t % 3, P * k:P * (k + 1)], ident[:])
                        ins.then_inc(a_ready[b], 1)
                    elif step == "qturn":
                        b = take(place, step, arg)
                        pe.wait_ge(q_tern, 2 * (arg + 1))
                        for r in range(2):
                            for k in range(KT):
                                ins = nc.tensor.transpose(a_bank16[b][:, r, k, :], tern[:, r, 0, P * k:P * (k + 1)], ident16[:])
                        ins.then_inc(a_ready[b], 1)
                    elif step == "v":
                        t = arg
                        b = take(place, step, arg)
                        if t == 0:
                            for other in range(2):
                                landed(place, step, arg, other)
                        src = attention_buffers(place)[1]
                        for k in range(KT):
                            for part in range(2):
                                ins = nc.tensor.matmul(a_bank[b][:], src[:, part, k, P * t:P * (t + 1)], wqkv[:, k, 2 * D:3 * D],
                                                       start=(k == 0 and part == 0), stop=(k == KT - 1 and part == 1))
                        ins.then_inc(a_ready[b], 1)
                    elif step in ("q", "k"):
                        g = arg
                        b = take(place, step, arg)
                        src = attention_buffers(place)[1]
                        col = "qk".index(step) * D + P * g
                        for k in range(KT):
                            for part in range(2):
                                ins = nc.tensor.matmul(a_bank[b][:], wqkv[:, k, col:col + P], src[:, part, k, :],
                                                       start=(k == 0 and part == 0), stop=(k == KT - 1 and part == 1))
                        ins.then_inc(a_ready[b], 1)
                    elif step == "kturn":
                        b = take(place, step, arg)
                        pe.wait_ge(a_free[0], place.copied("k", arg, 0) + 1)
                        for c in range(TT - 1):
                            ins = nc.tensor.transpose(a_bank[b][:, P * c:P * (c + 1)], flow[:, P * c:P * (c + 1)], ident[:])
                        ins.then_inc(a_ready[b], 1)
                    elif step == "score":
                        g, c = arg
                        b = take(place, step, arg)
                        if c == 0:
                            pe.wait_ge(q_moved, 2 * (place.attn * GROUPS + (g + 1)))
                            pe.wait_ge(k_moved, 2 * (place.attn * GROUPS + (g + 1)))
                        for h in range(HG):
                            ins = nc.tensor.matmul(a_bank[b][:, P * h:P * (h + 1)], ks[0:BLOCKS * HD, h, P * c:P * (c + 1)],
                                                   qs[0:BLOCKS * HD, h, P * c:P * (c + 1)], start=True, stop=True)
                        ins.then_inc(a_ready[b], 1)
                    elif step == "kv":
                        g = arg
                        b = take(place, step, arg)
                        pe.wait_ge(kd_lo, place.attn * GROUPS + (g + 1))
                        if g == 0:
                            pe.wait_ge(a_free[1 - b], place.copied("v", TT - 2, 1 - b) + 2)
                        v = values(attention_buffers(place)[0])
                        for c in range(TT - 1):
                            for kp, vp in ((0, 0), (0, 1), (1, 0)):
                                ins = nc.tensor.matmul(a_bank[b][:, P * c:P * (c + 1)], kdec[:, kp, P * c:P * (c + 1)],
                                                       v[:, c, g, vp, :], start=(kp == vp), stop=(kp == 1))
                        ins.then_inc(a_ready[b], 1)
                    elif step == "pv":
                        g, c = arg
                        b = place.uses[step, arg][0]
                        if c == 0:
                            take(place, step, arg)
                        pe.wait_ge(sc_lo, TT * (place.attn * GROUPS + g) + (c + 1))
                        if c:
                            if c == 1:
                                pe.wait_ge(q_dec, place.attn * GROUPS + (g + 1))
                            if c >= 2:
                                pe.wait_ge(state_done, (TT - 2) * (place.attn * GROUPS + g) + (c - 1))
                            nc.tensor.matmul(a_bank[b][:, P * c:P * (c + 1)], qdec[:, P * c:P * (c + 1)], state[:, c - 1, :],
                                             start=False, stop=False, skip_group_check=True)
                        v = values(attention_buffers(place)[0])
                        for h in range(HG):
                            col = P * c + HD * h
                            for sp, vp in ((0, 0), (0, 1), (1, 0)):
                                ins = nc.tensor.matmul(a_bank[b][:, col:col + HD], sc[:, c % 2, sp, h, :],
                                                       v[:, c, g, vp, HD * h:HD * (h + 1)],
                                                       start=(c == 0 and h == 0 and sp == vp), stop=True, skip_group_check=True)
                        if c == TT - 1:
                            ins.then_inc(a_ready[b], 1)
                    elif step == "proj":
                        t = arg
                        b = take(place, step, arg)
                        if t == 0:
                            for other in range(2):
                                landed(place, step, arg, other)
                        src = attention_buffers(place)[1]
                        for k in range(KT):
                            for part in range(2):
                                ins = nc.tensor.matmul(a_bank[b][:], src[:, part, k, P * t:P * (t + 1)], wproj[:, k, :],
                                                       start=(k == 0 and part == 0), stop=(k == KT - 1 and part == 1))
                        ins.then_inc(a_ready[b], 1)

            program(pe, run)


_INS = ["L0_attn_x", "L0_attn_qkv_w", "L0_attn_qkv_norm_w", "L0_attn_proj_w", "L0_attn_proj_norm_w", "L0_attn_norm_w",
        "L0_attn_s", "L0_ffn_W1", "L0_ffn_W2", "L0_ffn_W3"]


def kernel(**inputs):
    import numpy as _np
    import concourse.bacc as _bacc
    from concourse import mybir as _mybir
    from concourse.bass_utils import run_bass_kernel_spmd as _run

    nc = _bacc.Bacc("TRN2", target_bir_lowering=False, num_devices=1)
    arrays, args = {}, []
    for name in _INS:
        a = _np.ascontiguousarray(inputs[name])
        arrays[f"in_{name}_dram"] = a
        args.append(nc.dram_tensor(f"in_{name}_dram", a.shape, _mybir.dt.from_np(a.dtype), kind="ExternalInput").ap())
    args.append(nc.dram_tensor("out_0_dram", inputs["L0_attn_x"].shape, _mybir.dt.float32, kind="ExternalOutput").ap())
    macaron_kernel(nc, *args)
    return _run(nc, [arrays], core_ids=[0]).results[0]["out_0_dram"]
```
